# Optimizing a Trainium2 kernel written in Bass

```python
import numpy as np
import jax
import jax.numpy as jnp

def _softmax(x, axis=-1):
    return jax.nn.softmax(x, axis=axis)

def _gelu(x):
    return jax.nn.gelu(x, approximate=True)

def _silu(x):
    return jax.nn.silu(x)

def _sigmoid(x):
    return jax.nn.sigmoid(x)

def _layernorm(x, axis=-1, eps=1e-05):
    m = jnp.mean(x, axis=axis, keepdims=True)
    v = jnp.var(x, axis=axis, keepdims=True)
    return (x - m) / jnp.sqrt(v + eps)

def _scatter_add(tgt, idx, src, axis=0):
    return tgt.at[idx].add(src)

def _segment_sum(src, seg, n):
    return jax.ops.segment_sum(src, seg, n)
kernel_name = 'mk_lm_tower_d2_tok_ids1024_r4_046d5b'

def setup_inputs(seed: int=0):
    np.random.seed(seed)
    _w = jnp.asarray

    def _rec_inputs():
        import jax
        import jax.numpy as jnp
        _rk = jax.random.key(seed)
        x = jax.random.randint(jax.random.fold_in(_rk, 1), (4, 512), 0, 12564, jnp.int32)
        return x
    x = _rec_inputs()

    def _L0_tok_setup():
        import jax, jax.numpy as jnp
        import numpy as np
        B, T, D, INNER, N, V, L, P = (4, 1024, 256, 512, 64, 50257, 4, 5000)
        DECAY, INP = (0.95, 0.05)

        def _silu(x):
            return x * jax.nn.sigmoid(x)

        def _layer(x, W_in_l, cw, cb, WB, WC, Dv, Wo, g, b):
            xp = x @ W_in_l.T
            x_in, x_gate = jnp.split(xp, 2, axis=-1)
            xc = jnp.transpose(x_in, (0, 2, 1))
            xc = jnp.pad(xc, ((0, 0), (0, 0), (3, 0)))
            xc = jax.lax.conv_general_dilated(xc, cw, window_strides=(1,), padding='VALID', dimension_numbers=('NCH', 'OIH', 'NCH'), feature_group_count=INNER)
            xc = xc + cb[None, :, None]
            u = _silu(jnp.transpose(xc, (0, 2, 1)))
            Bu = u @ WB.T

            def step(h, bu):
                h = DECAY * h + INP * bu
                return (h, h)
            h0 = jnp.zeros((x.shape[0], Bu.shape[-1]), x.dtype)
            _, hs = jax.lax.scan(step, h0, jnp.swapaxes(Bu, 0, 1))
            hs = jnp.swapaxes(hs, 0, 1)
            y = hs @ WC.T + Dv * u
            y = y * _silu(x_gate)
            y = y @ Wo.T
            z = y + x
            mu = jnp.mean(z, axis=-1, keepdims=True)
            var = jnp.var(z, axis=-1, keepdims=True)
            return (z - mu) * jax.lax.rsqrt(var + 1e-05) * g + b
        key = jax.random.key(seed)
        ks = jax.random.split(key, 10)
        s = 0.02
        return {'tokens': jax.random.randint(ks[0], (B, T), 0, V), 'tok_emb': jax.random.normal(ks[1], (V, D), jnp.float32) * s, 'pos_emb': jax.random.normal(ks[2], (P, D), jnp.float32) * s, 'W_in': jax.random.normal(ks[3], (L, 2 * INNER, D), jnp.float32) * s, 'conv_w': jax.random.normal(ks[4], (L, INNER, 1, 4), jnp.float32) * s, 'conv_b': jnp.zeros((L, INNER), jnp.float32), 'W_B': jax.random.normal(ks[5], (L, N, INNER), jnp.float32) * s, 'W_C': jax.random.normal(ks[6], (L, INNER, N), jnp.float32) * s, 'D_vec': jax.random.normal(ks[7], (L, INNER), jnp.float32) * s, 'W_out': jax.random.normal(ks[8], (L, D, INNER), jnp.float32) * s, 'ln_g': jnp.ones((L, D), jnp.float32), 'ln_b': jnp.zeros((L, D), jnp.float32)}
    _L0_tok_all = _L0_tok_setup()
    _L0_tok_in = {k: v for k, v in _L0_tok_all.items() if k in ('tok_emb', 'pos_emb', 'W_in', 'conv_w', 'conv_b', 'W_B', 'W_C', 'D_vec', 'W_out', 'ln_g', 'ln_b')}
    del _L0_tok_all

    def _L0_attn_setup():
        import jax, jax.numpy as jnp
        import numpy as np
        from jax import lax
        D_MODEL, D_STATE, D_CONV, EXPAND = (256, 16, 4, 2)
        D_INNER = D_MODEL * EXPAND
        B, L = (2, 256)
        key = jax.random.key(seed)
        ks = jax.random.split(key, 8)
        x = jax.random.normal(ks[0], (B, L, D_MODEL), dtype=jnp.float32)
        in_proj_w = jax.random.normal(ks[1], (D_MODEL, 2 * D_INNER), jnp.float32) * D_MODEL ** (-0.5)
        conv_w = jax.random.normal(ks[2], (D_INNER, 1, D_CONV), jnp.float32) * D_CONV ** (-0.5)
        conv_b = jax.random.normal(ks[3], (D_INNER,), jnp.float32) * 0.02
        x_proj_w = jax.random.normal(ks[4], (D_INNER, 1 + 2 * D_STATE), jnp.float32) * D_INNER ** (-0.5)
        dt_w = jax.random.normal(ks[5], (D_INNER,), jnp.float32)
        dt_b = jax.random.normal(ks[6], (D_INNER,), jnp.float32) * 0.02
        A = jnp.arange(1, D_STATE + 1, dtype=jnp.float32)[None, :] * jnp.ones((D_INNER, 1), jnp.float32)
        A_log = jnp.clip(jnp.log(A), -6.0, 6.0)
        Dp = jnp.ones((D_INNER,), jnp.float32)
        out_proj_w = jax.random.normal(ks[7], (D_INNER, D_MODEL), jnp.float32) * D_INNER ** (-0.5)
        return dict(x=x, in_proj_w=in_proj_w, conv_w=conv_w, conv_b=conv_b, x_proj_w=x_proj_w, dt_w=dt_w, dt_b=dt_b, A_log=A_log, D=Dp, out_proj_w=out_proj_w)
    _L0_attn_all = _L0_attn_setup()
    _L0_attn_in = {k: v for k, v in _L0_attn_all.items() if k in ('in_proj_w', 'conv_w', 'conv_b', 'x_proj_w', 'dt_w', 'dt_b', 'A_log', 'D', 'out_proj_w')}
    del _L0_attn_all

    def _L0_ffn_setup():
        import jax, jax.numpy as jnp
        import numpy as np
        B, L, D = (4, 512, 256)
        H = 16
        E = 16
        NS = 16
        S = NS // E
        F = 1024
        EPS = 1e-05

        def _layernorm(x, g, b):
            mu = jnp.mean(x, axis=-1, keepdims=True)
            var = jnp.mean(jnp.square(x - mu), axis=-1, keepdims=True)
            return (x - mu) * jax.lax.rsqrt(var + EPS) * g + b

        def _mha(q, k, v, Wq, bq, Wk, bk, Wv, bv, Wo, bo):
            Bq, Lq, Dm = q.shape
            dh = Dm // H
            qh = (q @ Wq + bq).reshape(Bq, Lq, H, dh)
            kh = (k @ Wk + bk).reshape(Bq, -1, H, dh)
            vh = (v @ Wv + bv).reshape(Bq, -1, H, dh)
            scores = jnp.einsum('bqhd,bkhd->bhqk', qh, kh) / jnp.asarray(np.sqrt(dh), q.dtype)
            attn = jax.nn.softmax(scores, axis=-1)
            out = jnp.einsum('bhqk,bkhd->bqhd', attn, vh).reshape(Bq, Lq, Dm)
            return out @ Wo + bo
        key = jax.random.key(seed)
        ks = jax.random.split(key, 32)
        s = 0.02
        d = {}
        d['x'] = jax.random.normal(ks[0], (B, L, D), jnp.float32)
        d['slot_query'] = jax.random.normal(ks[1], (1, NS, D), jnp.float32) * 0.01
        for i, nm in enumerate(['d_Wq', 'd_Wk', 'd_Wv', 'd_Wo']):
            d[nm] = jax.random.normal(ks[2 + i], (D, D), jnp.float32) * s
        for nm in ['d_bq', 'd_bk', 'd_bv', 'd_bo']:
            d[nm] = jnp.zeros((D,), jnp.float32)
        for i, nm in enumerate(['c_Wq', 'c_Wk', 'c_Wv', 'c_Wo']):
            d[nm] = jax.random.normal(ks[6 + i], (D, D), jnp.float32) * s
        for nm in ['c_bq', 'c_bk', 'c_bv', 'c_bo']:
            d[nm] = jnp.zeros((D,), jnp.float32)
        d['e_ln_g'] = jnp.ones((E, D), jnp.float32)
        d['e_ln_b'] = jnp.zeros((E, D), jnp.float32)
        d['e_W1'] = jax.random.normal(ks[10], (E, D, F), jnp.float32) * s
        d['e_b1'] = jnp.zeros((E, F), jnp.float32)
        d['e_Wg'] = jax.random.normal(ks[11], (E, D, F), jnp.float32) * s
        d['e_bg'] = jnp.zeros((E, F), jnp.float32)
        d['e_W2'] = jax.random.normal(ks[12], (E, F, D), jnp.float32) * s
        d['e_b2'] = jnp.zeros((E, D), jnp.float32)
        return d
    _L0_ffn_all = _L0_ffn_setup()
    _L0_ffn_in = {k: v for k, v in _L0_ffn_all.items() if k in ('slot_query', 'd_Wq', 'd_Wk', 'd_Wv', 'd_Wo', 'd_bq', 'd_bk', 'd_bv', 'd_bo', 'c_Wq', 'c_Wk', 'c_Wv', 'c_Wo', 'c_bq', 'c_bk', 'c_bv', 'c_bo', 'e_ln_g', 'e_ln_b', 'e_W1', 'e_b1', 'e_Wg', 'e_bg', 'e_W2', 'e_b2')}
    del _L0_ffn_all

    def _L1_attn_setup():
        import jax, jax.numpy as jnp
        import numpy as np
        B, L, H, I, K, G = (2, 1024, 256, 512, 4, 8)
        EPS = 1e-05

        def _layernorm(x, g, b):
            m = x.mean(-1, keepdims=True)
            v = jnp.var(x, axis=-1, keepdims=True)
            return (x - m) * jax.lax.rsqrt(v + EPS) * g + b
        key = jax.random.key(seed)
        ks = jax.random.split(key, 8)
        s = 0.02
        return {'hidden_states': jax.random.normal(ks[0], (B, L, H), jnp.float32), 'in_proj_w': jax.random.normal(ks[1], (2 * I, H), jnp.float32) * s, 'conv_w': jax.random.normal(ks[2], (I, I // G, K), jnp.float32) * s, 'conv_b': jax.random.normal(ks[3], (I,), jnp.float32) * s, 'ln_g': jnp.ones((I,), jnp.float32), 'ln_b': jnp.zeros((I,), jnp.float32), 'fc_w': jax.random.normal(ks[4], (H, I), jnp.float32) * s, 'fc_b': jnp.zeros((H,), jnp.float32), 'cproj_w': jax.random.normal(ks[5], (I, H), jnp.float32) * s, 'cproj_b': jnp.zeros((I,), jnp.float32), 'out_w': jax.random.normal(ks[6], (H, I), jnp.float32) * s}
    _L1_attn_all = _L1_attn_setup()
    _L1_attn_in = {k: v for k, v in _L1_attn_all.items() if k in ('in_proj_w', 'conv_w', 'conv_b', 'ln_g', 'ln_b', 'fc_w', 'fc_b', 'cproj_w', 'cproj_b', 'out_w')}
    del _L1_attn_all

    def _L1_ffn_setup():
        import jax, jax.numpy as jnp
        import numpy as np
        E = 8
        TOPK = 2

        def _moe_forward(x, Wg, W1, W2, W3):
            B, S, D = x.shape
            xt = x.reshape(-1, D)
            T = xt.shape[0]
            logits = xt @ Wg.T
            scores = jax.nn.softmax(logits, axis=-1)
            w, idx = jax.lax.top_k(scores, TOPK)
            w = w / (w.sum(axis=-1, keepdims=True) + 1e-20)
            cw = jnp.zeros((T, E), xt.dtype).at[jnp.arange(T)[:, None], idx].add(w)
            h = jax.nn.silu(jnp.einsum('td,ehd->teh', xt, W1)) * jnp.einsum('td,ehd->teh', xt, W3)
            out = jnp.einsum('teh,edh->ted', h, W2)
            y = jnp.einsum('te,ted->td', cw, out)
            return y.reshape(B, S, D)
        key = jax.random.key(seed)
        k0, k1, k2, k3, k4 = jax.random.split(key, 5)
        B, S, D, H = (1, 512, 256, 704)
        scale = 0.02
        x = jax.random.normal(k0, (B, S, D), jnp.float32)
        Wg = jax.random.normal(k1, (E, D), jnp.float32) * scale
        W1 = jax.random.normal(k2, (E, H, D), jnp.float32) * scale
        W2 = jax.random.normal(k3, (E, D, H), jnp.float32) * scale
        W3 = jax.random.normal(k4, (E, H, D), jnp.float32) * scale
        return {'x': x, 'Wg': Wg, 'W1': W1, 'W2': W2, 'W3': W3}
    _L1_ffn_all = _L1_ffn_setup()
    _L1_ffn_in = {k: v for k, v in _L1_ffn_all.items() if k in ('Wg', 'W1', 'W2', 'W3')}
    del _L1_ffn_all
    return {'x': x, 'L0_tok_tok_emb': _L0_tok_in['tok_emb'], 'L0_tok_pos_emb': _L0_tok_in['pos_emb'], 'L0_tok_W_in': _L0_tok_in['W_in'], 'L0_tok_conv_w': _L0_tok_in['conv_w'], 'L0_tok_conv_b': _L0_tok_in['conv_b'], 'L0_tok_W_B': _L0_tok_in['W_B'], 'L0_tok_W_C': _L0_tok_in['W_C'], 'L0_tok_D_vec': _L0_tok_in['D_vec'], 'L0_tok_W_out': _L0_tok_in['W_out'], 'L0_tok_ln_g': _L0_tok_in['ln_g'], 'L0_tok_ln_b': _L0_tok_in['ln_b'], 'L0_attn_in_proj_w': _L0_attn_in['in_proj_w'], 'L0_attn_conv_w': _L0_attn_in['conv_w'], 'L0_attn_conv_b': _L0_attn_in['conv_b'], 'L0_attn_x_proj_w': _L0_attn_in['x_proj_w'], 'L0_attn_dt_w': _L0_attn_in['dt_w'], 'L0_attn_dt_b': _L0_attn_in['dt_b'], 'L0_attn_A_log': _L0_attn_in['A_log'], 'L0_attn_D': _L0_attn_in['D'], 'L0_attn_out_proj_w': _L0_attn_in['out_proj_w'], 'L0_ffn_slot_query': _L0_ffn_in['slot_query'], 'L0_ffn_d_Wq': _L0_ffn_in['d_Wq'], 'L0_ffn_d_Wk': _L0_ffn_in['d_Wk'], 'L0_ffn_d_Wv': _L0_ffn_in['d_Wv'], 'L0_ffn_d_Wo': _L0_ffn_in['d_Wo'], 'L0_ffn_d_bq': _L0_ffn_in['d_bq'], 'L0_ffn_d_bk': _L0_ffn_in['d_bk'], 'L0_ffn_d_bv': _L0_ffn_in['d_bv'], 'L0_ffn_d_bo': _L0_ffn_in['d_bo'], 'L0_ffn_c_Wq': _L0_ffn_in['c_Wq'], 'L0_ffn_c_Wk': _L0_ffn_in['c_Wk'], 'L0_ffn_c_Wv': _L0_ffn_in['c_Wv'], 'L0_ffn_c_Wo': _L0_ffn_in['c_Wo'], 'L0_ffn_c_bq': _L0_ffn_in['c_bq'], 'L0_ffn_c_bk': _L0_ffn_in['c_bk'], 'L0_ffn_c_bv': _L0_ffn_in['c_bv'], 'L0_ffn_c_bo': _L0_ffn_in['c_bo'], 'L0_ffn_e_ln_g': _L0_ffn_in['e_ln_g'], 'L0_ffn_e_ln_b': _L0_ffn_in['e_ln_b'], 'L0_ffn_e_W1': _L0_ffn_in['e_W1'], 'L0_ffn_e_b1': _L0_ffn_in['e_b1'], 'L0_ffn_e_Wg': _L0_ffn_in['e_Wg'], 'L0_ffn_e_bg': _L0_ffn_in['e_bg'], 'L0_ffn_e_W2': _L0_ffn_in['e_W2'], 'L0_ffn_e_b2': _L0_ffn_in['e_b2'], 'L1_attn_in_proj_w': _L1_attn_in['in_proj_w'], 'L1_attn_conv_w': _L1_attn_in['conv_w'], 'L1_attn_conv_b': _L1_attn_in['conv_b'], 'L1_attn_ln_g': _L1_attn_in['ln_g'], 'L1_attn_ln_b': _L1_attn_in['ln_b'], 'L1_attn_fc_w': _L1_attn_in['fc_w'], 'L1_attn_fc_b': _L1_attn_in['fc_b'], 'L1_attn_cproj_w': _L1_attn_in['cproj_w'], 'L1_attn_cproj_b': _L1_attn_in['cproj_b'], 'L1_attn_out_w': _L1_attn_in['out_w'], 'L1_ffn_Wg': _L1_ffn_in['Wg'], 'L1_ffn_W1': _L1_ffn_in['W1'], 'L1_ffn_W2': _L1_ffn_in['W2'], 'L1_ffn_W3': _L1_ffn_in['W3']}

def reference(x, L0_tok_tok_emb, L0_tok_pos_emb, L0_tok_W_in, L0_tok_conv_w, L0_tok_conv_b, L0_tok_W_B, L0_tok_W_C, L0_tok_D_vec, L0_tok_W_out, L0_tok_ln_g, L0_tok_ln_b, L0_attn_in_proj_w, L0_attn_conv_w, L0_attn_conv_b, L0_attn_x_proj_w, L0_attn_dt_w, L0_attn_dt_b, L0_attn_A_log, L0_attn_D, L0_attn_out_proj_w, L0_ffn_slot_query, L0_ffn_d_Wq, L0_ffn_d_Wk, L0_ffn_d_Wv, L0_ffn_d_Wo, L0_ffn_d_bq, L0_ffn_d_bk, L0_ffn_d_bv, L0_ffn_d_bo, L0_ffn_c_Wq, L0_ffn_c_Wk, L0_ffn_c_Wv, L0_ffn_c_Wo, L0_ffn_c_bq, L0_ffn_c_bk, L0_ffn_c_bv, L0_ffn_c_bo, L0_ffn_e_ln_g, L0_ffn_e_ln_b, L0_ffn_e_W1, L0_ffn_e_b1, L0_ffn_e_Wg, L0_ffn_e_bg, L0_ffn_e_W2, L0_ffn_e_b2, L1_attn_in_proj_w, L1_attn_conv_w, L1_attn_conv_b, L1_attn_ln_g, L1_attn_ln_b, L1_attn_fc_w, L1_attn_fc_b, L1_attn_cproj_w, L1_attn_cproj_b, L1_attn_out_w, L1_ffn_Wg, L1_ffn_W1, L1_ffn_W2, L1_ffn_W3):
    import jax
    import jax.numpy as jnp

    def _L0_tok_ref(tokens, tok_emb, pos_emb, W_in, conv_w, conv_b, W_B, W_C, D_vec, W_out, ln_g, ln_b):
        import jax, jax.numpy as jnp
        import numpy as np
        B, T, D, INNER, N, V, L, P = (4, 1024, 256, 512, 64, 50257, 4, 5000)
        DECAY, INP = (0.95, 0.05)

        def _silu(x):
            return x * jax.nn.sigmoid(x)

        def _layer(x, W_in_l, cw, cb, WB, WC, Dv, Wo, g, b):
            xp = x @ W_in_l.T
            x_in, x_gate = jnp.split(xp, 2, axis=-1)
            xc = jnp.transpose(x_in, (0, 2, 1))
            xc = jnp.pad(xc, ((0, 0), (0, 0), (3, 0)))
            xc = jax.lax.conv_general_dilated(xc, cw, window_strides=(1,), padding='VALID', dimension_numbers=('NCH', 'OIH', 'NCH'), feature_group_count=INNER)
            xc = xc + cb[None, :, None]
            u = _silu(jnp.transpose(xc, (0, 2, 1)))
            Bu = u @ WB.T

            def step(h, bu):
                h = DECAY * h + INP * bu
                return (h, h)
            h0 = jnp.zeros((x.shape[0], Bu.shape[-1]), x.dtype)
            _, hs = jax.lax.scan(step, h0, jnp.swapaxes(Bu, 0, 1))
            hs = jnp.swapaxes(hs, 0, 1)
            y = hs @ WC.T + Dv * u
            y = y * _silu(x_gate)
            y = y @ Wo.T
            z = y + x
            mu = jnp.mean(z, axis=-1, keepdims=True)
            var = jnp.var(z, axis=-1, keepdims=True)
            return (z - mu) * jax.lax.rsqrt(var + 1e-05) * g + b
        x = tok_emb[tokens] + pos_emb[jnp.arange(tokens.shape[1])][None]
        for l in range(L):
            x = _layer(x, W_in[l], conv_w[l], conv_b[l], W_B[l], W_C[l], D_vec[l], W_out[l], ln_g[l], ln_b[l])
        return x

    def _L0_attn_ref(x, in_proj_w, conv_w, conv_b, x_proj_w, dt_w, dt_b, A_log, D, out_proj_w):
        import jax, jax.numpy as jnp
        import numpy as np
        from jax import lax
        D_MODEL, D_STATE, D_CONV, EXPAND = (256, 16, 4, 2)
        D_INNER = D_MODEL * EXPAND
        B, L = (2, 256)
        x = x.astype(jnp.float32)
        b, l, _ = x.shape
        S = D_STATE
        xz = x @ in_proj_w
        xi, z = jnp.split(xz, 2, axis=-1)
        xc = lax.conv_general_dilated(jnp.transpose(xi, (0, 2, 1)), conv_w, window_strides=(1,), padding=[(D_CONV - 1, 0)], dimension_numbers=('NCH', 'OIH', 'NCH'), feature_group_count=D_INNER)
        xc = jnp.transpose(xc + conv_b[None, :, None], (0, 2, 1))
        xc = jax.nn.silu(xc)
        bcdt = xc @ x_proj_w
        dt_raw, Bs, Cs = (bcdt[..., :1], bcdt[..., 1:1 + S], bcdt[..., 1 + S:])
        dt = jax.nn.softplus(dt_raw * dt_w + dt_b)
        A = -jnp.exp(jnp.clip(A_log, -6.0, 6.0))
        dA = jnp.exp(dt[..., None] * A[None, None])
        dBx = dt[..., None] * Bs[:, :, None, :] * xc[..., None]

        def step(h, inp):
            dA_t, dBx_t, C_t = inp
            h = jnp.clip(dA_t * h + dBx_t, -10000.0, 10000.0)
            y = jnp.einsum('bds,bs->bd', h, C_t)
            return (h, y)
        h0 = jnp.zeros((b, D_INNER, S), jnp.float32)
        xs = (jnp.moveaxis(dA, 1, 0), jnp.moveaxis(dBx, 1, 0), jnp.moveaxis(Cs, 1, 0))
        _, ys = lax.scan(step, h0, xs)
        y = jnp.moveaxis(ys, 0, 1) + xc * D[None, None]
        y = y * jax.nn.silu(z)
        return y @ out_proj_w

    def _L0_ffn_ref(x, slot_query, d_Wq, d_Wk, d_Wv, d_Wo, d_bq, d_bk, d_bv, d_bo, c_Wq, c_Wk, c_Wv, c_Wo, c_bq, c_bk, c_bv, c_bo, e_ln_g, e_ln_b, e_W1, e_b1, e_Wg, e_bg, e_W2, e_b2):
        import jax, jax.numpy as jnp
        import numpy as np
        B, L, D = (4, 512, 256)
        H = 16
        E = 16
        NS = 16
        S = NS // E
        F = 1024
        EPS = 1e-05

        def _layernorm(x, g, b):
            mu = jnp.mean(x, axis=-1, keepdims=True)
            var = jnp.mean(jnp.square(x - mu), axis=-1, keepdims=True)
            return (x - mu) * jax.lax.rsqrt(var + EPS) * g + b

        def _mha(q, k, v, Wq, bq, Wk, bk, Wv, bv, Wo, bo):
            Bq, Lq, Dm = q.shape
            dh = Dm // H
            qh = (q @ Wq + bq).reshape(Bq, Lq, H, dh)
            kh = (k @ Wk + bk).reshape(Bq, -1, H, dh)
            vh = (v @ Wv + bv).reshape(Bq, -1, H, dh)
            scores = jnp.einsum('bqhd,bkhd->bhqk', qh, kh) / jnp.asarray(np.sqrt(dh), q.dtype)
            attn = jax.nn.softmax(scores, axis=-1)
            out = jnp.einsum('bhqk,bkhd->bqhd', attn, vh).reshape(Bq, Lq, Dm)
            return out @ Wo + bo
        Bx = x.shape[0]
        q = jnp.broadcast_to(slot_query, (Bx, NS, D))
        o = q + _mha(q, x, x, d_Wq, d_bq, d_Wk, d_bk, d_Wv, d_bv, d_Wo, d_bo)
        os = o.reshape(Bx, E, S, D)
        h = _layernorm(os, e_ln_g[None, :, None, :], e_ln_b[None, :, None, :])
        u = jax.nn.silu(jnp.einsum('besd,edf->besf', h, e_W1) + e_b1[None, :, None, :])
        g = jax.nn.silu(jnp.einsum('besd,edf->besf', h, e_Wg) + e_bg[None, :, None, :])
        y = jnp.einsum('besf,efd->besd', u * g, e_W2) + e_b2[None, :, None, :]
        o = o + y.reshape(Bx, NS, D)
        out = _mha(x, o, o, c_Wq, c_bq, c_Wk, c_bk, c_Wv, c_bv, c_Wo, c_bo)
        return out

    def _L1_attn_ref(hidden_states, in_proj_w, conv_w, conv_b, ln_g, ln_b, fc_w, fc_b, cproj_w, cproj_b, out_w):
        import jax, jax.numpy as jnp
        import numpy as np
        B, L, H, I, K, G = (2, 1024, 256, 512, 4, 8)
        EPS = 1e-05

        def _layernorm(x, g, b):
            m = x.mean(-1, keepdims=True)
            v = jnp.var(x, axis=-1, keepdims=True)
            return (x - m) * jax.lax.rsqrt(v + EPS) * g + b
        p = hidden_states @ in_proj_w.T
        h, gate = (p[..., :I], p[..., I:])
        gate = jax.nn.silu(gate)
        hc = jnp.transpose(h, (0, 2, 1))
        conv = jax.lax.conv_general_dilated(hc, conv_w, window_strides=(1,), padding=[(K - 1, 0)], feature_group_count=G, dimension_numbers=('NCH', 'OIH', 'NCH'))
        conv = conv + conv_b[None, :, None]
        h = jnp.transpose(conv, (0, 2, 1)) * gate
        residual = h
        hn = _layernorm(h, ln_g, ln_b)
        m = jax.nn.silu(hn @ fc_w.T + fc_b) @ cproj_w.T + cproj_b
        h = m + residual
        return h @ out_w.T

    def _L1_ffn_ref(x, Wg, W1, W2, W3):
        import jax, jax.numpy as jnp
        import numpy as np
        E = 8
        TOPK = 2

        def _moe_forward(x, Wg, W1, W2, W3):
            B, S, D = x.shape
            xt = x.reshape(-1, D)
            T = xt.shape[0]
            logits = xt @ Wg.T
            scores = jax.nn.softmax(logits, axis=-1)
            w, idx = jax.lax.top_k(scores, TOPK)
            w = w / (w.sum(axis=-1, keepdims=True) + 1e-20)
            cw = jnp.zeros((T, E), xt.dtype).at[jnp.arange(T)[:, None], idx].add(w)
            h = jax.nn.silu(jnp.einsum('td,ehd->teh', xt, W1)) * jnp.einsum('td,ehd->teh', xt, W3)
            out = jnp.einsum('teh,edh->ted', h, W2)
            y = jnp.einsum('te,ted->td', cw, out)
            return y.reshape(B, S, D)
        return _moe_forward(x, Wg, W1, W2, W3)
    h = _L0_tok_ref(x, L0_tok_tok_emb, L0_tok_pos_emb, L0_tok_W_in, L0_tok_conv_w, L0_tok_conv_b, L0_tok_W_B, L0_tok_W_C, L0_tok_D_vec, L0_tok_W_out, L0_tok_ln_g, L0_tok_ln_b)
    h = h + _L0_attn_ref(_layernorm(h, axis=-1), L0_attn_in_proj_w, L0_attn_conv_w, L0_attn_conv_b, L0_attn_x_proj_w, L0_attn_dt_w, L0_attn_dt_b, L0_attn_A_log, L0_attn_D, L0_attn_out_proj_w)
    h = h + _L0_ffn_ref(_layernorm(h, axis=-1), L0_ffn_slot_query, L0_ffn_d_Wq, L0_ffn_d_Wk, L0_ffn_d_Wv, L0_ffn_d_Wo, L0_ffn_d_bq, L0_ffn_d_bk, L0_ffn_d_bv, L0_ffn_d_bo, L0_ffn_c_Wq, L0_ffn_c_Wk, L0_ffn_c_Wv, L0_ffn_c_Wo, L0_ffn_c_bq, L0_ffn_c_bk, L0_ffn_c_bv, L0_ffn_c_bo, L0_ffn_e_ln_g, L0_ffn_e_ln_b, L0_ffn_e_W1, L0_ffn_e_b1, L0_ffn_e_Wg, L0_ffn_e_bg, L0_ffn_e_W2, L0_ffn_e_b2)
    h = h + _L1_attn_ref(_layernorm(h, axis=-1), L1_attn_in_proj_w, L1_attn_conv_w, L1_attn_conv_b, L1_attn_ln_g, L1_attn_ln_b, L1_attn_fc_w, L1_attn_fc_b, L1_attn_cproj_w, L1_attn_cproj_b, L1_attn_out_w)
    h = h + _L1_ffn_ref(_layernorm(h, axis=-1), L1_ffn_Wg, L1_ffn_W1, L1_ffn_W2, L1_ffn_W3)
    return h

_drawn_inputs = setup_inputs


def setup_inputs(seed=0):
    import zlib

    import numpy as np

    out = dict(_drawn_inputs(seed))
    spreads = {'L0_tok_conv_b': (0.0, 0.8),
     'L0_tok_ln_g': (1.0, 0.2),
     'L0_tok_ln_b': (0.0, 0.1),
     'L0_attn_D': (1.0, 0.2),
     'L0_ffn_d_bq': (0.0, 0.8),
     'L0_ffn_d_bk': (0.0, 2.0),
     'L0_ffn_d_bv': (0.0, 0.8),
     'L0_ffn_d_bo': (0.0, 0.8),
     'L0_ffn_c_bq': (0.0, 0.8),
     'L0_ffn_c_bk': (0.0, 2.0),
     'L0_ffn_c_bv': (0.0, 2.0),
     'L0_ffn_c_bo': (0.0, 0.8),
     'L0_ffn_e_ln_g': (1.0, 0.6),
     'L0_ffn_e_ln_b': (0.0, 0.8),
     'L0_ffn_e_b1': (0.0, 0.8),
     'L0_ffn_e_bg': (0.0, 0.8),
     'L0_ffn_e_b2': (0.0, 0.8),
     'L1_attn_ln_g': (1.0, 0.6),
     'L1_attn_ln_b': (0.0, 2.0),
     'L1_attn_fc_b': (0.0, 2.0),
     'L1_attn_cproj_b': (0.0, 0.8)}
    factors = {'L0_tok_W_in': 8.0,
     'L0_tok_conv_w': 8.0,
     'L0_tok_W_B': 8.0,
     'L0_tok_W_C': 8.0,
     'L0_tok_D_vec': 8.0,
     'L0_tok_W_out': 8.0,
     'L0_attn_conv_b': 3.844,
     'L0_attn_dt_b': 8.0,
     'L0_ffn_slot_query': 8.0,
     'L0_ffn_d_Wq': 8.0,
     'L0_ffn_d_Wk': 8.0,
     'L0_ffn_d_Wv': 8.0,
     'L0_ffn_d_Wo': 8.0,
     'L0_ffn_c_Wq': 8.0,
     'L0_ffn_c_Wk': 8.0,
     'L0_ffn_c_Wv': 5.882,
     'L0_ffn_e_W1': 8.0,
     'L0_ffn_e_Wg': 8.0,
     'L0_ffn_e_W2': 8.0,
     'L1_attn_conv_b': 64.0,
     'L1_ffn_Wg': 20.567,
     'L1_ffn_W1': 16.992,
     'L1_ffn_W2': 15.495,
     'L1_ffn_W3': 15.531,
     'L1_attn_in_proj_w': 8.0,
     'L1_attn_conv_w': 8.0,
     'L1_attn_fc_w': 8.0,
     'L1_attn_cproj_w': 8.0,
     'L1_attn_out_w': 8.0}
    for name, (base, spread) in spreads.items():
        noise = np.random.default_rng([zlib.crc32(name.encode()), seed]).standard_normal(out[name].shape)
        drawn = base * np.exp(spread * noise) if base else spread * noise
        out[name] = jnp.asarray(drawn.astype(out[name].dtype))
    for name, factor in factors.items():
        out[name] = (out[name] * factor).astype(out[name].dtype)
    return out
```

```python
from contextlib import ExitStack

import numpy as np
import concourse.bass as bass
from concourse import mybir

ALU = mybir.AluOpType
ACT = mybir.ActivationFunctionType
F32 = mybir.dt.float32
I32 = mybir.dt.int32
U32 = mybir.dt.uint32
AX = mybir.AxisListType

P = 128
D = 256
KD = D // P
B = 4
T = 512
TT = T // P
INNER = 512
MI = INNER // P
EPS = 1e-5
START = 8


def at(eng, sem, done):
    eng.wait_ge(sem, done + START)


def embed_stage(nc, K, a):
    with ExitStack() as ctx:
        sem = lambda n: K["sem"](n)
        idx = ctx.enter_context(nc.sbuf_tensor("token_ids", [P, B * TT], I32))
        pos = ctx.enter_context(nc.sbuf_tensor("positions", [P, TT, D], F32))
        ids_loaded, pos_loaded, rows_gathered, filled = sem("ids_loaded"), sem("pos_loaded"), sem("rows_gathered"), sem("consts_filled")
        embedded = sem("embedded")
        block = ctx.enter_context(nc.Block())
        h, ident = K["h"], K["ident"]

        @block.sync
        def _(sp):
            sp.dma_start(idx[:, :], a["x"]).then_inc(ids_loaded, 16)
            sp.dma_start(pos[:, :, :], a["pos_emb"][0:T, :].rearrange("(t p) d -> p t d", p=P)).then_inc(pos_loaded, 16)

        @block.gpsimd
        def _(pool):
            pool.memset(ident[:, :], 0.0).then_inc(filled, 1)
            pool.memset(K["ones"][:, :], 1.0).then_inc(filled, 1)
            pool.memset(K["mhalf"][:, :], -0.5).then_inc(filled, 1)
            pool.memset(K["eps"][:, :], EPS).then_inc(filled, 1)
            pool.wait_ge(filled, 1)
            pool.affine_select(out=ident[:, :], in_=ident[:, :], compare_op=ALU.not_equal, fill=1.0,
                               base=0, pattern=[[-1, P]], channel_multiplier=1).then_inc(filled, 1)
            pool.wait_ge(ids_loaded, 16)
            for n in range(B * TT):
                pool.indirect_dma_start(
                    out=h[:, n // TT, n % TT, :], out_offset=None, in_=a["tok_emb"][:, :],
                    in_offset=bass.IndirectOffsetOnAxis(ap=idx[:, n:n + 1].bitcast(U32), axis=0),
                ).then_inc(rows_gathered, 16)

        @block.vector
        def _(dve):
            dve.wait_ge(pos_loaded, 16)
            for b in range(B):
                if b == 0:
                    dve.wait_ge(rows_gathered, 16 * B * TT)
                dve.tensor_tensor(h[:, b, :, :], h[:, b, :, :], pos[:, :, :], ALU.add).then_inc(embedded, 1)


def token_stage(nc, K, a):
    L, N, DECAY, INP, TAPS = 4, 64, 0.95, 0.05, 4
    with ExitStack() as ctx:
        sem = lambda n: K["sem"](n)
        sb = lambda n, s, d=F32: ctx.enter_context(nc.sbuf_tensor(n, s, d))
        h, ident, bank = K["h"], K["ident"], K["bank"]
        w_in = sb("w_in", [P, KD, 2 * INNER])
        w_b = sb("w_b", [P, MI, N])
        w_c = sb("w_c", [N, INNER])
        w_c5 = sb("w_c5", [N, INNER])
        w_out = sb("w_out", [P, MI, D])
        par = sb("par", [P, 24])
        ln_g, ln_b = sb("ln_g", [P, D]), sb("ln_b", [P, D])
        decay = sb("decay", [N, T])
        xT = sb("xT", [P, 2, KD, T])
        acc = sb("acc", [P, 2, T])
        u = sb("u", [P, 2, MI, T])
        sg = sb("sg", [P, 2, MI, T])
        hs = sb("hs", [N, 2, T])
        yt = sb("yt", [P, 2, T])
        yg = sb("yg", [P, 2, MI, T])
        z = sb("z", [P, 2, TT, D])
        st = sb("st", [P, 2, TT, 6])
        mv = sb("mv", [P, 2, TT, 2])
        ve = sb("ve", [P, 2, TT])
        rstd = sb("rstd", [P, 2, TT])
        xn = sb("xn", [P, 2, TT, D])
        xg = sb("xg", [P, 2, TT, D])
        spare = sb("spare", [P, 1])

        w_in_loaded, w_small_loaded, w_out_loaded, ln_loaded = sem("w_in_loaded"), sem("w_small_loaded"), sem("w_out_loaded"), sem("ln_loaded")
        decay_set, w_c_scaled = sem("decay_set"), sem("w_c_scaled")
        xT_psum, xT_ready = sem("xT_psum"), sem("xT_ready")
        p_psum, p_tap, p_conv1, p_conv2, p_conv, u_ready = sem("p_psum"), sem("p_tap"), sem("p_conv1"), sem("p_conv2"), sem("p_conv"), sem("u_ready")
        g_psum, g_ready = sem("g_psum"), sem("g_ready")
        bu_psum, hs_ready = sem("bu_psum"), sem("hs_ready")
        y_psum, yt_ready, yg_ready = sem("y_psum"), sem("yt_ready"), sem("yg_ready")
        o_psum, z_ready, stats, var, veps, rstd_ready, xn_ready, xg_ready, x_ready = (
            sem("o_psum"), sem("z_ready"), sem("stats"), sem("var"), sem("veps"), sem("rstd_ready"), sem("xn_ready"), sem("xg_ready"), sem("x_ready"))
        block = ctx.enter_context(nc.Block())
        PT = (0, 1)
        PP, PG, PB, PY = (2, 3), 4, 5, (6, 7)

        @block.sync
        def _(sp):
            for q in (g_psum, p_psum, yt_ready, o_psum, x_ready, z_ready, u_ready, hs_ready, yg_ready, xT_ready, p_conv, g_ready,
                      w_c_scaled, xT_psum, y_psum, bu_psum, xn_ready, veps, stats, p_tap, p_conv1, p_conv2, rstd_ready, xg_ready, var):
                sp.sem_inc(q, START)
            with sp.Fori(0, L) as l:
                at(sp, g_psum, l * (B * MI))
                at(sp, p_psum, l * (B * MI))
                sp.dma_start(w_in[:, :, :], a["W_inT"][l]).then_inc(w_in_loaded, 16)
                at(sp, yt_ready, l * (B * MI))
                sp.dma_start(par[:, :], a["tok_par"][l]).then_inc(w_small_loaded, 16)
                sp.dma_start(w_b[:, :, :], a["W_BT"][l]).then_inc(w_small_loaded, 16)
                sp.dma_start(w_c[:, :], a["W_CT"][l]).then_inc(w_small_loaded, 16)
                at(sp, o_psum, l * (2 * B))
                sp.dma_start(w_out[:, :, :], a["W_outT"][l]).then_inc(w_out_loaded, 16)
                at(sp, x_ready, l * B)
                sp.dma_start(ln_g[:, :], a["tok_ln_g"][l].broadcast_to([P, D])).then_inc(ln_loaded, 16)
                sp.dma_start(ln_b[:, :], a["tok_ln_b"][l].broadcast_to([P, D])).then_inc(ln_loaded, 16)

        @block.tensor
        def _(pe):
            with pe.Fori(0, L) as l:
                for s in range(B + 2):
                    if s < B:
                        at(pe, x_ready, l * B + (s + 1 - B))
                        at(pe, z_ready, l * (2 * B) + max(0, 2 * (s - 2)))
                        for k in range(KD):
                            for t in range(TT):
                                mm = pe.transpose(bank[PT[k]][:, t * P:(t + 1) * P], h[:, s, t, k * P:(k + 1) * P], ident[:, :])
                        mm.then_inc(xT_psum, 1)
                    if 1 <= s <= B:
                        b = s - 1
                        at(pe, u_ready, l * (B * MI) + MI * (b + 1))
                        at(pe, hs_ready, l * B + b)
                        if b == 0:
                            pe.wait_ge(w_small_loaded, l * 48 + 48)
                        for k in range(MI):
                            mm = pe.matmul(bank[PB][0:N, :], w_b[:, k, :], u[:, b % 2, k, :], start=(k == 0), stop=(k == MI - 1))
                        mm.then_inc(bu_psum, 1)
                    if s >= 2:
                        b = s - 2
                        at(pe, yg_ready, l * (B * MI) + MI * (b + 1))
                        if s < B:
                            at(pe, xT_ready, l * B + s + 1)
                        else:
                            at(pe, z_ready, l * (2 * B) + 2 * b)
                        if b == 0:
                            pe.wait_ge(w_out_loaded, l * 16 + 16)
                        for j in range(2):
                            for t in range(2):
                                for k in range(MI):
                                    mm = pe.matmul(bank[PT[j]][:, t * D:(t + 1) * D],
                                                   yg[:, b % 2, k, (2 * j + t) * P:(2 * j + t + 1) * P], w_out[:, k, :],
                                                   start=(k == 0), stop=(k == MI - 1))
                            mm.then_inc(o_psum, 1)
                    if s < B:
                        at(pe, xT_ready, l * B + s + 1)
                        if s == 0:
                            pe.wait_ge(w_in_loaded, l * 16 + 16)
                        for m in range(MI):
                            f = s * MI + m
                            at(pe, p_conv, l * (B * MI) + max(0, f - 1))
                            for k in range(KD):
                                mm = pe.matmul(bank[PP[m % 2]][:, :], w_in[:, k, m * P:(m + 1) * P], xT[:, s % 2, k, :],
                                               start=(k == 0), stop=(k == KD - 1))
                            mm.then_inc(p_psum, 1)
                            at(pe, g_ready, l * (B * MI) + f)
                            for k in range(KD):
                                mm = pe.matmul(bank[PG][:, :], w_in[:, k, INNER + m * P:INNER + (m + 1) * P], xT[:, s % 2, k, :],
                                               start=(k == 0), stop=(k == KD - 1))
                            mm.then_inc(g_psum, 1)
                    if 1 <= s <= B:
                        b = s - 1
                        at(pe, hs_ready, l * B + b + 1)
                        at(pe, w_c_scaled, l + 1)
                        for m in range(MI):
                            f = b * MI + m
                            at(pe, yt_ready, l * (B * MI) + max(0, f - 1))
                            pe.matmul(bank[PY[m % 2]][:, :], w_c5[:, m * P:(m + 1) * P], hs[:, b % 2, :],
                                      start=True, stop=True).then_inc(y_psum, 1)

        @block.scalar
        def _(act):
            with act.Fori(0, L) as l:
                for s in range(B):
                    at(act, xT_psum, l * B + s + 1)
                    for k in range(KD):
                        i = act.activation(xT[:, s % 2, k, :], bank[PT[k]][:, :], ACT.Copy)
                    i.then_inc(xT_ready, 1)
                    if s == 0:
                        act.wait_ge(w_small_loaded, l * 48 + 48)
                        at(act, y_psum, l * (B * MI))
                        act.activation(w_c5[:, :], w_c[:, :], ACT.Copy, scale=INP).then_inc(w_c_scaled, 1)

                    def silu_u(m):
                        at(act, p_conv, l * (B * MI) + s * MI + m + 1)
                        if m == 0:
                            at(act, yt_ready, l * (B * MI) + max(0, (s - 1) * MI))
                        act.activation(u[:, s % 2, m, :], acc[:, m % 2, :], ACT.Silu).then_inc(u_ready, 1)

                    for m in range(MI):
                        f = s * MI + m
                        at(act, p_psum, l * (B * MI) + f + 1)
                        at(act, u_ready, l * (B * MI) + max(0, f - 1))
                        act.activation(acc[:, m % 2, :], bank[PP[m % 2]][:, :], ACT.Identity,
                                       bias=par[:, 16 + m:17 + m], scale=par[:, 4 * m + 3:4 * m + 4]).then_inc(p_tap, 1)
                        at(act, g_psum, l * (B * MI) + f + 1)
                        if m == 0:
                            at(act, yg_ready, l * (B * MI) + max(0, (s - 1) * MI))
                        act.activation(sg[:, s % 2, m, :], bank[PG][:, :], ACT.Silu).then_inc(g_ready, 1)
                        if m:
                            silu_u(m - 1)
                    silu_u(MI - 1)

        @block.vector
        def _(dve):
            dve.memset(decay[:, :], DECAY).then_inc(decay_set, 1)
            dve.wait_ge(decay_set, 1)
            with dve.Fori(0, L) as l:
                for s in range(B + 2):
                    if 1 <= s <= B:
                        b = s - 1
                        at(dve, bu_psum, l * B + b + 1)
                        at(dve, y_psum, l * (B * MI) + max(0, (b - 1) * MI))
                        dve.tensor_tensor_scan(hs[:, b % 2, :], decay[:, :], bank[PB][0:N, :], 0.0, ALU.mult, ALU.add).then_inc(hs_ready, 1)
                    if s >= 2:
                        b = s - 2
                        for j in range(2):
                            at(dve, o_psum, l * (2 * B) + 2 * b + j + 1)
                            if j == 0:
                                at(dve, xn_ready, l * B + max(0, b - 1))
                            dve.tensor_tensor(z[:, b % 2, 2 * j:2 * j + 2, :].rearrange("p t d -> p (t d)"), bank[PT[j]][:, :],
                                              h[:, b, 2 * j:2 * j + 2, :].rearrange("p t d -> p (t d)"), ALU.add).then_inc(z_ready, 1)
                        at(dve, z_ready, l * (2 * B) + 2 * b + 2)
                        for t in range(TT):
                            i = dve.bn_stats(st[:, b % 2, t, :], z[:, b % 2, t, :])
                        i.then_inc(stats, 1)
                        at(dve, stats, l * B + b + 1)
                        at(dve, veps, l * B + max(0, b - 1))
                        dve.memset(spare[:, :], 0.0)
                        for t in range(TT):
                            i = dve.bn_aggr(mv[:, b % 2, t, :], st[:, b % 2, t, :])
                        i.then_inc(var, 1)
                    if s < B:
                        for m in range(MI):
                            f = s * MI + m
                            pb = bank[PP[m % 2]]
                            for j, done in ((1, p_conv1), (2, p_conv2), (3, p_conv)):
                                at(dve, p_tap if j == 1 else p_conv1 if j == 2 else p_conv2, l * (B * MI) + f + 1)
                                dve.scalar_tensor_tensor(acc[:, m % 2, j:T], pb[:, 0:T - j], par[:, 4 * m + 3 - j:4 * m + 4 - j],
                                                         acc[:, m % 2, j:T], ALU.mult, ALU.add).then_inc(done, 1)
                    if s >= 2:
                        b = s - 2
                        at(dve, rstd_ready, l * B + b + 1)
                        at(dve, xg_ready, l * B + max(0, b - 1))
                        for t in range(TT):
                            i = dve.tensor_scalar(xn[:, b % 2, t, :], z[:, b % 2, t, :], mv[:, b % 2, t, 0:1],
                                                  rstd[:, b % 2, t:t + 1], ALU.subtract, ALU.mult)
                        i.then_inc(xn_ready, 1)
                    if 1 <= s <= B:
                        b = s - 1
                        for m in range(MI):
                            f = b * MI + m
                            at(dve, y_psum, l * (B * MI) + f + 1)
                            at(dve, u_ready, l * (B * MI) + f + 1)
                            at(dve, yg_ready, l * (B * MI) + max(0, f - 1))
                            dve.scalar_tensor_tensor(yt[:, m % 2, :], u[:, b % 2, m, :], par[:, 20 + m:21 + m],
                                                     bank[PY[m % 2]][:, :], ALU.mult, ALU.add).then_inc(yt_ready, 1)

        @block.gpsimd
        def _(pool):
            with pool.Fori(0, L) as l:
                for s in range(1, B + 2):
                    if s >= 2:
                        b = s - 2
                        at(pool, var, l * B + b + 1)
                        at(pool, rstd_ready, l * B + b)
                        pool.tensor_tensor(ve[:, b % 2, :], mv[:, b % 2, :, 1], K["eps"][:, 0:TT], ALU.add).then_inc(veps, 1)
                        at(pool, veps, l * B + b + 1)
                        at(pool, xn_ready, l * B + max(0, b - 1))
                        pool.tensor_tensor(rstd[:, b % 2, :], ve[:, b % 2, :], K["mhalf"][:, 0:TT], ALU.pow).then_inc(rstd_ready, 1)
                        if b == 0:
                            pool.wait_ge(ln_loaded, l * 32 + 32)
                        at(pool, xn_ready, l * B + b + 1)
                        pool.tensor_tensor(xg[:, b % 2, :, :], xn[:, b % 2, :, :], ln_g[:, :].rearrange("p (o d) -> p o d", o=1).broadcast_to([P, TT, D]), ALU.mult).then_inc(xg_ready, 1)
                        at(pool, xg_ready, l * B + b + 1)
                        pool.tensor_tensor(h[:, b, :, :], xg[:, b % 2, :, :], ln_b[:, :].rearrange("p (o d) -> p o d", o=1).broadcast_to([P, TT, D]), ALU.add).then_inc(x_ready, 1)
                    if s <= B:
                        b = s - 1
                        for m in range(MI):
                            f = b * MI + m
                            at(pool, yt_ready, l * (B * MI) + f + 1)
                            at(pool, g_ready, l * (B * MI) + f + 1)
                            if m == 0:
                                at(pool, o_psum, l * (2 * B) + max(0, 2 * (b - 1)))
                            pool.tensor_tensor(yg[:, b % 2, m, :], yt[:, m % 2, :], sg[:, b % 2, m, :], ALU.mult).then_inc(yg_ready, 1)


class Norm:

    def __init__(self, ctx, nc, K, name, banks):
        sem = lambda n: K["sem"](f"{name}_{n}")
        sb = lambda n, s: ctx.enter_context(nc.sbuf_tensor(f"{name}_{n}", s, F32))
        self.h, self.ident, self.K = K["h"], K["ident"], K
        self.banks = banks
        self.st, self.mv, self.ve, self.rstd = sb("st", [P, TT, 6]), sb("mv", [P, TT, 2]), sb("ve", [P, TT]), sb("rstd", [P, TT])
        self.spare = sb("spare", [P, 1])
        self.xn, self.xT = sb("xn", [P, TT, D]), sb("xT", [P, KD, T])
        self.stats, self.var, self.veps, self.rstd_ready = sem("stats"), sem("var"), sem("veps"), sem("rstd_ready")
        self.xn_ready, self.xT_psum, self.xT_ready = sem("xn_ready"), sem("xT_psum"), sem("xT_ready")
        self.sems = (self.stats, self.var, self.veps, self.rstd_ready, self.xn_ready, self.xT_psum, self.xT_ready)

    def dve_stats(self, dve, b, hb=None):
        hb = b if hb is None else hb
        for t in range(TT):
            i = dve.bn_stats(self.st[:, t, :], self.h[:, hb, t, :])
        i.then_inc(self.stats, 1)
        at(dve, self.stats, b + 1)
        at(dve, self.veps, b)
        dve.memset(self.spare[:, :], 0.0)
        for t in range(TT):
            i = dve.bn_aggr(self.mv[:, t, :], self.st[:, t, :])
        i.then_inc(self.var, 1)

    def pool_rstd(self, pool, b):
        at(pool, self.var, b + 1)
        at(pool, self.rstd_ready, b)
        pool.tensor_tensor(self.ve[:, :], self.mv[:, :, 1], self.K["eps"][:, 0:TT], ALU.add).then_inc(self.veps, 1)
        at(pool, self.veps, b + 1)
        at(pool, self.xn_ready, b)
        pool.tensor_tensor(self.rstd[:, :], self.ve[:, :], self.K["mhalf"][:, 0:TT], ALU.pow).then_inc(self.rstd_ready, 1)

    def dve_apply(self, dve, b, hb=None):
        hb = b if hb is None else hb
        at(dve, self.rstd_ready, b + 1)
        at(dve, self.xT_psum, b)
        for t in range(TT):
            i = dve.tensor_scalar(self.xn[:, t, :], self.h[:, hb, t, :], self.mv[:, t, 0:1], self.rstd[:, t:t + 1],
                                  ALU.subtract, ALU.mult)
        i.then_inc(self.xn_ready, 1)

    def pe_turn(self, pe, b):
        at(pe, self.xn_ready, b + 1)
        for k in range(KD):
            for t in range(TT):
                mm = pe.transpose(self.banks[k][:, t * P:(t + 1) * P], self.xn[:, t, k * P:(k + 1) * P], self.ident[:, :])
        mm.then_inc(self.xT_psum, 1)

    def act_copy(self, act, b):
        at(act, self.xT_psum, b + 1)
        for k in range(KD):
            i = act.activation(self.xT[:, k, :], self.banks[k][:, :], ACT.Copy)
        i.then_inc(self.xT_ready, 1)


def start(eng, *sems):
    for q in sems:
        eng.sem_inc(q, START)


def scan_stage(nc, K, a):
    S, SP2, LIM, SURE = 16, 8, 10000.0, 9000.0
    with ExitStack() as ctx:
        sem = lambda n: K["sem"]("s2_" + n)
        sb = lambda n, s, d=F32: ctx.enter_context(nc.sbuf_tensor("s2_" + n, s, d))
        h, ident, bank = K["h"], K["ident"], K["bank"]
        nm = Norm(ctx, nc, K, "s2n", (bank[0], bank[1]))
        w_in, w_x, w_dt, w_out = sb("w_in", [P, KD, 2 * INNER]), sb("w_x", [P, MI, 33]), sb("w_dt", [P, MI, P]), sb("w_out", [P, MI, D])
        par = sb("par", [P, 16 + 4 * MI])
        a_log, neg_a = sb("a_log", [P, MI, S]), sb("neg_a", [P, MI, S])
        acc, xc, sz = sb("acc", [P, 2, T]), sb("xc", [P, MI, T]), sb("sz", [P, MI, T])
        pre, soft = sb("pre", [P, MI, T]), sb("soft", [P, MI, T])
        dt, bc = sb("dt", [P, MI, T]), sb("bc", [P, TT, 2 * S])
        dtxT, w = sb("dtxT", [P, TT, INNER]), sb("w", [P, 2, TT, INNER])
        dA, hs, y = sb("dA", [P, 2, MI, T]), sb("hs", [P, 2, MI, T]), sb("y", [P, TT, INNER])
        dtx, y2 = soft, pre
        yg = sb("yg", [P, MI, T])

        a_inv, absmax, allmax, bound, clips = sb("a_inv", [P, MI]), sb("absmax", [P, 2]), sb("allmax", [1, 2]), sb("bound", [1, 1]), sb("clips", [1, 1], I32)
        step_sum = sb("step_sum", [P, 1])
        absmax_psum = sem("absmax_psum")
        bnd, absmax_ready, allmax_ready, clips_ready = sem("bnd"), sem("absmax_ready"), sem("allmax_ready"), sem("clips_ready")

        loaded, neg_a_ready, w_dt_ready = sem("loaded"), sem("neg_a_ready"), sem("w_dt_ready")
        p_psum, p_tap, p_conv1, p_conv2, p_conv, xc_ready = sem("p_psum"), sem("p_tap"), sem("p_conv1"), sem("p_conv2"), sem("p_conv"), sem("xc_ready")
        z_psum, sz_ready = sem("z_psum"), sem("sz_ready")
        bc_psum, bc_ready, raw_psum = sem("bc_psum"), sem("bc_ready"), sem("raw_psum")
        pre_ready, abs_ready, exp_ready, ln_ready, dt_ready, dtx_ready = (
            sem("pre_ready"), sem("abs_ready"), sem("exp_ready"), sem("ln_ready"), sem("dt_ready"), sem("dtx_ready"))
        dtxT_psum, dtxT_ready = sem("dtxT_psum"), sem("dtxT_ready")
        w_pool, w_act, dA_ready, dBx_psum, hs_ready, hsT_psum, y_zero, y_added = (
            sem("w_pool"), sem("w_act"), sem("dA_ready"), sem("dBx_psum"), sem("hs_ready"), sem("hsT_psum"), sem("y_zero"), sem("y_added"))
        yT_psum, y2_ready, yg_ready, o_psum, h_ready = sem("yT_psum"), sem("y2_ready"), sem("yg_ready"), sem("o_psum"), sem("h_ready")
        block = ctx.enter_context(nc.Block())

        @block.sync
        def _(sp):
            start(sp, *nm.sems, absmax_psum, bnd, absmax_ready, allmax_ready, clips_ready, p_psum, p_tap, p_conv1, p_conv2, p_conv, xc_ready, z_psum, sz_ready, bc_psum, bc_ready, raw_psum,
                  pre_ready, abs_ready, exp_ready, ln_ready, dt_ready, dtx_ready, dtxT_psum, dtxT_ready, w_pool, w_act, dA_ready,
                  dBx_psum, hs_ready, hsT_psum, y_zero, y_added, yT_psum, y2_ready, yg_ready, o_psum, h_ready)
            for to, src in ((w_in[:, :, :], a["s2_in"]), (w_x[:, :, :], a["s2_x"]), (w_out[:, :, :], a["s2_out"]),
                            (par[:, :], a["s2_par"]), (a_log[:, :, :], a["s2_alog"])):
                sp.dma_start(to, src).then_inc(loaded, 16)

        @block.tensor
        def _(pe):
            pe.wait_ge(loaded, 80)
            pe.wait_ge(w_dt_ready, MI)
            with pe.Fori(0, B) as b:
                at(pe, h_ready, b * 2)
                nm.pe_turn(pe, b)
                at(pe, nm.xT_ready, b + 1)
                for m in range(MI):
                    at(pe, p_conv, b * MI + max(0, m - 1))
                    for k in range(KD):
                        mm = pe.matmul(bank[2 + m % 2][:, :], w_in[:, k, m * P:(m + 1) * P], nm.xT[:, k, :], start=(k == 0), stop=(k == KD - 1))
                    mm.then_inc(p_psum, 1)
                    at(pe, sz_ready, b * MI + m)
                    for k in range(KD):
                        mm = pe.matmul(bank[4][:, :], w_in[:, k, INNER + m * P:INNER + (m + 1) * P], nm.xT[:, k, :], start=(k == 0), stop=(k == KD - 1))
                    mm.then_inc(z_psum, 1)
                at(pe, xc_ready, (b + 1) * MI)
                for k in range(MI):
                    mm = pe.matmul(bank[6][:, :], w_dt[:, k, :], xc[:, k, :], start=(k == 0), stop=(k == MI - 1))
                mm.then_inc(raw_psum, 1)
                for t in range(TT):
                    for k in range(MI):
                        mm = pe.matmul(bank[5][:, t * 2 * S:(t + 1) * 2 * S], xc[:, k, t * P:(t + 1) * P], w_x[:, k, 1:33], start=(k == 0), stop=(k == MI - 1))
                mm.then_inc(bc_psum, 1)
                at(pe, absmax_ready, (b + 1) * 2)
                for i in range(2):
                    mm = pe.transpose(bank[7][0:1, i * P:(i + 1) * P], absmax[:, i:i + 1], ident[:, :])
                mm.then_inc(absmax_psum, 1)
                at(pe, dtx_ready, (b + 1) * MI)
                for t in range(TT):
                    for k in range(MI):
                        mm = pe.transpose(bank[t][:, k * P:(k + 1) * P], dtx[:, k, t * P:(t + 1) * P], ident[:, :])
                    mm.then_inc(dtxT_psum, 1)
                with pe.Fori(0, SP2) as j:
                    at(pe, dtxT_ready, (b + 1) * TT)
                    at(pe, bc_ready, b + 1)
                    at(pe, pre_ready, (b + 1) * MI)
                    for p in range(2):
                        at(pe, w_pool, b * (2 * S) + j * 4 + 2 * p + 2)
                        at(pe, w_act, b * (2 * S) + j * 4 + 2 * p + 2)
                        for c in range(MI):
                            at(pe, hs_ready, b * (S * MI) + j * (2 * MI) + (p - 1) * MI + c + 1)
                            for t in range(TT):
                                mm = pe.transpose(bank[c][:, t * P:(t + 1) * P], w[:, p, t, c * P:(c + 1) * P], ident[:, :])
                            mm.then_inc(dBx_psum, 1)
                    for p in range(2):
                        at(pe, hs_ready, b * (S * MI) + j * (2 * MI) + (p + 1) * MI)
                        for t in range(TT):
                            at(pe, y_added, b * (S * TT) + j * (2 * TT) + (p - 1) * TT + t + 1)
                            for c in range(MI):
                                mm = pe.transpose(bank[4 + t][:, c * P:(c + 1) * P], hs[:, p, c, t * P:(t + 1) * P], ident[:, :])
                            mm.then_inc(hsT_psum, 1)
                at(pe, y_added, (b + 1) * (S * TT))
                for c in range(MI):
                    for t in range(TT):
                        mm = pe.transpose(bank[c][:, t * P:(t + 1) * P], y[:, t, c * P:(c + 1) * P], ident[:, :])
                    mm.then_inc(yT_psum, 1)
                at(pe, yg_ready, (b + 1) * MI)
                for g in range(2):
                    for t in range(2):
                        for k in range(MI):
                            mm = pe.matmul(bank[4 + g][:, t * D:(t + 1) * D], yg[:, k, (2 * g + t) * P:(2 * g + t + 1) * P], w_out[:, k, :],
                                           start=(k == 0), stop=(k == MI - 1))
                    mm.then_inc(o_psum, 1)

        @block.scalar
        def _(act):
            act.wait_ge(loaded, 80)
            act.wait_ge(neg_a_ready, 1)
            act.activation(neg_a[:, :, :], a_log[:, :, :], ACT.Exp).then_inc(neg_a_ready, 1)
            act.wait_ge(neg_a_ready, 3)
            with act.Fori(0, B) as b:
                nm.act_copy(act, b)

                def silu_x(m):
                    at(act, p_conv, b * MI + m + 1)
                    act.activation(xc[:, m, :], acc[:, m % 2, :], ACT.Silu).then_inc(xc_ready, 1)

                for m in range(MI):
                    at(act, p_psum, b * MI + m + 1)
                    at(act, xc_ready, b * MI + max(0, m - 1))
                    act.activation(acc[:, m % 2, :], bank[2 + m % 2][:, :], ACT.Identity,
                                   bias=par[:, 16 + m:17 + m], scale=par[:, 4 * m + 3:4 * m + 4]).then_inc(p_tap, 1)
                    at(act, z_psum, b * MI + m + 1)
                    act.activation(sz[:, m, :], bank[4][:, :], ACT.Silu).then_inc(sz_ready, 1)
                    if m:
                        silu_x(m - 1)
                silu_x(MI - 1)
                for m in range(MI):
                    at(act, pre_ready, b * MI + m + 1)
                    act.activation(soft[:, m, :], pre[:, m, :], ACT.Abs).then_inc(abs_ready, 1)
                for m in range(MI):
                    at(act, abs_ready, b * MI + m + 1)
                    act.activation(soft[:, m, :], soft[:, m, :], ACT.Exp, scale=-1.0).then_inc(exp_ready, 1)
                for m in range(MI):
                    at(act, exp_ready, b * MI + m + 1)
                    act.activation(soft[:, m, :], soft[:, m, :], ACT.Ln, bias=1.0).then_inc(ln_ready, 1)
                for t in range(TT):
                    at(act, dtxT_psum, b * TT + t + 1)
                    act.activation(dtxT[:, t, :], bank[t][:, :], ACT.Copy).then_inc(dtxT_ready, 1)
                with act.Fori(0, SP2) as j:
                    at(act, bc_ready, b + 1)
                    at(act, dt_ready, (b + 1) * MI)
                    at(act, dtxT_ready, (b + 1) * TT)
                    for p in range(2):
                        at(act, hs_ready, b * (S * MI) + j * (2 * MI) + (p - 1) * MI)
                        for c in range(MI):
                            act.activation(dA[:, p, c, :], dt[:, c, :], ACT.Exp, scale=neg_a[:, c, :][:, bass.ds(j * 2 + p, 1)]).then_inc(dA_ready, 1)
                        at(act, dBx_psum, b * (S * MI) + j * (2 * MI) + (p - 1) * MI)
                        for t in (2, 3):
                            act.activation(w[:, p, t, :], dtxT[:, t, :], ACT.Copy, scale=bc[:, t, :][:, bass.ds(j * 2 + p, 1)]).then_inc(w_act, 1)

        @block.vector
        def _(dve):
            dve.wait_ge(loaded, 80)
            dve.tensor_scalar(a_log[:, :, :], a_log[:, :, :], -6.0, 6.0, ALU.max, ALU.min).then_inc(neg_a_ready, 1)
            for k in range(MI):
                dve.tensor_scalar(w_dt[:, k, :], K["ones"][:, :], w_x[:, k, 0:1], None, ALU.mult).then_inc(w_dt_ready, 1)
            dve.wait_ge(neg_a_ready, 2)
            dve.tensor_reduce(a_inv[:, :], neg_a[:, :, :], AX.X, ALU.min).then_inc(w_dt_ready, 1)
            dve.wait_ge(w_dt_ready, MI + 1)
            dve.reciprocal(a_inv[:, :], a_inv[:, :]).then_inc(w_dt_ready, 1)
            dve.wait_ge(w_dt_ready, MI + 2)
            dve.tensor_scalar(neg_a[:, :, :], neg_a[:, :, :], -1.0, None, ALU.mult).then_inc(neg_a_ready, 1)
            with dve.Fori(0, B) as b:
                nm.dve_stats(dve, b)
                nm.dve_apply(dve, b)
                for m in range(MI):
                    pb = bank[2 + m % 2]
                    for i, got, done in ((1, p_tap, p_conv1), (2, p_conv1, p_conv2), (3, p_conv2, p_conv)):
                        at(dve, got, b * MI + m + 1)
                        dve.scalar_tensor_tensor(acc[:, m % 2, i:T], pb[:, 0:T - i], par[:, 4 * m + 3 - i:4 * m + 4 - i],
                                                 acc[:, m % 2, i:T], ALU.mult, ALU.add).then_inc(done, 1)
                at(dve, yg_ready, b * MI)
                for m in range(MI):
                    at(dve, raw_psum, b + 1)
                    dve.tensor_scalar(pre[:, m, :], bank[6][:, :], par[:, 20 + m:21 + m], par[:, 24 + m:25 + m], ALU.mult, ALU.add).then_inc(pre_ready, 1)
                at(dve, bc_psum, b + 1)
                dve.tensor_copy(bc[:, :, :].rearrange("p t s -> p (t s)"), bank[5][:, 0:TT * 2 * S]).then_inc(bc_ready, 1)
                for m in range(MI):
                    at(dve, ln_ready, b * MI + m + 1)
                    dve.scalar_tensor_tensor(dt[:, m, :], pre[:, m, :], 0.0, soft[:, m, :], ALU.max, ALU.add).then_inc(dt_ready, 1)
                for m in range(MI):
                    at(dve, dt_ready, b * MI + m + 1)
                    dve.tensor_tensor(dtx[:, m, :], dt[:, m, :], xc[:, m, :], ALU.mult).then_inc(dtx_ready, 1)
                at(dve, yT_psum, b * MI)
                for m in range(MI):
                    dve.scalar_tensor_tensor(y[:, m, :], dt[:, m, :], a_inv[:, m:m + 1], xc[:, m, :], ALU.add, ALU.mult).then_inc(bnd, 1)
                at(dve, bnd, (b + 1) * MI)
                dve.tensor_reduce(absmax[:, 0:1], y[:, :, :].rearrange("p t s -> p (t s)"), AX.X, ALU.max, apply_absolute_value=True).then_inc(absmax_ready, 1)
                dve.tensor_reduce(absmax[:, 1:2], bc[:, :, 0:S], AX.XY, ALU.max, apply_absolute_value=True).then_inc(absmax_ready, 1)
                at(dve, absmax_ready, b * 2 + 1)
                dve.memset(y[:, :, :], 0.0).then_inc(y_zero, 1)
                at(dve, absmax_psum, b + 1)
                dve.tensor_reduce(allmax[:, :], bank[7][0:1, 0:2 * P].rearrange("p (i c) -> p i c", i=2), AX.X, ALU.max).then_inc(allmax_ready, 1)
                at(dve, allmax_ready, b + 1)
                dve.tensor_tensor(bound[:, :], allmax[0:1, 0:1], allmax[0:1, 1:2], ALU.mult).then_inc(clips_ready, 1)
                at(dve, clips_ready, b * 2 + 1)
                dve.tensor_scalar(clips[:, :], bound[:, :], SURE, None, ALU.is_le).then_inc(clips_ready, 1)
                at(dve, clips_ready, b * 2 + 2)
                dve.memset(nm.spare[:, :], 0.0)
                sure = dve.value_load(clips[0:1, 0:1], min_val=0, max_val=1)
                with dve.Fori(0, SP2) as j:
                    for p in range(2):
                        for c in range(MI):
                            def operands():
                                at(dve, hsT_psum, b * (S * TT) + j * (2 * TT))
                                at(dve, dA_ready, b * (S * MI) + j * (2 * MI) + p * MI + c + 1)
                                at(dve, dBx_psum, b * (S * MI) + j * (2 * MI) + p * MI + c + 1)

                            with dve.If(sure == 1):
                                operands()
                                dve.tensor_tensor_scan(hs[:, p, c, :], dA[:, p, c, :], bank[c][:, :], 0.0, ALU.mult, ALU.add).then_inc(hs_ready, 1)
                            with dve.Else():
                                operands()
                                dve.tensor_scalar(hs[:, p, c, 0:1], bank[c][:, 0:1], -LIM, LIM, ALU.max, ALU.min)
                                with dve.Fori(0, T - 1) as n:
                                    dve.drain()
                                    dve.scalar_tensor_tensor(step_sum[:, :], dA[:, p, c, bass.ds(n + 1, 1)], hs[:, p, c, bass.ds(n, 1)],
                                                             bank[c][:, bass.ds(n + 1, 1)], ALU.mult, ALU.add)
                                    dve.drain()
                                    dve.tensor_scalar(hs[:, p, c, bass.ds(n + 1, 1)], step_sum[:, :], -LIM, LIM, ALU.max, ALU.min)
                                dve.drain().then_inc(hs_ready, 1)
                    for p in range(2):
                        at(dve, y_zero, b + 1)
                        at(dve, y_added, b * (S * TT) + j * (2 * TT) + p * TT)
                        for t in range(TT):
                            at(dve, hsT_psum, b * (S * TT) + j * (2 * TT) + p * TT + t + 1)
                            dve.scalar_tensor_tensor(y[:, t, :], bank[4 + t][:, :], bc[:, t, :][:, bass.ds(j * 2 + (S + p), 1)],
                                                     y[:, t, :], ALU.mult, ALU.add).then_inc(y_added, 1)
                for c in range(MI):
                    at(dve, yT_psum, b * MI + c + 1)
                    dve.scalar_tensor_tensor(y2[:, c, :], xc[:, c, :], par[:, 28 + c:29 + c], bank[c][:, :], ALU.mult, ALU.add).then_inc(y2_ready, 1)
                for g in range(2):
                    at(dve, o_psum, b * 2 + g + 1)
                    hb = h[:, b, 2 * g:2 * g + 2, :].rearrange("p t d -> p (t d)")
                    dve.tensor_tensor(hb, bank[4 + g][:, :], hb, ALU.add).then_inc(h_ready, 1)
                at(dve, h_ready, (b + 1) * 2)

        @block.gpsimd
        def _(pool):
            with pool.Fori(0, B) as b:
                nm.pool_rstd(pool, b)
                with pool.Fori(0, SP2) as j:
                    at(pool, bc_ready, b + 1)
                    at(pool, dtxT_ready, (b + 1) * TT)
                    for p in range(2):
                        at(pool, dBx_psum, b * (S * MI) + j * (2 * MI) + (p - 1) * MI)
                        for t in (0, 1):
                            pool.tensor_tensor(w[:, p, t, :], dtxT[:, t, :], bc[:, t, :][:, bass.ds(j * 2 + p, 1)].broadcast_to([P, INNER]), ALU.mult).then_inc(w_pool, 1)
                for c in range(MI):
                    at(pool, y2_ready, b * MI + c + 1)
                    at(pool, o_psum, b * 2)
                    pool.tensor_tensor(yg[:, c, :], y2[:, c, :], sz[:, c, :], ALU.mult).then_inc(yg_ready, 1)


def slot_stage(nc, K, a):
    H, NS, F = 16, 16, 1024
    HS, R, KF = H * NS, B * NS, F // P
    G, GW = 4, 32
    NQ = NS // G
    with ExitStack() as ctx:
        sem = lambda n: K["sem"]("s3_" + n)
        sb = lambda n, s, d=F32: ctx.enter_context(nc.sbuf_tensor("s3_" + n, s, d))
        h, ident, bank = K["h"], K["ident"], K["bank"]
        nm = Norm(ctx, nc, K, "s3n", (bank[0], bank[1]))
        wts = {n: sb(n, [P, KD, D]) for n in ("dWq", "dWkT", "dWv", "dWo", "cWqT", "cWk", "cWv", "cWo")}
        cols = sb("cols", [P, KD, 7])
        e_bias, e_b2 = sb("e_bias", [P, 2 * F]), sb("e_b2", [P, KD, NS])
        slotT, rows = sb("slotT", [P, KD, NS]), sb("rows", [R, 4, D])
        c_bo = sb("c_bo", [P, D])
        W1, Wg, W2 = sb("W1", [P, G, KD, F]), sb("Wg", [P, G, KD, F]), sb("W2", [P, G, KF, D])
        mask = sb("mask", [P, KD, H])
        bqw = sb("bqw", [P, KD, P])
        qh, qblk, md, sbias = sb("qh", [P, KD, NS]), sb("qblk", [P, KD, HS]), sb("md", [P, KD, HS]), sb("sbias", [P, 2])
        mx, top, nb, sm, rs = (sb(n, [P, 2]) for n in ("mx", "top", "nb", "sm", "rs"))
        pr, prT, gT = sb("pr", [P, 2, T]), sb("prT", [P, TT, HS]), sb("gT", [P, KD, HS])
        own, att, attb = sb("own", [P, KD, HS]), sb("att", [P, B, KD, NS]), sb("attb", [P, KD, R])
        o, qbo, st, mv, ve, rstd, on, og, ob = (sb("o", [R, D]), sb("qbo", [R, D]), sb("st", [R, 6]), sb("mv", [R, 2]), sb("ve", [R, 1]),
                                               sb("rstd", [R, 1]), sb("on", [R, D]), sb("og", [R, D]), sb("ob", [R, D]))
        oT, hT, oTb, o2T = (sb(n, [P, KD, NS, B]) for n in ("oT", "hT", "oTb", "o2T"))
        hx = sb("hx", [P, KD, G, GW])
        pre, ug, ugT, yx = sb("pre", [P, 2 * F]), sb("ug", [P, F]), sb("ugT", [P, KF, G * GW]), sb("yx", [P, D])
        kc, vc = sb("kc", [P, KD, B, NS]), sb("vc", [P, KD, B, NS])
        kblk, vblk, mb, rb, vw = sb("kblk", [P, KD, HS]), sb("vblk", [P, KD, HS]), sb("mb", [P, KD, HS]), sb("rb", [P, HS]), sb("vw", [P, 2, D])
        by_tile = lambda x: x.rearrange("p (t s) -> p t s", t=TT)
        cm, cs, cr = sb("cm", [P, TT * H]), sb("cs", [P, TT * H]), sb("cr", [P, TT * H])
        sc, cp = by_tile(pr[:, :, :].rearrange("p g t -> p (g t)")), prT
        ce, cd, cpT = by_tile(ug[:, :]), by_tile(ugT[:, :, :].rearrange("p f c -> p (f c)")), pre[:, 0:2 * T].rearrange("p (g t) -> p g t", g=2)

        loaded, bias_loaded, W1_loaded, Wg_loaded, W2_loaded = sem("loaded"), sem("bias_loaded"), sem("W1_loaded"), sem("Wg_loaded"), sem("W2_loaded")
        bias_zero, hx_ready, ugT_psum, ugT_ready, yx_ready, yT_psum = sem("bias_zero"), sem("hx_ready"), sem("ugT_psum"), sem("ugT_ready"), sem("yx_ready"), sem("yT_psum")
        mask1, masked, setup_pe, setup_dve, qblk_ready = sem("mask1"), sem("masked"), sem("setup_pe"), sem("setup_dve"), sem("qblk_ready")
        s_psum, mx_ready, top_ready, nb_ready, pr_exp, rs_ready, pr_ready = (
            sem(n) for n in ("s_psum", "mx_ready", "top_ready", "nb_ready", "pr_exp", "rs_ready", "pr_ready"))
        prT_psum, prT_ready, g_psum, g_ready, v_psum, own_ready, att_ready = (
            sem(n) for n in ("prT_psum", "prT_ready", "g_psum", "g_ready", "v_psum", "own_ready", "att_ready"))
        o_psum, join, jpool, jpe, jact = sem("o_psum"), sem("join"), sem("jpool"), sem("jpe"), sem("jact")
        u_psum, pre_ready, silu_ready, ug_ready, y_psum, o2_ready = (sem(n) for n in ("u_psum", "pre_ready", "silu_ready", "ug_ready", "y_psum", "o2_ready"))
        kv_psum, kv_ready = sem("kv_psum"), sem("kv_ready")
        kblk_ready, mb_psum, mb_ready, rb_psum, rb_ready, vw_psum, vw_ready = (
            sem(n) for n in ("kblk_ready", "mb_psum", "mb_ready", "rb_psum", "rb_ready", "vw_psum", "vw_ready"))
        sc_psum, sc_ready, cm_ready, cd_ready, ce_ready, cs_ready, cr_ready, cp_ready = (
            sem(n) for n in ("sc_psum", "sc_ready", "cm_ready", "cd_ready", "ce_ready", "cs_ready", "cr_ready", "cp_ready"))
        cpT_psum, cpT_ready, c_psum, hb_ready, h_ready = (sem(n) for n in ("cpT_psum", "cpT_ready", "c_psum", "hb_ready", "h_ready"))
        NLOAD = 16 * (len(wts) + 6)
        block = ctx.enter_context(nc.Block())
        headmask = lambda k: mask[:, k, :].rearrange("p (h o) -> p h o", o=1).broadcast_to([P, H, NS])
        by_head = lambda x: x.rearrange("p (h s) -> p h s", h=H)
        over_heads = lambda x: x.rearrange("p (o s) -> p o s", o=1).broadcast_to([P, H, NS])

        @block.sync
        def _(sp):
            start(sp, *nm.sems, s_psum, mx_ready, top_ready, nb_ready, pr_exp, rs_ready, pr_ready, prT_psum, prT_ready, g_psum, g_ready,
                  v_psum, own_ready, att_ready, hx_ready, ugT_psum, ugT_ready, yx_ready, yT_psum, u_psum, pre_ready, silu_ready, ug_ready, y_psum, o2_ready,
                  kblk_ready, mb_psum, mb_ready, rb_psum, rb_ready, vw_psum, vw_ready, sc_psum, sc_ready, cm_ready, cd_ready,
                  ce_ready, cs_ready, cr_ready, cp_ready, cpT_psum, cpT_ready, c_psum, hb_ready, h_ready)
            for n, t in wts.items():
                sp.dma_start(t[:, :, :], a["s3_" + n]).then_inc(loaded, 16)
            for to, src in ((cols[:, :, :], a["s3_cols"]), (e_b2[:, :, :], a["s3_b2"]),
                            (slotT[:, :, :], a["s3_slotT"]), (rows[:, :, :], a["s3_rows"]), (c_bo[:, :], a["s3_cbo"].broadcast_to([P, D]))):
                sp.dma_start(to, src).then_inc(loaded, 16)
            sp.dma_start(mask[:, :, :], a["s3_mask"]).then_inc(loaded, 16)
            sp.wait_ge(bias_zero, 1)
            with sp.Fori(0, NQ) as q:
                at(sp, pre_ready, q * 4)
                for g in range(G):
                    sp.dma_start(e_bias[GW * g:GW * g + B, :], a["s3_bias"][bass.ds(q * G + g, 1), :].broadcast_to([B, 2 * F])).then_inc(bias_loaded, 16)
                for w, name, done, used in ((W1, "s3_W1", W1_loaded, q * 4), (Wg, "s3_Wg", Wg_loaded, q * 4)):
                    at(sp, u_psum, used - (2 if w is W1 else 0))
                    for g in range(G):
                        sp.dma_start(w[:, g, :, :], a[name][q * G + g]).then_inc(done, 16)
                at(sp, y_psum, q)
                for g in range(G):
                    sp.dma_start(W2[:, g, :, :], a["s3_W2"][q * G + g]).then_inc(W2_loaded, 16)

        @block.tensor
        def _(pe):
            pe.wait_ge(loaded, NLOAD)
            for m in range(KD):
                for k in range(KD):
                    mm = pe.matmul(bank[2][:, m * NS:(m + 1) * NS], wts["dWq"][:, k, m * P:(m + 1) * P], slotT[:, k, :], start=(k == 0), stop=(k == KD - 1))
            mm.then_inc(setup_pe, 1)
            pe.wait_ge(qblk_ready, KD)
            for m in range(KD):
                for k in range(KD):
                    mm = pe.matmul(bank[3][:, m * HS:(m + 1) * HS], wts["dWkT"][:, k, m * P:(m + 1) * P], qblk[:, k, :], start=(k == 0), stop=(k == KD - 1))
            for g in range(2):
                for k in range(KD):
                    mm = pe.matmul(bank[4][:, g:g + 1], qblk[:, k, g * P:(g + 1) * P], cols[:, k, 1:2], start=(k == 0), stop=(k == KD - 1))
            mm.then_inc(setup_pe, 1)
            pe.wait_ge(setup_dve, 3)
            with pe.Fori(0, B) as b:
                nm.pe_turn(pe, b)
                at(pe, nm.xT_ready, b + 1)
                for g in range(2):
                    at(pe, pr_exp, b * 2 + g)
                    for k in range(KD):
                        mm = pe.matmul(bank[2 + g][:, :], md[:, k, g * P:(g + 1) * P], nm.xT[:, k, :], start=(k == 0), stop=(k == KD - 1))
                    mm.then_inc(s_psum, 1)
                at(pe, pr_ready, (b + 1) * 2)
                for q in range(2):
                    for t in range(2):
                        for g in range(2):
                            mm = pe.transpose(bank[4 + q][:, t * HS + g * P:t * HS + (g + 1) * P], pr[:, g, (2 * q + t) * P:(2 * q + t + 1) * P], ident[:, :])
                    mm.then_inc(prT_psum, 1)
                at(pe, prT_ready, (b + 1) * 2)
                for m in range(KD):
                    for t in range(TT):
                        mm = pe.matmul(bank[6][:, m * HS:(m + 1) * HS], nm.xn[:, t, m * P:(m + 1) * P], prT[:, t, :], start=(t == 0), stop=(t == TT - 1))
                mm.then_inc(g_psum, 1)
                at(pe, g_ready, b + 1)
                at(pe, own_ready, b * KD)
                for m in range(KD):
                    for k in range(KD):
                        mm = pe.matmul(bank[7][:, m * HS:(m + 1) * HS], wts["dWv"][:, k, m * P:(m + 1) * P], gT[:, k, :], start=(k == 0), stop=(k == KD - 1))
                mm.then_inc(v_psum, 1)
            pe.wait_ge(join, KD)
            for k in range(KD):
                mm = pe.matmul(bank[0][0:R, 0:D], attb[:, k, :], wts["dWo"][:, k, :], start=(k == 0), stop=(k == KD - 1))
            mm.then_inc(jpe, 1)
            pe.wait_ge(join, KD + 2)
            for k in range(KD):
                mm = pe.transpose(bank[1][:, k * R:(k + 1) * R], o[:, k * P:(k + 1) * P], ident[0:R, 0:R])
            mm.then_inc(jpe, 1)
            pe.wait_ge(jpool, 4)
            for k in range(KD):
                mm = pe.transpose(bank[2][:, k * R:(k + 1) * R], ob[:, k * P:(k + 1) * P], ident[0:R, 0:R])
            mm.then_inc(jpe, 1)
            with pe.Fori(0, NQ) as q:
                at(pe, hx_ready, q + 1)
                for j, (w, there) in enumerate(((W1, W1_loaded), (Wg, Wg_loaded))):
                    pe.wait_ge(there, (q + 1) * (16 * G))
                    for c in range(2):
                        at(pe, pre_ready, q * 4 + (2 * j + c + 1) - 4)
                        for k in range(KD):
                            for g in range(G):
                                mm = pe.matmul(bank[2 * j + c][GW * g:GW * (g + 1), :], hx[:, k, g, :], w[:, g, k, c * 512:(c + 1) * 512],
                                               start=(k == 0), stop=(k == KD - 1))
                        mm.then_inc(u_psum, 1)
                at(pe, ug_ready, q + 1)
                for f in range(KF):
                    mm = pe.transpose(bank[4 + f // 4][:, (f % 4) * P:(f % 4 + 1) * P], ug[:, f * P:(f + 1) * P], ident[:, :])
                mm.then_inc(ugT_psum, 1)
                at(pe, ugT_ready, q * 2 + 2)
                pe.wait_ge(W2_loaded, (q + 1) * (16 * G))
                for f in range(KF):
                    for g in range(G):
                        mm = pe.matmul(bank[6][GW * g:GW * (g + 1), 0:D], ugT[:, f, GW * g:GW * (g + 1)], W2[:, g, f, :], start=(f == 0), stop=(f == KF - 1))
                mm.then_inc(y_psum, 1)
                at(pe, yx_ready, q + 1)
                for k in range(KD):
                    mm = pe.transpose(bank[7][:, k * P:(k + 1) * P], yx[:, k * P:(k + 1) * P], ident[:, :])
                mm.then_inc(yT_psum, 1)
            pe.wait_ge(o2_ready, NQ * KD + START)
            for j, w in enumerate(("cWk", "cWv")):
                for m in range(KD):
                    for k in range(KD):
                        mm = pe.matmul(bank[6 + j][:, m * R:(m + 1) * R], wts[w][:, k, m * P:(m + 1) * P], o2T[:, k, :, :].rearrange("p s b -> p (s b)"), start=(k == 0), stop=(k == KD - 1))
                mm.then_inc(kv_psum, 1)
            with pe.Fori(0, B) as b:
                nm.pe_turn(pe, b + B)
                at(pe, kblk_ready, b * (2 * KD) + 2 * KD)
                at(pe, h_ready, b * 2)
                for m in range(KD):
                    for k in range(KD):
                        mm = pe.matmul(bank[2][:, m * HS:(m + 1) * HS], wts["cWqT"][:, k, m * P:(m + 1) * P], kblk[:, k, :], start=(k == 0), stop=(k == KD - 1))
                mm.then_inc(mb_psum, 1)
                for k in range(KD):
                    mm = pe.matmul(bank[3][:, 0:HS], bqw[:, k, :], kblk[:, k, :], start=(k == 0), stop=(k == KD - 1))
                mm.then_inc(rb_psum, 1)
                for g in range(2):
                    for k in range(KD):
                        mm = pe.matmul(bank[4][:, g * D:(g + 1) * D], vblk[:, k, g * P:(g + 1) * P], wts["cWo"][:, k, :], start=(k == 0), stop=(k == KD - 1))
                mm.then_inc(vw_psum, 1)
                at(pe, nm.xT_ready, b + (B + 1))
                at(pe, mb_ready, b + 1)
                for q in range(2):
                    for t in range(2):
                        for k in range(KD):
                            mm = pe.matmul(bank[5 + q][:, t * HS:(t + 1) * HS], nm.xT[:, k, (2 * q + t) * P:(2 * q + t + 1) * P], mb[:, k, :], start=(k == 0), stop=(k == KD - 1))
                    mm.then_inc(sc_psum, 1)
                at(pe, cp_ready, b + 1)
                for g in range(2):
                    for t in range(TT):
                        mm = pe.transpose(bank[g][:, t * P:(t + 1) * P], cp[:, t, g * P:(g + 1) * P], ident[:, :])
                    mm.then_inc(cpT_psum, 1)
                at(pe, cpT_ready, b * 2 + 2)
                at(pe, vw_ready, b + 1)
                for q, bk in ((0, 2), (1, 7)):
                    for t in range(2):
                        for g in range(2):
                            mm = pe.matmul(bank[bk][:, t * D:(t + 1) * D], cpT[:, g, (2 * q + t) * P:(2 * q + t + 1) * P], vw[:, g, :], start=(g == 0), stop=(g == 1))
                    mm.then_inc(c_psum, 1)

        @block.scalar
        def _(act):
            with act.Fori(0, B) as b:
                nm.act_copy(act, b)
                for g in range(2):
                    at(act, nb_ready, b * 2 + g + 1)
                    at(act, s_psum, b * 2 + g + 1)
                    at(act, prT_psum, b * 2)
                    act.activation(pr[:, g, :], bank[2 + g][:, :], ACT.Exp, bias=nb[:, g:g + 1], accum_out=sm[:, g:g + 1]).then_inc(pr_exp, 1)
                for q in range(2):
                    at(act, prT_psum, b * 2 + q + 1)
                    at(act, g_psum, b)
                    act.activation(prT[:, 2 * q:2 * q + 2, :], bank[4 + q][:, :], ACT.Copy).then_inc(prT_ready, 1)
                at(act, g_psum, b + 1)
                at(act, v_psum, b)
                act.activation(gT[:, :, :], bank[6][:, :], ACT.Copy).then_inc(g_ready, 1)
            act.wait_ge(jpe, 2)
            for k in range(KD):
                act.activation(oT[:, k, :, :], bank[1][:, k * R:(k + 1) * R].rearrange("p (b s) -> p s b", b=B), ACT.Copy).then_inc(jact, 1)
            act.wait_ge(jpe, 3)
            for k in range(KD):
                act.activation(hT[:, k, :, :], bank[2][:, k * R:(k + 1) * R].rearrange("p (b s) -> p s b", b=B), ACT.Copy).then_inc(jact, 1)
            with act.Fori(0, NQ) as q:
                at(act, pre_ready, q * 4 + 4)
                act.activation(pre[:, :], pre[:, :], ACT.Silu).then_inc(silu_ready, 1)
                for c in range(2):
                    at(act, ugT_psum, q + 1)
                    act.activation(ugT[:, 4 * c:4 * c + 4, :], bank[4 + c][:, :], ACT.Copy).then_inc(ugT_ready, 1)
            with act.Fori(0, B) as b:
                nm.act_copy(act, b + B)
                at(act, mb_psum, b + 1)
                at(act, sc_psum, b * 2)
                act.activation(mb[:, :, :], bank[2][:, :], ACT.Copy).then_inc(mb_ready, 1)
                at(act, rb_psum, b + 1)
                at(act, sc_ready, b * 2)
                act.activation(rb[:, :], bank[3][:, 0:HS], ACT.Copy).then_inc(rb_ready, 1)
                at(act, vw_psum, b + 1)
                at(act, c_psum, b * 2)
                act.activation(vw[:, :, :], bank[4][:, :], ACT.Copy).then_inc(vw_ready, 1)
                at(act, cd_ready, b + 1)
                at(act, cp_ready, b)
                act.activation(ce[:, :, :], cd[:, :, :], ACT.Exp).then_inc(ce_ready, 1)
                for g in range(2):
                    at(act, cpT_psum, b * 2 + g + 1)
                    at(act, c_psum, b * 2)
                    act.activation(cpT[:, g, :], bank[g][:, :], ACT.Copy).then_inc(cpT_ready, 1)

        @block.vector
        def _(dve):
            dve.memset(e_bias[:, :], 0.0).then_inc(bias_zero, 1)
            dve.memset(hx[:, :, :, :], 0.0).then_inc(bias_zero, 1)
            dve.wait_ge(bias_zero, 2)
            dve.wait_ge(loaded, NLOAD)
            dve.wait_ge(setup_pe, 1)
            for m in range(KD):
                dve.tensor_scalar(qh[:, m, :], bank[2][:, m * NS:(m + 1) * NS], cols[:, m, 0:1], 0.25, ALU.add, ALU.mult).then_inc(setup_dve, 1)
            dve.wait_ge(setup_dve, 2)
            for m in range(KD):
                dve.tensor_tensor(by_head(qblk[:, m, :]), headmask(m), over_heads(qh[:, m, :]), ALU.mult).then_inc(qblk_ready, 1)
            for k in range(KD):
                dve.tensor_scalar(bqw[:, k, :], K["ones"][:, :], cols[:, k, 3:4], None, ALU.mult)
            dve.wait_ge(setup_pe, 2)
            dve.tensor_copy(sbias[:, :], bank[4][:, 0:2])
            dve.tensor_copy(md[:, :, :].rearrange("p k s -> p (k s)"), bank[3][:, :]).then_inc(setup_dve, 1)
            dve.wait_ge(setup_dve, 3)
            with dve.Fori(0, B) as b:
                nm.dve_stats(dve, b)
                at(dve, g_psum, b)
                nm.dve_apply(dve, b)
                for g in range(2):
                    at(dve, s_psum, b * 2 + g + 1)
                    at(dve, nb_ready, b * 2 + g)
                    dve.tensor_reduce(mx[:, g:g + 1], bank[2 + g][:, :], AX.X, ALU.max).then_inc(mx_ready, 1)
                    at(dve, mx_ready, b * 2 + g + 1)
                    dve.tensor_scalar(top[:, g:g + 1], mx[:, g:g + 1], sbias[:, g:g + 1], -1.0, ALU.add, ALU.mult).then_inc(top_ready, 1)
                    at(dve, top_ready, b * 2 + g + 1)
                    at(dve, pr_exp, b * 2)
                    dve.tensor_scalar(nb[:, g:g + 1], top[:, g:g + 1], sbias[:, g:g + 1], None, ALU.add).then_inc(nb_ready, 1)
                for g in range(2):
                    at(dve, pr_exp, b * 2 + g + 1)
                    dve.reciprocal(rs[:, g:g + 1], sm[:, g:g + 1]).then_inc(rs_ready, 1)
                    at(dve, rs_ready, b * 2 + g + 1)
                    dve.tensor_scalar(pr[:, g, :], pr[:, g, :], rs[:, g:g + 1], None, ALU.mult).then_inc(pr_ready, 1)
                at(dve, v_psum, b + 1)
                for m in range(KD):
                    dve.tensor_tensor(by_head(own[:, m, :]), by_head(bank[7][:, m * HS:(m + 1) * HS]), headmask(m), ALU.mult).then_inc(own_ready, 1)
                at(dve, own_ready, b * KD + KD)
                for m in range(KD):
                    dve.tensor_reduce(att[:, b, m, :], own[:, m, :].rearrange("p (h s) -> p s h", h=H), AX.X, ALU.add).then_inc(att_ready, 1)
            dve.wait_ge(att_ready, B * KD + START)
            for m in range(KD):
                dve.tensor_scalar(attb[:, m, :].rearrange("p (b s) -> p b s", b=B), att[:, :, m, :], cols[:, m, 2:3], None, ALU.add).then_inc(join, 1)
            dve.tensor_tensor(qbo[:, :], rows[:, 0, :], rows[:, 1, :], ALU.add).then_inc(join, 1)
            dve.wait_ge(join, KD + 1)
            dve.wait_ge(jpe, 1)
            dve.tensor_tensor(o[:, :], bank[0][0:R, 0:D], qbo[:, :], ALU.add).then_inc(join, 1)
            dve.wait_ge(join, KD + 2)
            dve.bn_stats(st[:, :], o[:, :]).then_inc(join, 1)
            dve.wait_ge(join, KD + 3)
            dve.bn_aggr(mv[:, :], st[:, :]).then_inc(join, 1)
            dve.wait_ge(jpool, 2)
            dve.wait_ge(join, KD + 4)
            dve.tensor_scalar(on[:, :], o[:, :], mv[:, 0:1], rstd[:, :], ALU.subtract, ALU.mult).then_inc(join, 1)
            dve.wait_ge(jact, KD)
            for k in range(KD):
                dve.tensor_tensor(oTb[:, k, :, :], oT[:, k, :, :], e_b2[:, k, :].rearrange("p (s o) -> p s o", o=1).broadcast_to([P, NS, B]), ALU.add).then_inc(jact, 1)
            dve.wait_ge(jact, 3 * KD)
            with dve.Fori(0, NQ) as q:
                at(dve, u_psum, q * 4)
                dve.tensor_copy(hx[:, :, :, 0:B], hT[:, :, bass.ds(q * G, G), :]).then_inc(hx_ready, 1)
                dve.wait_ge(bias_loaded, (q + 1) * (16 * G))
                at(dve, ug_ready, q)
                for c in range(4):
                    at(dve, u_psum, q * 4 + c + 1)
                    dve.tensor_tensor(pre[:, c * 512:(c + 1) * 512], bank[c][:, :], e_bias[:, c * 512:(c + 1) * 512], ALU.add).then_inc(pre_ready, 1)
                at(dve, silu_ready, q + 1)
                at(dve, ugT_psum, q)
                dve.tensor_tensor(ug[:, :], pre[:, 0:F], pre[:, F:2 * F], ALU.mult).then_inc(ug_ready, 1)
                at(dve, y_psum, q + 1)
                at(dve, yT_psum, q)
                dve.tensor_copy(yx[:, :], bank[6][:, 0:D]).then_inc(yx_ready, 1)
                at(dve, yT_psum, q + 1)
                for k in range(KD):
                    dve.tensor_tensor(o2T[:, k, bass.ds(q * G, G), :], bank[7][:, k * P:(k + 1) * P].rearrange("p (g c) -> p g c", g=G)[:, :, 0:B],
                                      oTb[:, k, bass.ds(q * G, G), :], ALU.add).then_inc(o2_ready, 1)
            for m in range(KD):
                dve.wait_ge(kv_psum, 1)
                dve.tensor_scalar(kc[:, m, :, :], bank[6][:, m * R:(m + 1) * R].rearrange("p (s b) -> p b s", b=B), cols[:, m, 4:5], 0.25, ALU.add, ALU.mult).then_inc(kv_ready, 1)
            for m in range(KD):
                dve.wait_ge(kv_psum, 2)
                dve.tensor_scalar(vc[:, m, :, :], bank[7][:, m * R:(m + 1) * R].rearrange("p (s b) -> p b s", b=B), cols[:, m, 5:6], None, ALU.add).then_inc(kv_ready, 1)
            dve.wait_ge(kv_ready, 2 * KD)
            with dve.Fori(0, B) as b:
                nm.dve_stats(dve, b + B, b)
                nm.dve_apply(dve, b + B, b)
                at(dve, vw_psum, b)
                for src, to in ((kc, kblk), (vc, vblk)):
                    for m in range(KD):
                        dve.tensor_tensor(by_head(to[:, m, :]), headmask(m), src[:, m, bass.ds(b, 1), :].broadcast_to([P, H, NS]), ALU.mult).then_inc(kblk_ready, 1)
                at(dve, rb_ready, b + 1)
                for q in range(2):
                    at(dve, sc_psum, b * 2 + q + 1)
                    dve.tensor_tensor(sc[:, 2 * q:2 * q + 2, :], bank[5 + q][:, :].rearrange("p (t s) -> p t s", t=2),
                                      rb[:, :].rearrange("p (o s) -> p o s", o=1).broadcast_to([P, 2, HS]), ALU.add).then_inc(sc_ready, 1)
                flat = lambda x: x.rearrange("p t (h s) -> p (t h) s", h=H)
                wide = lambda x: x.rearrange("p (t o) -> p t o", o=1).broadcast_to([P, TT * H, NS])
                at(dve, sc_ready, b * 2 + 2)
                dve.tensor_reduce(cm[:, :], flat(sc[:, :, :]), AX.X, ALU.max).then_inc(cm_ready, 1)
                at(dve, cm_ready, b + 1)
                at(dve, ce_ready, b)
                dve.tensor_tensor(flat(cd[:, :, :]), flat(sc[:, :, :]), wide(cm[:, :]), ALU.subtract).then_inc(cd_ready, 1)
                at(dve, ce_ready, b + 1)
                dve.tensor_reduce(cs[:, :], flat(ce[:, :, :]), AX.X, ALU.add).then_inc(cs_ready, 1)
                at(dve, cs_ready, b + 1)
                dve.reciprocal(cr[:, :], cs[:, :]).then_inc(cr_ready, 1)
                at(dve, cr_ready, b + 1)
                at(dve, cpT_psum, b * 2)
                dve.tensor_tensor(flat(cp[:, :, :]), flat(ce[:, :, :]), wide(cr[:, :]), ALU.mult).then_inc(cp_ready, 1)
                at(dve, hb_ready, b + 1)
                for q, bk in ((0, 2), (1, 7)):
                    at(dve, c_psum, b * 2 + q + 1)
                    hb = h[:, b, 2 * q:2 * q + 2, :].rearrange("p t d -> p (t d)")
                    dve.tensor_tensor(hb, bank[bk][:, :], hb, ALU.add).then_inc(h_ready, 1)

        @block.gpsimd
        def _(pool):
            with pool.Fori(0, B) as b:
                nm.pool_rstd(pool, b)
            pool.wait_ge(join, KD + 4)
            pool.tensor_tensor(ve[:, :], mv[:, 1:2], K["eps"][0:R, 0:1], ALU.add).then_inc(jpool, 1)
            pool.wait_ge(jpool, 1)
            pool.tensor_tensor(rstd[:, :], ve[:, :], K["mhalf"][0:R, 0:1], ALU.pow).then_inc(jpool, 1)
            pool.wait_ge(join, KD + 5)
            pool.tensor_tensor(og[:, :], on[:, :], rows[:, 2, :], ALU.mult).then_inc(jpool, 1)
            pool.wait_ge(jpool, 3)
            pool.tensor_tensor(ob[:, :], og[:, :], rows[:, 3, :], ALU.add).then_inc(jpool, 1)
            with pool.Fori(0, B) as b:
                nm.pool_rstd(pool, b + B)
                at(pool, nm.xn_ready, b + (B + 1))
                pool.tensor_tensor(h[:, b, :, :], h[:, b, :, :], c_bo[:, :].rearrange("p (o d) -> p o d", o=1).broadcast_to([P, TT, D]), ALU.add).then_inc(hb_ready, 1)


def conv_stage(nc, K, a):
    TAPS, H1 = 4, T + 3
    with ExitStack() as ctx:
        sem = lambda n: K["sem"]("s4_" + n)
        sb = lambda n, s, d=F32: ctx.enter_context(nc.sbuf_tensor("s4_" + n, s, d))
        h, ident, bank = K["h"], K["ident"], K["bank"]
        nm = Norm(ctx, nc, K, "s4n", (bank[0], bank[1]))
        w_in, w_cv, w_fc, w_cp, w_out = (sb("w_in", [P, KD, 2 * INNER]), sb("w_cv", [P, MI, TAPS, P]), sb("w_fc", [P, MI, D]),
                                         sb("w_cp", [P, KD, INNER]), sb("w_out", [P, MI, D]))
        par = sb("par", [P, 4 * MI + KD])
        hc, sg, r = sb("hc", [P, MI, H1]), sb("sg", [P, MI, T]), sb("r", [P, MI, T])
        st, mv, ve, rstd, spare = sb("st", [P, TT, 6]), sb("mv", [P, TT, 2]), sb("ve", [P, TT]), sb("rstd", [P, TT]), sb("spare", [P, 1])
        rn, rnT, f, r2 = sb("rn", [P, TT, INNER]), sb("rnT", [P, MI, T]), sb("f", [P, KD, T]), sb("r2", [P, MI, T])
        loaded, zeroed = sem("loaded"), sem("zeroed")
        p_psum, hc_ready, g_psum, sg_ready, cv_psum, r_ready = (sem(n) for n in ("p_psum", "hc_ready", "g_psum", "sg_ready", "cv_psum", "r_ready"))
        rT_psum, stats, var, veps, rstd_ready, rn_ready = (sem(n) for n in ("rT_psum", "stats", "var", "veps", "rstd_ready", "rn_ready"))
        rnT_psum, rnT_ready, f_psum, f_ready, cp_psum, r2_ready, o_psum, h_ready = (
            sem(n) for n in ("rnT_psum", "rnT_ready", "f_psum", "f_ready", "cp_psum", "r2_ready", "o_psum", "h_ready"))
        block = ctx.enter_context(nc.Block())

        @block.sync
        def _(sp):
            start(sp, *nm.sems, p_psum, hc_ready, g_psum, sg_ready, cv_psum, r_ready, rT_psum, stats, var, veps, rstd_ready, rn_ready,
                  rnT_psum, rnT_ready, f_psum, f_ready, cp_psum, r2_ready, o_psum, h_ready)
            for to, src in ((w_in[:, :, :], a["s4_in"]), (par[:, :], a["s4_par"]), (w_fc[:, :, :], a["s4_fc"]),
                            (w_cp[:, :, :], a["s4_cp"]), (w_out[:, :, :], a["s4_out"])):
                sp.dma_start(to, src).then_inc(loaded, 16)
            sp.wait_ge(zeroed, 1)
            for g in range(2):
                q = slice(64 * g, 64 * g + 64)
                sp.dma_start(w_cv[q, :, :, q], a["s4_cv"][q]).then_inc(loaded, 16)

        @block.tensor
        def _(pe):
            pe.wait_ge(loaded, 16 * 7)
            pe.wait_ge(zeroed, 2)
            with pe.Fori(0, B) as b:
                at(pe, f_ready, b * KD)
                nm.pe_turn(pe, b)
                at(pe, nm.xT_ready, b + 1)
                for m in range(MI):
                    at(pe, hc_ready, b * MI + m - 1)
                    at(pe, r2_ready, b * MI)
                    for k in range(KD):
                        mm = pe.matmul(bank[2 + m % 2][:, :], w_in[:, k, m * P:(m + 1) * P], nm.xT[:, k, :], start=(k == 0), stop=(k == KD - 1))
                    mm.then_inc(p_psum, 1)
                    at(pe, sg_ready, b * MI + m)
                    at(pe, rnT_ready, b * MI)
                    for k in range(KD):
                        mm = pe.matmul(bank[4][:, :], w_in[:, k, INNER + m * P:INNER + (m + 1) * P], nm.xT[:, k, :], start=(k == 0), stop=(k == KD - 1))
                    mm.then_inc(g_psum, 1)
                for m in range(MI):
                    at(pe, hc_ready, b * MI + m + 1)
                    at(pe, r_ready, b * MI + m - 1)
                    if m < 2:
                        at(pe, h_ready, b * 2)
                    for j in range(TAPS):
                        mm = pe.matmul(bank[5 + m % 2][:, :], w_cv[:, m, j, :], hc[:, m, j:j + T], start=(j == 0), stop=(j == TAPS - 1))
                    mm.then_inc(cv_psum, 1)
                at(pe, r_ready, b * MI + MI)
                for t in range(TT):
                    for c in range(MI):
                        mm = pe.transpose(bank[t][:, c * P:(c + 1) * P], r[:, c, t * P:(t + 1) * P], ident[:, :])
                    mm.then_inc(rT_psum, 1)
                at(pe, rn_ready, b * TT + TT)
                at(pe, sg_ready, b * MI + MI)
                for c in range(MI):
                    for t in range(TT):
                        mm = pe.transpose(bank[4 + c][:, t * P:(t + 1) * P], rn[:, t, c * P:(c + 1) * P], ident[:, :])
                    mm.then_inc(rnT_psum, 1)
                at(pe, rnT_ready, b * MI + MI)
                for m in range(KD):
                    for k in range(MI):
                        mm = pe.matmul(bank[m][:, :], w_fc[:, k, m * P:(m + 1) * P], rnT[:, k, :], start=(k == 0), stop=(k == MI - 1))
                    mm.then_inc(f_psum, 1)
                at(pe, f_ready, b * KD + KD)
                for m in range(MI):
                    at(pe, r2_ready, b * MI + m - 1)
                    for k in range(KD):
                        mm = pe.matmul(bank[2 + m % 2][:, :], w_cp[:, k, m * P:(m + 1) * P], f[:, k, :], start=(k == 0), stop=(k == KD - 1))
                    mm.then_inc(cp_psum, 1)
                at(pe, r2_ready, b * MI + MI)
                for g in range(2):
                    for t in range(2):
                        for k in range(MI):
                            mm = pe.matmul(bank[6 + g][:, t * D:(t + 1) * D], r2[:, k, (2 * g + t) * P:(2 * g + t + 1) * P], w_out[:, k, :], start=(k == 0), stop=(k == MI - 1))
                    mm.then_inc(o_psum, 1)

        @block.scalar
        def _(act):
            act.wait_ge(loaded, 16 * 7)
            with act.Fori(0, B) as b:
                nm.act_copy(act, b)
                for m in range(MI):
                    at(act, p_psum, b * MI + m + 1)
                    at(act, cv_psum, b * MI)
                    act.activation(hc[:, m, TAPS - 1:H1], bank[2 + m % 2][:, :], ACT.Copy).then_inc(hc_ready, 1)
                    at(act, g_psum, b * MI + m + 1)
                    at(act, r_ready, b * MI)
                    act.activation(sg[:, m, :], bank[4][:, :], ACT.Silu).then_inc(sg_ready, 1)
                for c in range(MI):
                    at(act, rnT_psum, b * MI + c + 1)
                    at(act, f_psum, b * KD)
                    act.activation(rnT[:, c, :], bank[4 + c][:, :], ACT.Identity, bias=par[:, 8 + c:9 + c], scale=par[:, 4 + c:5 + c]).then_inc(rnT_ready, 1)
                for m in range(KD):
                    at(act, f_psum, b * KD + m + 1)
                    at(act, cp_psum, b * MI)
                    act.activation(f[:, m, :], bank[m][:, :], ACT.Silu, bias=par[:, 16 + m:17 + m]).then_inc(f_ready, 1)

        @block.vector
        def _(dve):
            dve.memset(w_cv[:, :, :, :], 0.0).then_inc(zeroed, 1)
            dve.memset(hc[:, :, 0:TAPS - 1], 0.0).then_inc(zeroed, 1)
            dve.wait_ge(loaded, 16 * 7)
            with dve.Fori(0, B) as b:
                nm.dve_stats(dve, b)
                nm.dve_apply(dve, b)
                for m in range(MI):
                    at(dve, cv_psum, b * MI + m + 1)
                    at(dve, sg_ready, b * MI + m + 1)
                    dve.scalar_tensor_tensor(r[:, m, :], bank[5 + m % 2][:, :], par[:, m:m + 1], sg[:, m, :], ALU.add, ALU.mult).then_inc(r_ready, 1)
                for t in range(TT):
                    at(dve, rT_psum, b * TT + t + 1)
                    i = dve.bn_stats(st[:, t, :], bank[t][:, :])
                i.then_inc(stats, 1)
                at(dve, stats, b + 1)
                at(dve, veps, b)
                dve.memset(spare[:, :], 0.0)
                for t in range(TT):
                    i = dve.bn_aggr(mv[:, t, :], st[:, t, :])
                i.then_inc(var, 1)
                at(dve, rstd_ready, b + 1)
                at(dve, rnT_psum, b * MI)
                for t in range(TT):
                    dve.tensor_scalar(rn[:, t, :], bank[t][:, :], mv[:, t, 0:1], rstd[:, t:t + 1], ALU.subtract, ALU.mult).then_inc(rn_ready, 1)
                at(dve, o_psum, b * 2)
                for m in range(MI):
                    at(dve, cp_psum, b * MI + m + 1)
                    dve.scalar_tensor_tensor(r2[:, m, :], bank[2 + m % 2][:, :], par[:, 12 + m:13 + m], r[:, m, :], ALU.add, ALU.add).then_inc(r2_ready, 1)
                for g in range(2):
                    at(dve, o_psum, b * 2 + g + 1)
                    hb = h[:, b, 2 * g:2 * g + 2, :].rearrange("p t d -> p (t d)")
                    dve.tensor_tensor(hb, bank[6 + g][:, :], hb, ALU.add).then_inc(h_ready, 1)

        @block.gpsimd
        def _(pool):
            with pool.Fori(0, B) as b:
                nm.pool_rstd(pool, b)
                at(pool, var, b + 1)
                at(pool, rstd_ready, b)
                pool.tensor_tensor(ve[:, :], mv[:, :, 1], K["eps"][:, 0:TT], ALU.add).then_inc(veps, 1)
                at(pool, veps, b + 1)
                at(pool, rn_ready, b * TT)
                pool.tensor_tensor(rstd[:, :], ve[:, :], K["mhalf"][:, 0:TT], ALU.pow).then_inc(rstd_ready, 1)


def expert_stage(nc, K, a, out):
    E, F, TOK = 8, 704, B * T
    NTT = TOK // P
    NT = (2 * TOK + E * (P - 1)) // P
    U = 3
    STEPS = NT // U
    FC = [(i * P, min(P, F - i * P)) for i in range(-(-F // P))]
    assert NT == U * STEPS
    with ExitStack() as ctx:
        sem = lambda n: K["sem"]("s5_" + n)
        sb = lambda n, s, d=F32: ctx.enter_context(nc.sbuf_tensor("s5_" + n, s, d))
        h, ident, bank = K["h"], K["ident"], K["bank"]
        X = nc.dram_tensor("expert_inputs", (NT * P, D), F32, kind="Internal").ap()
        Y = nc.dram_tensor("expert_outputs", (NT * P, D), F32, kind="Internal").ap()
        with ExitStack() as first:
            fsb = lambda n, s, d=F32: first.enter_context(nc.sbuf_tensor("s5_" + n, s, d))
            w13, w2 = sb("w13", [P, E, KD, 2 * F]), sb("w2", [P, E, len(FC), D])
            wts, slots, texp = sb("wts", [P, 2, NTT]), sb("slots", [P, 2, NTT], I32), sb("texp", [1, NT], I32)
            w_loaded = sem("w_loaded")
            nm = Norm(first, nc, K, "s5n", (bank[0], bank[1]))
            zeros = fsb("zeros", [P, D])
            wg, xall = fsb("wg", [P, KD, E]), fsb("xall", [P, B, TT, D])
            tri, iota_e, iota_t = fsb("tri", [P, P]), fsb("iota_e", [P, E]), fsb("iota_t", [1, NT])
            lg, mx, ex, sm, rs, scr = (fsb("lg", [P, NTT, E]), fsb("mx", [P, NTT]), fsb("ex", [P, NTT, E]), fsb("sm", [P, NTT]), fsb("rs", [P, NTT]), fsb("scr", [P, NTT, E]))
            m8, i8, best = fsb("m8", [P, NTT, 8]), fsb("i8", [P, NTT, 8], U32), fsb("best", [P, 2, NTT])
            den, rden = fsb("den", [P, NTT]), fsb("rden", [P, NTT])
            hot, both = fsb("hot", [P, 2, NTT, E]), fsb("both", [P, NTT, E])
            place, base, cnt, cnti, tiles, ends = (fsb("place", [P, NTT, E]), fsb("base", [P, NTT + 1, E]), fsb("cnt", [P, E]), fsb("cnti", [P, E], I32),
                                                   fsb("tiles", [P, E]), fsb("ends", [P, E + 1]))
            pick, slotf, tef = fsb("pick", [P, NTT, E]), fsb("slotf", [P, 2, NTT]), fsb("tef", [1, NT])
            loaded, zero_set, cleared = sem("loaded"), sem("zero_set"), sem("cleared")
            xall_ready, l_psum, l_ready, step, exped, rank_psum = sem("xall_ready"), sem("l_psum"), sem("l_ready"), sem("step"), sem("exped"), sem("rank_psum")
            scattered = sem("scattered")
            with nc.Block() as block:
                @block.sync
                def _(sp):
                    start(sp, *nm.sems, xall_ready, l_psum, l_ready)
                    for to, src in ((wg[:, :, :], a["s5_wg"]), (tri[:, :], a["s5_tri"]), (iota_e[:, :], a["s5_iota_e"]), (iota_t[:, :], a["s5_iota_t"])):
                        sp.dma_start(to, src).then_inc(loaded, 16)
                    sp.wait_ge(zero_set, 1)
                    for i in range(NT):
                        sp.dma_start(X[i * P:(i + 1) * P, :], zeros[:, :]).then_inc(cleared, 16)
                    for e in range(E):
                        sp.dma_start(w13[:, e, :, :], a["s5_w13"][e]).then_inc(w_loaded, 16)
                        sp.dma_start(w2[:, e, 0:5, :], a["s5_w2"][e, 0:5 * P].rearrange("(c p) d -> p c d", p=P)).then_inc(w_loaded, 16)
                        sp.dma_start(w2[0:F - 5 * P, e, 5, :], a["s5_w2"][e, 5 * P:F]).then_inc(w_loaded, 16)

                @block.tensor
                def _(pe):
                    pe.wait_ge(loaded, 64)
                    with pe.Fori(0, B) as b:
                        nm.pe_turn(pe, b)
                        at(pe, nm.xT_ready, b + 1)
                        at(pe, l_ready, b)
                        for t in range(TT):
                            for k in range(KD):
                                mm = pe.matmul(bank[2][:, t * E:(t + 1) * E], nm.xT[:, k, t * P:(t + 1) * P], wg[:, k, :], start=(k == 0), stop=(k == KD - 1))
                        mm.then_inc(l_psum, 1)
                    pe.wait_ge(step, 11)
                    pe.matmul(bank[3][:, 0:NTT * E], tri[:, :], both[:, :, :], start=True, stop=True)
                    pe.matmul(bank[4][:, 0:NTT * E], K["ones"][:, :], both[:, :, :], start=True, stop=True).then_inc(rank_psum, 1)

                @block.scalar
                def _(act):
                    with act.Fori(0, B) as b:
                        nm.act_copy(act, b)
                    act.wait_ge(step, 2)
                    act.activation(ex[:, :, :], ex[:, :, :], ACT.Exp).then_inc(exped, 1)

                @block.vector
                def _(dve):
                    dve.memset(zeros[:, :], 0.0).then_inc(zero_set, 1)
                    dve.wait_ge(loaded, 64)
                    with dve.Fori(0, B) as b:
                        nm.dve_stats(dve, b)
                        at(dve, xall_ready, b)
                        nm.dve_apply(dve, b)
                        at(dve, l_psum, b + 1)
                        dve.tensor_copy(lg[:, bass.ds(b * TT, TT), :].rearrange("p t e -> p (t e)"), bank[2][:, 0:TT * E]).then_inc(l_ready, 1)
                    dve.wait_ge(l_ready, B + START)
                    done = 0

                    def then(i):
                        nonlocal done
                        i.then_inc(step, 1)
                        done += 1
                        dve.wait_ge(step, done)

                    per_tile = lambda x: x.rearrange("p (t o) -> p t o", o=1).broadcast_to([P, NTT, E])
                    per_exp = lambda x: x.rearrange("p (o e) -> p o e", o=1).broadcast_to([P, NTT, E])
                    then(dve.tensor_reduce(mx[:, :], lg[:, :, :], AX.X, ALU.max))
                    then(dve.tensor_tensor(ex[:, :, :], lg[:, :, :], per_tile(mx[:, :]), ALU.subtract))
                    dve.wait_ge(exped, 1)
                    then(dve.tensor_reduce(sm[:, :], ex[:, :, :], AX.X, ALU.add))
                    then(dve.reciprocal(rs[:, :], sm[:, :]))
                    then(dve.tensor_tensor(scr[:, :, :], ex[:, :, :], per_tile(rs[:, :]), ALU.mult))
                    for t in range(NTT):
                        i = dve.max(m8[:, t, :], scr[:, t, :])
                    then(i)
                    for t in range(NTT):
                        i = dve.max_index(i8[:, t, :], m8[:, t, :], scr[:, t, :])
                    then(i)
                    then(dve.tensor_copy(best[:, :, :], i8[:, :, 0:2].rearrange("p t k -> p k t")))
                    for k in range(2):
                        then(dve.tensor_tensor(hot[:, k, :, :], per_exp(iota_e[:, :]), per_tile(best[:, k, :]), ALU.is_equal))
                    then(dve.tensor_tensor(both[:, :, :], hot[:, 0, :, :], hot[:, 1, :, :], ALU.add))
                    then(dve.scalar_tensor_tensor(den[:, :], m8[:, :, 0], 1e-20, m8[:, :, 1], ALU.add, ALU.add))
                    then(dve.reciprocal(rden[:, :], den[:, :]))
                    for k in range(2):
                        then(dve.tensor_tensor(wts[:, k, :], m8[:, :, k], rden[:, :], ALU.mult))
                    dve.wait_ge(rank_psum, 1)
                    then(dve.memset(base[:, 0, :], 0.0))
                    for t in range(NTT):
                        then(dve.tensor_tensor(base[:, t + 1, :], bank[4][:, t * E:(t + 1) * E], base[:, t, :], ALU.add))
                    then(dve.tensor_scalar(cnt[:, :], base[:, NTT, :], float(P - 1), None, ALU.add))
                    then(dve.tensor_copy(cnti[:, :], cnt[:, :]))
                    then(dve.tensor_scalar(cnti[:, :], cnti[:, :], 7, None, ALU.arith_shift_right))
                    then(dve.tensor_copy(tiles[:, :], cnti[:, :]))
                    then(dve.memset(ends[:, 0:1], 0.0))
                    for e in range(E):
                        then(dve.tensor_tensor(ends[:, e + 1:e + 2], ends[:, e:e + 1], tiles[:, e:e + 1], ALU.add))
                    then(dve.tensor_tensor(place[:, :, :].rearrange("p t e -> p (t e)"), bank[3][:, 0:NTT * E], base[:, 0:NTT, :].rearrange("p t e -> p (t e)"), ALU.add))
                    then(dve.tensor_scalar(cnt[:, :], ends[:, 0:E], float(P), None, ALU.mult))
                    then(dve.tensor_tensor(place[:, :, :], place[:, :, :], per_exp(cnt[:, :]), ALU.add))
                    for k in range(2):
                        then(dve.tensor_tensor(pick[:, :, :], place[:, :, :], hot[:, k, :, :], ALU.mult))
                        then(dve.tensor_reduce(slotf[:, k, :], pick[:, :, :], AX.X, ALU.add))
                    then(dve.tensor_copy(slots[:, :, :], slotf[:, :, :]))
                    then(dve.tensor_scalar(tef[:, :], iota_t[:, :], ends[0:1, 1:2], None, ALU.is_ge))
                    for e in range(2, E):
                        then(dve.scalar_tensor_tensor(tef[:, :], iota_t[:, :], ends[0:1, e:e + 1], tef[:, :], ALU.is_ge, ALU.add))
                    then(dve.tensor_copy(texp[:, :], tef[:, :]))
                    K["routed"] = done

                @block.gpsimd
                def _(pool):
                    with pool.Fori(0, B) as b:
                        nm.pool_rstd(pool, b)
                        at(pool, nm.xn_ready, b + 1)
                        pool.tensor_copy(xall[:, b, :, :], nm.xn[:, :, :])
                        pool.drain().then_inc(xall_ready, 1)
                    pool.wait_ge(step, K["routed"])
                    pool.wait_ge(xall_ready, B + START)
                    pool.wait_ge(cleared, 16 * NT)
                    for k in range(2):
                        for t in range(NTT):
                            pool.indirect_dma_start(
                                out=X[:, :], out_offset=bass.IndirectOffsetOnAxis(ap=slots[:, k, t:t + 1].bitcast(U32), axis=0),
                                in_=xall[:, t // TT, t % TT, :], in_offset=None).then_inc(scattered, 16)
                    pool.wait_ge(scattered, 16 * 2 * NTT)

        xt, xT = sb("xt", [P, U, D]), sb("xT", [P, U, KD, P])
        s1, hh, hT, yt = sb("s1", [P, 2, F]), sb("hh", [P, U, F]), sb("hT", [P, 2, len(FC), P]), sb("yt", [P, U, D])
        x_loaded, x_psum, x_ready = [sem(f"x_loaded{u}") for u in range(U)], sem("x_psum"), sem("x_ready")
        h_psum, s1_ready, hh_ready, hT_psum, hT_ready, y_psum, y_ready = (sem(n) for n in ("h_psum", "s1_ready", "hh_ready", "hT_psum", "hT_ready", "y_psum", "y_ready"))
        y_stored = [sem(f"y_stored{u}") for u in range(U)]
        with nc.Block() as block:
            n_of = lambda i, u: i * U + u

            @block.sync
            def _(sp):
                start(sp, x_psum, x_ready, h_psum, s1_ready, hh_ready, hT_psum, hT_ready, y_psum, y_ready)
                for u in range(U):
                    sp.dma_start(xt[:, u, :], X[u * P:(u + 1) * P, :]).then_inc(x_loaded[u], 16)

                def store(i, u):
                    at(sp, y_ready, i * U + u + 1)
                    sp.dma_start(Y[bass.ds(i * (U * P) + u * P, P), :], yt[:, u, :]).then_inc(y_stored[u], 16)

                with sp.Fori(0, STEPS - 1) as i:
                    for u in range(U):
                        at(sp, x_psum, i * U + u + 1)
                        sp.dma_start(xt[:, u, :], X[bass.ds(i * (U * P) + (U + u) * P, P), :]).then_inc(x_loaded[u], 16)
                        store(i, u)
                for u in range(U):
                    store(STEPS - 1, u)
                for u in range(U):
                    sp.wait_ge(y_stored[u], 16 * STEPS)

            @block.tensor
            def _(pe):
                def turn(i, u):
                    pe.wait_ge(x_loaded[u % U], (i + u // U) * 16 + 16)
                    at(pe, x_ready, i * U + u)
                    for k in range(KD):
                        mm = pe.transpose(bank[3][:, k * P:(k + 1) * P], xt[:, u % U, k * P:(k + 1) * P], ident[:, :])
                    mm.then_inc(x_psum, 1)

                def up(i, u):
                    e = pe.value_load(texp[0:1, bass.ds(i * U + u, 1)], min_val=0, max_val=E - 1)
                    at(pe, x_ready, i * U + u + 1)
                    at(pe, hh_ready, i * U + u)
                    for bk, c0, c1 in ((0, 0, 512), (1, 512, 1024), (2, 1024, 2 * F)):
                        for k in range(KD):
                            mm = pe.matmul(bank[bk][:, 0:c1 - c0], xT[:, u % U, k, :], w13[:, bass.ds(e, 1), k, c0:c1].rearrange("p o c -> p (o c)"), start=(k == 0), stop=(k == KD - 1))
                        mm.then_inc(h_psum, 1)

                def down(i, u):
                    e = pe.value_load(texp[0:1, bass.ds(i * U + u, 1)], min_val=0, max_val=E - 1)
                    at(pe, hh_ready, i * U + u + 1)
                    at(pe, hT_ready, i * U + u)
                    for c, (c0, w) in enumerate(FC):
                        mm = pe.transpose(bank[4 + c // 4][0:w, (c % 4) * P:(c % 4 + 1) * P], hh[:, u % U, c0:c0 + w], ident[:, :])
                    mm.then_inc(hT_psum, 1)
                    at(pe, hT_ready, i * U + u + 1)
                    at(pe, y_ready, i * U + u)
                    for c, (c0, w) in enumerate(FC):
                        mm = pe.matmul(bank[6][:, 0:D], hT[0:w, 0, c, :], w2[0:w, bass.ds(e, 1), c, :].rearrange("p o c -> p (o c)"), start=(c == 0), stop=(c == len(FC) - 1))
                    mm.then_inc(y_psum, 1)

                pe.wait_ge(w_loaded, 48 * E)
                turn(0, 0)
                turn(0, 1)
                up(0, 0)
                with pe.Fori(0, STEPS - 1) as i:
                    for u in range(U):
                        up(i, u + 1)
                        turn(i, u + 2)
                        down(i, u)
                up(STEPS - 1, 1)
                turn(STEPS - 1, 2)
                down(STEPS - 1, 0)
                up(STEPS - 1, 2)
                down(STEPS - 1, 1)
                down(STEPS - 1, 2)

            @block.scalar
            def _(act):
                def copy_x(i, u):
                    at(act, x_psum, i * U + u + 1)
                    act.activation(xT[:, u % U, :, :], bank[3][:, 0:D], ACT.Copy).then_inc(x_ready, 1)

                def silu(i, u):
                    at(act, h_psum, i * (3 * U) + 3 * u + 2)
                    at(act, hh_ready, i * U + u - 1)
                    act.activation(s1[:, 0, 0:512], bank[0][:, :], ACT.Silu)
                    act.activation(s1[:, 0, 512:F], bank[1][:, 0:F - 512], ACT.Silu).then_inc(s1_ready, 1)

                def copy_h(i, u):
                    at(act, hT_psum, i * U + u + 1)
                    at(act, y_psum, i * U + u)
                    act.activation(hT[:, 0, 0:4, :], bank[4][:, :], ACT.Copy)
                    act.activation(hT[:, 0, 4, :], bank[5][:, 0:P], ACT.Copy)
                    act.activation(hT[0:F - 5 * P, 0, 5, :], bank[5][0:F - 5 * P, P:2 * P], ACT.Copy).then_inc(hT_ready, 1)

                copy_x(0, 0)
                copy_x(0, 1)
                silu(0, 0)
                with act.Fori(0, STEPS - 1) as i:
                    for u in range(U):
                        silu(i, u + 1)
                        copy_x(i, u + 2)
                        copy_h(i, u)
                silu(STEPS - 1, 1)
                copy_x(STEPS - 1, 2)
                copy_h(STEPS - 1, 0)
                silu(STEPS - 1, 2)
                copy_h(STEPS - 1, 1)
                copy_h(STEPS - 1, 2)

            @block.vector
            def _(dve):
                def gate(i, u):
                    at(dve, s1_ready, i * U + u + 1)
                    at(dve, h_psum, i * (3 * U) + 3 * u + 3)
                    at(dve, hT_psum, i * U + u - (U - 1))
                    q = 1024 - F
                    dve.tensor_tensor(hh[:, u % U, 0:q], s1[:, 0, 0:q], bank[1][:, F - 512:512], ALU.mult)
                    dve.tensor_tensor(hh[:, u % U, q:F], s1[:, 0, q:F], bank[2][:, 0:F - q], ALU.mult).then_inc(hh_ready, 1)

                def copy_y(i, u, first):
                    at(dve, y_psum, i * U + u + 1)
                    if not first:
                        dve.wait_ge(y_stored[u], i * 16)
                    dve.tensor_copy(yt[:, u, :], bank[6][:, 0:D]).then_inc(y_ready, 1)

                gate(0, 0)
                for u in range(U):
                    gate(0, u + 1)
                    copy_y(0, u, True)
                with dve.Fori(1, STEPS - 1) as i:
                    for u in range(U):
                        gate(i, u + 1)
                        copy_y(i, u, False)
                gate(STEPS - 1, 1)
                copy_y(STEPS - 1, 0, False)
                gate(STEPS - 1, 2)
                copy_y(STEPS - 1, 1, False)
                copy_y(STEPS - 1, 2, False)

        G = 4
        yg = sb("yg", [P, G, 2, D])
        gathered, added, out_written = [sem(f"gathered{g}") for g in range(G)], sem("added"), sem("out_written")
        with nc.Block() as block:
            @block.gpsimd
            def _(pool):
                for t in range(NTT):
                    if t >= G:
                        pool.wait_ge(added, 2 * (t - G + 1))
                    for k in range(2):
                        pool.indirect_dma_start(out=yg[:, t % G, k, :], out_offset=None, in_=Y[:, :],
                                                in_offset=bass.IndirectOffsetOnAxis(ap=slots[:, k, t:t + 1].bitcast(U32), axis=0)).then_inc(gathered[t % G], 16)

            @block.vector
            def _(dve):
                for t in range(NTT):
                    dve.wait_ge(gathered[t % G], 32 * (t // G + 1))
                    for k in range(2):
                        ht = h[:, t // TT, t % TT, :]
                        dve.scalar_tensor_tensor(ht, yg[:, t % G, k, :], wts[:, k, t:t + 1], ht, ALU.mult, ALU.add).then_inc(added, 1)
                        dve.wait_ge(added, 2 * t + k + 1)

            @block.sync
            def _(sp):
                for b in range(B):
                    sp.wait_ge(added, 2 * TT * (b + 1))
                    sp.dma_start(out[b].rearrange("(t p) d -> p t d", p=P), h[:, b, :, :]).then_inc(out_written, 16)
                sp.wait_ge(out_written, 16 * B)


def write_out(nc, K, out):
    with nc.semaphore("out_written") as out_written, nc.Block() as block:
        @block.sync
        def _(sp):
            sp.dma_start(out.rearrange("b (t p) d -> p b t d", p=P), K["h"][:, :, :, :]).then_inc(out_written, 16)
            sp.wait_ge(out_written, 16)


def program(nc, a, out):
    with ExitStack() as ctx:
        sb = lambda n, s, d=F32: ctx.enter_context(nc.sbuf_tensor(n, s, d))
        K = {"h": sb("h", [P, B, TT, D]), "ident": sb("ident", [P, P]), "ones": sb("ones", [P, P]), "mhalf": sb("mhalf", [P, 16]), "eps": sb("eps", [P, 16]),
             "bank": [ctx.enter_context(nc.psum_tensor(f"bank{i}", [P, 512], F32)) for i in range(8)]}
        made = []

        def new_semaphore(name):
            made.append(nc.alloc_semaphore(name))
            return made[-1]

        K["sem"] = new_semaphore
        for stage in (embed_stage, token_stage, scan_stage, slot_stage, conv_stage):
            stage(nc, K, a)
            nc.clear_and_free_semaphores(made)
            nc.all_engine_barrier()
            made.clear()
        expert_stage(nc, K, a, out)


def kernel(**inputs):
    import concourse.bacc as _bacc
    from concourse.bass_utils import run_bass_kernel_spmd as _run
    i = {k: np.asarray(v) for k, v in inputs.items()}
    L = 4

    def kT(w, k):
        w = np.swapaxes(w, -1, -2)
        return np.moveaxis(w.reshape(*w.shape[:-2], k, w.shape[-2] // k, w.shape[-1]), -2, -3)

    def col(v):
        return np.swapaxes(v.reshape(*v.shape[:-1], v.shape[-1] // P, P), -1, -2)

    cw = i["L0_tok_conv_w"][:, :, 0, :].reshape(L, MI, P, 4).transpose(0, 2, 1, 3).reshape(L, P, 16)
    lay = {
        "x": i["x"].reshape(B * TT, P).T,
        "tok_emb": i["L0_tok_tok_emb"], "pos_emb": i["L0_tok_pos_emb"],
        "W_inT": kT(i["L0_tok_W_in"], KD),
        "W_BT": kT(i["L0_tok_W_B"], MI),
        "W_CT": np.swapaxes(i["L0_tok_W_C"], 1, 2),
        "W_outT": kT(i["L0_tok_W_out"], MI),
        "tok_par": np.concatenate([cw, col(i["L0_tok_conv_b"]), col(i["L0_tok_D_vec"])], axis=-1),
        "tok_ln_g": i["L0_tok_ln_g"].reshape(L, 1, D), "tok_ln_b": i["L0_tok_ln_b"].reshape(L, 1, D),
    }
    cw = i["L0_attn_conv_w"][:, 0, :].reshape(MI, P, 4).transpose(1, 0, 2).reshape(P, 16)
    rows = lambda w, k: w.reshape(k, w.shape[0] // k, w.shape[1]).transpose(1, 0, 2)
    lay.update({
        "s2_in": rows(i["L0_attn_in_proj_w"], KD), "s2_x": rows(i["L0_attn_x_proj_w"], MI), "s2_out": rows(i["L0_attn_out_proj_w"], MI),
        "s2_par": np.concatenate([cw] + [col(i["L0_attn_" + k]) for k in ("conv_b", "dt_w", "dt_b", "D")], axis=-1),
        "s2_alog": rows(i["L0_attn_A_log"], MI),
    })
    g = lambda k: i["L0_ffn_" + k]
    lay.update({"s3_" + n: rows(g(n[0] + "_" + n[1:3]), KD) for n in ("dWq", "dWv", "dWo", "cWk", "cWv", "cWo")})
    lay.update({
        "s3_dWkT": rows(g("d_Wk").T, KD), "s3_cWqT": rows(g("c_Wq").T, KD),
        "s3_cols": np.stack([g(k).reshape(KD, P).T for k in ("d_bq", "d_bk", "d_bv", "c_bq", "c_bk", "c_bv", "c_bo")], axis=-1),
        "s3_bias": np.concatenate([g("e_b1"), g("e_bg")], axis=1),
        "s3_b2": g("e_b2").reshape(16, KD, P).transpose(2, 1, 0),
        "s3_slotT": rows(g("slot_query")[0].T, KD),
        "s3_rows": np.stack([np.tile(g("slot_query")[0], (B, 1)), np.tile(g("d_bo"), (B * 16, 1)), np.tile(g("e_ln_g"), (B, 1)), np.tile(g("e_ln_b"), (B, 1))], axis=1),
        "s3_cbo": g("c_bo").reshape(1, D),
        "s3_mask": (np.arange(D)[:, None] // 16 == np.arange(16)[None, :]).astype(np.float32).reshape(KD, P, 16).transpose(1, 0, 2),
        "s3_W1": g("e_W1").reshape(16, KD, P, 1024).transpose(0, 2, 1, 3), "s3_Wg": g("e_Wg").reshape(16, KD, P, 1024).transpose(0, 2, 1, 3),
        "s3_W2": g("e_W2").reshape(16, 8, P, D).transpose(0, 2, 1, 3),
    })
    g = lambda k: i["L1_attn_" + k]
    lay.update({
        "s4_in": rows(g("in_proj_w").T, KD), "s4_fc": rows(g("fc_w").T, MI), "s4_cp": rows(g("cproj_w").T, KD), "s4_out": rows(g("out_w").T, MI),
        "s4_cv": g("conv_w").reshape(MI, 2, 64, 64, 4).transpose(1, 3, 0, 4, 2).reshape(P, MI, 4, 64),
        "s4_par": np.concatenate([col(g(k)) for k in ("conv_b", "ln_g", "ln_b", "cproj_b", "fc_b")], axis=-1),
    })
    g = lambda k: i["L1_ffn_" + k]
    w13 = np.concatenate([g("W1"), g("W3")], axis=1).transpose(0, 2, 1)
    lay.update({
        "s5_wg": rows(g("Wg").T, KD), "s5_w13": w13.reshape(8, KD, P, -1).transpose(0, 2, 1, 3), "s5_w2": g("W2").transpose(0, 2, 1),
        "s5_tri": np.triu(np.ones((P, P), np.float32), 1), "s5_iota_e": np.tile(np.arange(8, dtype=np.float32), (P, 1)),
        "s5_iota_t": np.arange(39, dtype=np.float32)[None],
    })
    nc = _bacc.Bacc("TRN2", target_bir_lowering=False, num_devices=1)
    arrays, args = {}, {}
    for name, v in lay.items():
        v = np.ascontiguousarray(v)
        arrays[f"in_{name}"] = v
        args[name] = nc.dram_tensor(f"in_{name}", v.shape, mybir.dt.from_np(v.dtype), kind="ExternalInput").ap()
    out = nc.dram_tensor("out_h", (B, T, D), F32, kind="ExternalOutput").ap()
    program(nc, args, out)
    r = _run(nc, [arrays], core_ids=[0])
    return r.results[0]["out_h"]
```

```python
from contextlib import ExitStack

import numpy as np
import concourse.bass as bass
from concourse import mybir

ALU = mybir.AluOpType
ACT = mybir.ActivationFunctionType
F32 = mybir.dt.float32
I32 = mybir.dt.int32
U32 = mybir.dt.uint32
F32R = mybir.dt.float32r
AX = mybir.AxisListType

P = 128
D = 256
KD = D // P
B = 4
T = 512
TT = T // P
INNER = 512
MI = INNER // P
EPS = 1e-5
START = 8


def at(eng, sem, done):
    eng.wait_ge(sem, done + START)


def split_product(pe, out, w, x, start, stop):
    terms = ((w[0], x[1]), (w[1], x[0]), (w[0], x[0]))
    for i, (a, b) in enumerate(terms):
        mm = pe.matmul(out, a, b, start=(start and i == 0), stop=(stop and i == len(terms) - 1))
    return mm


def embed_stage(nc, K, a):
    with ExitStack() as ctx:
        sem = lambda n: K["sem"](n)
        idx = ctx.enter_context(nc.sbuf_tensor("token_ids", [P, B * TT], I32))
        pos = ctx.enter_context(nc.sbuf_tensor("positions", [P, TT, D], F32))
        ids_loaded, pos_loaded, rows_gathered, filled = sem("ids_loaded"), sem("pos_loaded"), sem("rows_gathered"), sem("consts_filled")
        embedded = sem("embedded")
        block = ctx.enter_context(nc.Block())
        h, ident = K["h"], K["ident"]

        @block.sync
        def _(sp):
            sp.dma_start(idx[:, :], a["x"]).then_inc(ids_loaded, 16)
            sp.dma_start(pos[:, :, :], a["pos_emb"][0:T, :].rearrange("(t p) d -> p t d", p=P)).then_inc(pos_loaded, 16)

        @block.gpsimd
        def _(pool):
            pool.memset(ident[:, :], 0.0).then_inc(filled, 1)
            pool.memset(K["ones"][:, :], 1.0).then_inc(filled, 1)
            pool.memset(K["mhalf"][:, :], -0.5).then_inc(filled, 1)
            pool.memset(K["eps"][:, :], EPS).then_inc(filled, 1)
            pool.wait_ge(filled, 1)
            pool.affine_select(out=ident[:, :], in_=ident[:, :], compare_op=ALU.not_equal, fill=1.0,
                               base=0, pattern=[[-1, P]], channel_multiplier=1).then_inc(filled, 1)
            pool.wait_ge(ids_loaded, 16)
            for n in range(B * TT):
                pool.indirect_dma_start(
                    out=h[:, n // TT, n % TT, :], out_offset=None, in_=a["tok_emb"][:, :],
                    in_offset=bass.IndirectOffsetOnAxis(ap=idx[:, n:n + 1].bitcast(U32), axis=0),
                ).then_inc(rows_gathered, 16)

        @block.vector
        def _(dve):
            dve.memset(h[:, B, :, :], 0.0).then_inc(embedded, 1)
            dve.wait_ge(pos_loaded, 16)
            for b in range(B):
                if b == 0:
                    dve.wait_ge(rows_gathered, 16 * B * TT)
                dve.tensor_tensor(h[:, b, :, :], h[:, b, :, :], pos[:, :, :], ALU.add).then_inc(embedded, 1)


def token_stage(nc, K, a):
    L, N, DECAY, INP = 4, 64, 0.95, 0.05
    with ExitStack() as ctx:
        sem = lambda n: K["sem"](n)
        sb = lambda n, s, d=F32: ctx.enter_context(nc.sbuf_tensor(n, s, d))
        h, ident, bank = K["h"], K["ident"], K["bank"]
        w_in, w_in_high, w_in_low = sb("w_in", [P, KD, 2 * INNER]), sb("w_in_high", [P, KD, 2 * INNER], F32R), sb("w_in_low", [P, KD, 2 * INNER], F32R)
        w_b = sb("w_b", [P, MI, N])
        w_c, w_c5, w_c_high, w_c_low = sb("w_c", [N, INNER]), sb("w_c5", [N, INNER]), sb("w_c_high", [N, INNER], F32R), sb("w_c_low", [N, INNER], F32R)
        w_out = sb("w_out", [P, MI, D])
        par, taps, d_vec = sb("par", [P, L, 6 * MI]), sb("taps", [P, 5 * MI]), sb("d_vec", [P, MI])
        ln_g, ln_b = sb("ln_g", [P, D]), sb("ln_b", [P, D])
        decay = sb("decay", [N, T])
        xT, u, sg, hs, yg = sb("xT", [P, 2, 2, KD, T], F32R), sb("u", [P, 2, MI, T]), sb("sg", [P, 2, MI, T]), sb("hs", [N, T]), sb("yg", [P, 2, MI, T])
        hs_parts = sb("hs_parts", [N, 2, 2, T], F32R)
        z, st, mv, ve, rstd = sb("z", [P, 2, TT, D]), sb("st", [P, 2, TT, 6]), sb("mv", [P, 2, TT, 2]), sb("ve", [P, 2, TT]), sb("rstd", [P, 2, TT])
        xg = sb("xg", [P, TT, D])
        acc, yt = sb("acc", [P, 2, T]), sb("yt", [P, 2, T])
        spare = sb("spare", [P, 1])

        w_in_loaded, w_b_loaded, w_c_loaded, w_out_loaded, ln_loaded, par_loaded = (
            sem(n) for n in ("w_in_loaded", "w_b_loaded", "w_c_loaded", "w_out_loaded", "ln_loaded", "par_loaded"))
        w_in_split, taps_set, d_set, decay_set, w_c_scaled = (sem(n) for n in ("w_in_split", "taps_set", "d_set", "decay_set", "w_c_scaled"))
        w_c_split, hs_made, hs_high = sem("w_c_split"), sem("hs_made"), sem("hs_high")
        xT_psum, xT_high, xT_ready = sem("xT_psum"), sem("xT_high"), sem("xT_ready")
        p_psum, p_tap, p_conv1, p_conv2, p_conv, u_ready = sem("p_psum"), sem("p_tap"), sem("p_conv1"), sem("p_conv2"), sem("p_conv"), sem("u_ready")
        g_psum, g_ready = sem("g_psum"), sem("g_ready")
        bu_psum, hs_ready = sem("bu_psum"), sem("hs_ready")
        y_psum, yt_ready, yg_ready = sem("y_psum"), sem("yt_ready"), sem("yg_ready")
        o_psum, z_ready, stats, var, veps, rstd_ready, xg_ready, x_ready = (
            sem("o_psum"), sem("z_ready"), sem("stats"), sem("var"), sem("veps"), sem("rstd_ready"), sem("xg_ready"), sem("x_ready"))
        block = ctx.enter_context(nc.Block())
        PT = (0, 1)
        PP, PG, PB, PY = (2, 3), 4, 5, (6, 7)

        def pipeline(eng, step):
            for s in range(B):
                step(0, s, s, True, s >= 1, s >= 2, s >= 3)
            with eng.Fori(1, L) as l:
                for s in range(B):
                    step(l, s, l * B + s, True, True, True, True)
            step(L, 0, L * B, False, True, True, True)
            step(L, 1, L * B + 1, False, False, True, True)
            step(L, 2, L * B + 2, False, False, False, True)

        @block.sync
        def _(sp):
            start(sp, g_psum, p_psum, yt_ready, o_psum, x_ready, z_ready, u_ready, hs_ready, yg_ready, xT_ready, p_conv, g_ready,
                  w_c_scaled, xT_psum, y_psum, bu_psum, veps, stats, p_tap, p_conv1, p_conv2, rstd_ready, xg_ready, var,
                  w_c_split, hs_made, hs_high, w_in_split, xT_high, taps_set, d_set)
            sp.dma_start(w_in[:, :, :], a["W_inT"][0]).then_inc(w_in_loaded, 16)
            sp.dma_start(par[:, :, :], a["tok_par"].rearrange("l p c -> p l c")).then_inc(par_loaded, 16)
            sp.dma_start(w_b[:, :, :], a["W_BT"][0]).then_inc(w_b_loaded, 16)
            sp.dma_start(w_c[:, :], a["W_CT"][0]).then_inc(w_c_loaded, 16)
            sp.dma_start(w_out[:, :, :], a["W_outT"][0]).then_inc(w_out_loaded, 16)
            sp.dma_start(ln_g[:, :], a["tok_ln_g"][0].broadcast_to([P, D])).then_inc(ln_loaded, 16)
            sp.dma_start(ln_b[:, :], a["tok_ln_b"][0].broadcast_to([P, D])).then_inc(ln_loaded, 16)
            with sp.Fori(1, L) as l:
                at(sp, w_in_split, l * 2)
                sp.dma_start(w_in[:, :, :], a["W_inT"][l]).then_inc(w_in_loaded, 16)
                at(sp, w_c_scaled, l)
                sp.dma_start(w_c[:, :], a["W_CT"][l]).then_inc(w_c_loaded, 16)
                at(sp, bu_psum, l * B)
                sp.dma_start(w_b[:, :, :], a["W_BT"][l]).then_inc(w_b_loaded, 16)
                at(sp, o_psum, l * (2 * B))
                sp.dma_start(w_out[:, :, :], a["W_outT"][l]).then_inc(w_out_loaded, 16)
                at(sp, x_ready, l * B)
                sp.dma_start(ln_g[:, :], a["tok_ln_g"][l].broadcast_to([P, D])).then_inc(ln_loaded, 16)
                sp.dma_start(ln_b[:, :], a["tok_ln_b"][l].broadcast_to([P, D])).then_inc(ln_loaded, 16)

        w_parts = lambda k, c: (w_in_high[:, k, c:c + P], w_in_low[:, k, c:c + P])
        x_parts = lambda s, k: (xT[:, s % 2, 0, k, :], xT[:, s % 2, 1, k, :])

        @block.tensor
        def _(pe):
            def output_of_state(n, s, ms):
                for m in ms:
                    at(pe, yt_ready, n * MI + m - 1)
                    split_product(pe, bank[PY[m % 2]][:, :], (w_c_high[:, m * P:(m + 1) * P], w_c_low[:, m * P:(m + 1) * P]),
                                  (hs_parts[:, s % 2, 0, :], hs_parts[:, s % 2, 1, :]), True, True).then_inc(y_psum, 1)

            def step(l, s, n, new, mid, old, last):
                if new:
                    at(pe, x_ready, n + 1 - B)
                    at(pe, z_ready, 2 * n - 4)
                    for k in range(KD):
                        for t in range(TT):
                            mm = pe.transpose(bank[PT[k]][:, t * P:(t + 1) * P], h[:, s, t, k * P:(k + 1) * P], ident[:, :])
                    mm.then_inc(xT_psum, 1)
                if old:
                    output_of_state(n - 2, s, (2, 3))
                if mid:
                    at(pe, u_ready, MI * n)
                    at(pe, hs_ready, n - 1)
                    if s == 1:
                        pe.wait_ge(w_b_loaded, l * 16 + 16)
                    for k in range(MI):
                        mm = pe.matmul(bank[PB][0:N, :], w_b[:, k, :], u[:, (s + 1) % 2, k, :], start=(k == 0), stop=(k == MI - 1))
                    mm.then_inc(bu_psum, 1)
                if old:
                    at(pe, yg_ready, MI * (n - 1))
                    if new:
                        at(pe, xT_ready, n + 1)
                    else:
                        at(pe, z_ready, 2 * n - 4)
                    if s == 2:
                        pe.wait_ge(w_out_loaded, l * 16 + 16)
                    for j in range(2):
                        for t in range(2):
                            for k in range(MI):
                                mm = pe.matmul(bank[PT[j]][:, t * D:(t + 1) * D], yg[:, s % 2, k, (2 * j + t) * P:(2 * j + t + 1) * P], w_out[:, k, :],
                                               start=(k == 0), stop=(k == MI - 1))
                        mm.then_inc(o_psum, 1)
                if new:
                    at(pe, xT_ready, n + 1)
                    if s == 0:
                        at(pe, w_in_split, l * 2 + 2)
                    for m in range(MI):
                        at(pe, p_conv, n * MI + m - 1)
                        for k in range(KD):
                            mm = split_product(pe, bank[PP[m % 2]][:, :], w_parts(k, m * P), x_parts(s, k), k == 0, k == KD - 1)
                        mm.then_inc(p_psum, 1)
                        at(pe, g_ready, n * MI + m)
                        for k in range(KD):
                            mm = split_product(pe, bank[PG][:, :], w_parts(k, INNER + m * P), x_parts(s, k), k == 0, k == KD - 1)
                        mm.then_inc(g_psum, 1)
                if mid:
                    at(pe, hs_ready, n)
                    if s == 1:
                        at(pe, w_c_split, l * 2 + 2)
                    output_of_state(n - 1, s + 1, (0, 1))

            pipeline(pe, step)

        @block.scalar
        def _(act):
            def step(l, s, n, new, mid, old, last):
                def state_high():
                    at(act, hs_made, n)
                    at(act, y_psum, (n - 2) * MI)
                    act.activation(hs_parts[:, (s + 1) % 2, 0, :], hs[:, :], ACT.Copy).then_inc(hs_high, 1)

                if not new:
                    if mid:
                        state_high()
                    return
                at(act, xT_psum, n + 1)
                at(act, g_psum, n * MI - MI)
                for k in range(KD):
                    act.activation(xT[:, s % 2, 0, k, :], bank[PT[k]][:, :], ACT.Copy).then_inc(xT_high, 1)
                if s == 0:
                    act.wait_ge(w_in_loaded, l * 16 + 16)
                    at(act, g_psum, n * MI)
                    act.activation(w_in_high[:, :, :], w_in[:, :, :], ACT.Copy).then_inc(w_in_split, 1)
                if s == 1:
                    act.wait_ge(w_c_loaded, l * 16 + 16)
                    at(act, y_psum, n * MI - MI)
                    act.activation(w_c5[:, :], w_c[:, :], ACT.Copy, scale=INP).then_inc(w_c_scaled, 1)
                    at(act, w_c_scaled, l + 1)
                    act.activation(w_c_high[:, :], w_c5[:, :], ACT.Copy).then_inc(w_c_split, 1)

                def silu_u(m):
                    at(act, p_conv, n * MI + m + 1)
                    if m == 0:
                        at(act, yt_ready, n * MI - MI)
                    act.activation(u[:, s % 2, m, :], acc[:, m % 2, :], ACT.Silu).then_inc(u_ready, 1)

                if mid:
                    state_high()
                for m in range(MI):
                    at(act, p_psum, n * MI + m + 1)
                    at(act, u_ready, n * MI + m - 1)
                    if s == 0 and m == 0:
                        at(act, taps_set, l + 1)
                    act.activation(acc[:, m % 2, :], bank[PP[m % 2]][:, :], ACT.Identity,
                                   bias=taps[:, 16 + m:17 + m], scale=taps[:, 4 * m + 3:4 * m + 4]).then_inc(p_tap, 1)
                    at(act, g_psum, n * MI + m + 1)
                    if m == 0:
                        at(act, yg_ready, n * MI - MI)
                    act.activation(sg[:, s % 2, m, :], bank[PG][:, :], ACT.Silu).then_inc(g_ready, 1)
                    if m:
                        silu_u(m - 1)
                silu_u(MI - 1)

            pipeline(act, step)

        @block.vector
        def _(dve):
            dve.memset(decay[:, :], DECAY).then_inc(decay_set, 1)
            dve.wait_ge(decay_set, 1)
            dve.wait_ge(par_loaded, 16)

            def gate_input(n, s, ms):
                for m in ms:
                    at(dve, y_psum, n * MI + m + 1)
                    at(dve, yg_ready, n * MI + m - 1)
                    dve.scalar_tensor_tensor(yt[:, m % 2, :], u[:, s % 2, m, :], d_vec[:, m:m + 1], bank[PY[m % 2]][:, :], ALU.mult, ALU.add).then_inc(yt_ready, 1)

            def of_layer(l, cols):
                return par[:, l, cols] if isinstance(l, int) else par[:, bass.ds(l, 1), cols].rearrange("p l c -> p (l c)")

            def step(l, s, n, new, mid, old, last):
                if new:
                    if s == 0:
                        at(dve, p_conv, n * MI)
                        dve.tensor_copy(taps[:, :], of_layer(l, slice(0, 5 * MI))).then_inc(taps_set, 1)
                    for k in range(KD):
                        at(dve, xT_high, n * KD + k + 1)
                        i = dve.tensor_tensor(xT[:, s % 2, 1, k, :], bank[PT[k]][:, :], xT[:, s % 2, 0, k, :], ALU.subtract)
                    i.then_inc(xT_ready, 1)
                if old:
                    gate_input(n - 2, s, (2, 3))
                if new and s == 0:
                    at(dve, w_in_split, l * 2 + 1)
                    dve.tensor_tensor(w_in_low[:, :, :], w_in[:, :, :], w_in_high[:, :, :], ALU.subtract).then_inc(w_in_split, 1)
                if new and s == 1:
                    at(dve, yt_ready, n * MI - MI)
                    dve.tensor_copy(d_vec[:, :], of_layer(l, slice(5 * MI, 6 * MI))).then_inc(d_set, 1)
                if mid:
                    at(dve, bu_psum, n)
                    at(dve, hs_ready, n - 1)
                    dve.tensor_tensor_scan(hs[:, :], decay[:, :], bank[PB][0:N, :], 0.0, ALU.mult, ALU.add).then_inc(hs_made, 1)
                if last:
                    if s == 3:
                        dve.wait_ge(ln_loaded, l * 32 + 32)
                    at(dve, var, n - 2)
                    at(dve, x_ready, n - 3)
                    for t in range(TT):
                        i = dve.scalar_tensor_tensor(xg[:, t, :], z[:, (s + 1) % 2, t, :], mv[:, (s + 1) % 2, t, 0:1], ln_g[:, :], ALU.subtract, ALU.mult)
                    i.then_inc(xg_ready, 1)
                    at(dve, xg_ready, n - 2)
                    at(dve, rstd_ready, n - 2)
                    for t in range(TT):
                        i = dve.scalar_tensor_tensor(h[:, (s - 3) % B, t, :], xg[:, t, :], rstd[:, (s + 1) % 2, t:t + 1], ln_b[:, :], ALU.mult, ALU.add)
                    i.then_inc(x_ready, 1)
                if mid:
                    at(dve, hs_high, n)
                    at(dve, hs_made, n)
                    dve.tensor_tensor(hs_parts[:, (s + 1) % 2, 1, :], hs[:, :], hs_parts[:, (s + 1) % 2, 0, :], ALU.subtract).then_inc(hs_ready, 1)
                if new and s == 1:
                    at(dve, w_c_split, l * 2 + 1)
                    dve.tensor_tensor(w_c_low[:, :], w_c5[:, :], w_c_high[:, :], ALU.subtract).then_inc(w_c_split, 1)
                if old:
                    for j in range(2):
                        at(dve, o_psum, 2 * (n - 2) + j + 1)
                        if j == 0:
                            at(dve, x_ready, n - 3)
                        dve.tensor_tensor(z[:, s % 2, 2 * j:2 * j + 2, :].rearrange("p t d -> p (t d)"), bank[PT[j]][:, :],
                                          h[:, (s - 2) % B, 2 * j:2 * j + 2, :].rearrange("p t d -> p (t d)"), ALU.add).then_inc(z_ready, 1)
                    at(dve, z_ready, 2 * (n - 2) + 2)
                    for t in range(TT):
                        i = dve.bn_stats(st[:, s % 2, t, :], z[:, s % 2, t, :])
                    i.then_inc(stats, 1)
                    at(dve, stats, n - 1)
                    at(dve, veps, n - 3)
                    dve.memset(spare[:, :], 0.0)
                    for t in range(TT):
                        i = dve.bn_aggr(mv[:, s % 2, t, :], st[:, s % 2, t, :])
                    i.then_inc(var, 1)
                if new:
                    if s == 0:
                        at(dve, taps_set, l + 1)
                    for m in range(MI):
                        pb = bank[PP[m % 2]]
                        for j, before, done in ((1, p_tap, p_conv1), (2, p_conv1, p_conv2), (3, p_conv2, p_conv)):
                            at(dve, before, n * MI + m + 1)
                            dve.scalar_tensor_tensor(acc[:, m % 2, j:T], pb[:, 0:T - j], taps[:, 4 * m + 3 - j:4 * m + 4 - j],
                                                     acc[:, m % 2, j:T], ALU.mult, ALU.add).then_inc(done, 1)
                if mid:
                    if s == 1:
                        at(dve, d_set, l + 1)
                    at(dve, u_ready, n * MI)
                    gate_input(n - 1, s + 1, (0, 1))

            pipeline(dve, step)

        @block.gpsimd
        def _(pool):
            def gate(n, s, ms):
                for m in ms:
                    at(pool, yt_ready, n * MI + m + 1)
                    at(pool, g_ready, n * MI + m + 1)
                    pool.tensor_tensor(yg[:, s % 2, m, :], yt[:, m % 2, :], sg[:, s % 2, m, :], ALU.mult).then_inc(yg_ready, 1)

            def step(l, s, n, new, mid, old, last):
                if old:
                    gate(n - 2, s, (2, 3))
                    at(pool, var, n - 1)
                    at(pool, rstd_ready, n - 2)
                    pool.tensor_tensor(ve[:, s % 2, :], mv[:, s % 2, :, 1], K["eps"][:, 0:TT], ALU.add).then_inc(veps, 1)
                    at(pool, veps, n - 1)
                    at(pool, x_ready, n - 3)
                    pool.tensor_tensor(rstd[:, s % 2, :], ve[:, s % 2, :], K["mhalf"][:, 0:TT], ALU.pow).then_inc(rstd_ready, 1)
                if mid:
                    at(pool, o_psum, 2 * n - 4)
                    gate(n - 1, s + 1, (0, 1))

            pipeline(pool, step)


class Norm:

    def __init__(self, ctx, nc, K, name, banks):
        sem = lambda n: K["sem"](f"{name}_{n}")
        sb = lambda n, s: ctx.enter_context(nc.sbuf_tensor(f"{name}_{n}", s, F32))
        self.h, self.ident, self.K = K["h"], K["ident"], K
        self.banks = banks
        self.st, self.mv, self.ve, self.rstd = sb("st", [P, TT, 6]), sb("mv", [P, TT, 2]), sb("ve", [P, TT]), sb("rstd", [P, TT])
        self.spare = sb("spare", [P, 1])
        self.xn, self.xT = sb("xn", [P, TT, D]), sb("xT", [P, KD, T])
        self.stats, self.var, self.veps, self.rstd_ready = sem("stats"), sem("var"), sem("veps"), sem("rstd_ready")
        self.xn_ready, self.xT_psum, self.xT_ready = sem("xn_ready"), sem("xT_psum"), sem("xT_ready")
        self.sems = (self.stats, self.var, self.veps, self.rstd_ready, self.xn_ready, self.xT_psum, self.xT_ready)

    def dve_stats(self, dve, b, hb=None):
        hb = b if hb is None else hb
        for t in range(TT):
            i = dve.bn_stats(self.st[:, t, :], self.h[:, hb, t, :])
        i.then_inc(self.stats, 1)
        at(dve, self.stats, b + 1)
        at(dve, self.veps, b)
        dve.memset(self.spare[:, :], 0.0)
        for t in range(TT):
            i = dve.bn_aggr(self.mv[:, t, :], self.st[:, t, :])
        i.then_inc(self.var, 1)

    def pool_rstd(self, pool, b):
        at(pool, self.var, b + 1)
        at(pool, self.rstd_ready, b)
        pool.tensor_tensor(self.ve[:, :], self.mv[:, :, 1], self.K["eps"][:, 0:TT], ALU.add).then_inc(self.veps, 1)
        at(pool, self.veps, b + 1)
        at(pool, self.xn_ready, b)
        pool.tensor_tensor(self.rstd[:, :], self.ve[:, :], self.K["mhalf"][:, 0:TT], ALU.pow).then_inc(self.rstd_ready, 1)

    def dve_apply(self, dve, b, hb=None):
        hb = b if hb is None else hb
        at(dve, self.rstd_ready, b + 1)
        at(dve, self.xT_psum, b)
        for t in range(TT):
            i = dve.tensor_scalar(self.xn[:, t, :], self.h[:, hb, t, :], self.mv[:, t, 0:1], self.rstd[:, t:t + 1],
                                  ALU.subtract, ALU.mult)
        i.then_inc(self.xn_ready, 1)

    def pe_turn(self, pe, b):
        at(pe, self.xn_ready, b + 1)
        for k in range(KD):
            for t in range(TT):
                mm = pe.transpose(self.banks[k][:, t * P:(t + 1) * P], self.xn[:, t, k * P:(k + 1) * P], self.ident[:, :])
        mm.then_inc(self.xT_psum, 1)

    def act_copy(self, act, b):
        at(act, self.xT_psum, b + 1)
        for k in range(KD):
            i = act.activation(self.xT[:, k, :], self.banks[k][:, :], ACT.Copy)
        i.then_inc(self.xT_ready, 1)


def start(eng, *sems):
    for q in sems:
        eng.sem_inc(q, START)


def scan_stage(nc, K, a):
    S, SP2, LIM, SURE = 16, 8, 10000.0, 9000.0
    with ExitStack() as ctx:
        sem = lambda n: K["sem"]("s2_" + n)
        sb = lambda n, s, d=F32: ctx.enter_context(nc.sbuf_tensor("s2_" + n, s, d))
        h, ident, bank = K["h"], K["ident"], K["bank"]
        nm = Norm(ctx, nc, K, "s2n", (bank[4], bank[6]))
        w_in, w_x, w_dt, w_out = sb("w_in", [P, KD, 2 * INNER]), sb("w_x", [P, MI, 33]), sb("w_dt", [P, MI, P]), sb("w_out", [P, MI, D])
        par = sb("par", [P, 16 + 4 * MI])
        a_log, neg_a = sb("a_log", [P, MI, S]), sb("neg_a", [P, MI, S])
        acc, xc, sz = sb("acc", [P, 2, T]), sb("xc", [P, MI, T]), sb("sz", [P, MI, T])
        pre, soft = sb("pre", [P, MI, T]), sb("soft", [P, MI, T])
        dt, bc = sb("dt", [P, MI, T]), sb("bc", [P, TT, 2 * S])
        dtxT, w = sb("dtxT", [P, TT, INNER]), sb("w", [P, 2, TT, INNER])
        dA, hs, y = sb("dA", [P, 2, MI, T]), sb("hs", [P, 2, MI, T]), sb("y", [P, TT, INNER])
        dtx, y2 = soft, pre
        yg = sb("yg", [P, MI, T])

        a_inv, xmax, dtmax, reach, absmax, allmax, bound, clips = sb("a_inv", [P, MI]), sb("xmax", [P, MI]), sb("dtmax", [P, MI]), sb("reach", [P, MI]), sb("absmax", [P, 2]), sb("allmax", [1, 2]), sb("bound", [1, 1]), sb("clips", [1, 1], I32)
        step_sum = sb("step_sum", [P, 1])
        absmax_psum = sem("absmax_psum")
        bnd, absmax_ready, allmax_ready, clips_ready = sem("bnd"), sem("absmax_ready"), sem("allmax_ready"), sem("clips_ready")

        loaded, neg_a_ready, w_dt_ready = sem("loaded"), sem("neg_a_ready"), sem("w_dt_ready")
        p_psum, p_tap, p_conv1, p_conv2, p_conv, xc_ready = sem("p_psum"), sem("p_tap"), sem("p_conv1"), sem("p_conv2"), sem("p_conv"), sem("xc_ready")
        z_psum, sz_ready = sem("z_psum"), sem("sz_ready")
        bc_psum, bc_ready, raw_psum = sem("bc_psum"), sem("bc_ready"), sem("raw_psum")
        pre_ready, abs_ready, exp_ready, ln_ready, dt_ready, dtx_ready = (
            sem("pre_ready"), sem("abs_ready"), sem("exp_ready"), sem("ln_ready"), sem("dt_ready"), sem("dtx_ready"))
        dtxT_psum, dtxT_ready = sem("dtxT_psum"), sem("dtxT_ready")
        w_pool, w_act, dA_ready, dBx_psum, hs_ready, hsT_psum, y_zero, y_added = (
            sem("w_pool"), sem("w_act"), sem("dA_ready"), sem("dBx_psum"), sem("hs_ready"), sem("hsT_psum"), sem("y_zero"), sem("y_added"))
        yT_psum, y2_ready, yg_ready, o_psum, h_ready = sem("yT_psum"), sem("y2_ready"), sem("yg_ready"), sem("o_psum"), sem("h_ready")
        block = ctx.enter_context(nc.Block())

        @block.sync
        def _(sp):
            start(sp, *nm.sems, absmax_psum, bnd, absmax_ready, allmax_ready, clips_ready, p_psum, p_tap, p_conv1, p_conv2, p_conv, xc_ready, z_psum, sz_ready, bc_psum, bc_ready, raw_psum,
                  pre_ready, abs_ready, exp_ready, ln_ready, dt_ready, dtx_ready, dtxT_psum, dtxT_ready, w_pool, w_act, dA_ready,
                  dBx_psum, hs_ready, hsT_psum, y_zero, y_added, yT_psum, y2_ready, yg_ready, o_psum, h_ready)
            for to, src in ((w_in[:, :, :], a["s2_in"]), (w_x[:, :, :], a["s2_x"]), (w_out[:, :, :], a["s2_out"]),
                            (par[:, :], a["s2_par"]), (a_log[:, :, :], a["s2_alog"])):
                sp.dma_start(to, src).then_inc(loaded, 16)

        @block.tensor
        def _(pe):
            nm.pe_turn(pe, 0)
            pe.wait_ge(loaded, 80)
            pe.wait_ge(w_dt_ready, MI)
            def project(b):
                at(pe, nm.xT_ready, b + 1)
                at(pe, y2_ready, b * MI)
                for m in range(MI):
                    at(pe, p_conv, b * MI + max(0, m - 1))
                    for k in range(KD):
                        mm = pe.matmul(bank[2 + m % 2][:, :], w_in[:, k, m * P:(m + 1) * P], nm.xT[:, k, :], start=(k == 0), stop=(k == KD - 1))
                    mm.then_inc(p_psum, 1)
                    at(pe, sz_ready, b * MI + m)
                    for k in range(KD):
                        mm = pe.matmul(bank[4][:, :], w_in[:, k, INNER + m * P:INNER + (m + 1) * P], nm.xT[:, k, :], start=(k == 0), stop=(k == KD - 1))
                    mm.then_inc(z_psum, 1)

            def states(b):
                at(pe, xc_ready, (b + 1) * MI)
                for k in range(MI):
                    mm = pe.matmul(bank[6][:, :], w_dt[:, k, :], xc[:, k, :], start=(k == 0), stop=(k == MI - 1))
                mm.then_inc(raw_psum, 1)
                at(pe, h_ready, b * 2)
                for t in range(TT):
                    for k in range(MI):
                        mm = pe.matmul(bank[5][:, t * 2 * S:(t + 1) * 2 * S], xc[:, k, t * P:(t + 1) * P], w_x[:, k, 1:33], start=(k == 0), stop=(k == MI - 1))
                mm.then_inc(bc_psum, 1)
                at(pe, pre_ready, (b + 1) * MI)
                at(pe, sz_ready, (b + 1) * MI)
                nm.pe_turn(pe, b + 1)
                at(pe, dtx_ready, (b + 1) * MI)
                for t in range(TT):
                    for k in range(MI):
                        mm = pe.transpose(bank[t][:, k * P:(k + 1) * P], dtx[:, k, t * P:(t + 1) * P], ident[:, :])
                    mm.then_inc(dtxT_psum, 1)
                at(pe, absmax_ready, (b + 1) * 2)
                for i in range(2):
                    mm = pe.transpose(bank[7][0:1, i * P:(i + 1) * P], absmax[:, i:i + 1], ident[:, :])
                mm.then_inc(absmax_psum, 1)

                def turn_input(p, s):
                    at(pe, w_pool, b * (2 * S) + s * 2 + 2)
                    at(pe, w_act, b * (2 * S) + s * 2 + 2)
                    for c in range(MI):
                        at(pe, hs_ready, b * (S * MI) + (s - 1) * MI + c + 1)
                        for t in range(TT):
                            mm = pe.transpose(bank[c][:, t * P:(t + 1) * P], w[:, p, t, c * P:(c + 1) * P], ident[:, :])
                        mm.then_inc(dBx_psum, 1)

                def turn_state(p, s):
                    at(pe, hs_ready, b * (S * MI) + (s + 1) * MI)
                    for t in range(TT):
                        at(pe, y_added, b * (S * TT) + (s - 1) * TT + t + 1)
                        for c in range(MI):
                            mm = pe.transpose(bank[4 + t][:, c * P:(c + 1) * P], hs[:, p, c, t * P:(t + 1) * P], ident[:, :])
                        mm.then_inc(hsT_psum, 1)

                at(pe, dtxT_ready, (b + 1) * TT)
                at(pe, bc_ready, b + 1)
                at(pe, nm.xT_ready, b + 2)
                turn_input(0, 0)
                with pe.Fori(0, SP2 - 1) as j:
                    turn_input(1, 2 * j + 1)
                    turn_state(0, 2 * j)
                    turn_input(0, 2 * j + 2)
                    turn_state(1, 2 * j + 1)
                turn_input(1, S - 1)
                turn_state(0, S - 2)
                turn_state(1, S - 1)
                at(pe, y_added, (b + 1) * (S * TT))
                for c in range(MI):
                    for t in range(TT):
                        mm = pe.transpose(bank[c][:, t * P:(t + 1) * P], y[:, t, c * P:(c + 1) * P], ident[:, :])
                    mm.then_inc(yT_psum, 1)

            def output(b, after):
                at(pe, yg_ready, (b + 1) * MI)
                at(pe, sz_ready, (b + 1 + after) * MI)
                for g in range(2):
                    for t in range(2):
                        for k in range(MI):
                            mm = pe.matmul(bank[4 + g][:, t * D:(t + 1) * D], yg[:, k, (2 * g + t) * P:(2 * g + t + 1) * P], w_out[:, k, :],
                                           start=(k == 0), stop=(k == MI - 1))
                    mm.then_inc(o_psum, 1)

            project(0)
            with pe.Fori(0, B - 1) as b:
                states(b)
                project(b + 1)
                output(b, 1)
            states(B - 1)
            output(B - 1, 0)

        @block.scalar
        def _(act):
            nm.act_copy(act, 0)
            act.wait_ge(loaded, 80)
            act.wait_ge(neg_a_ready, 1)
            act.activation(neg_a[:, :, :], a_log[:, :, :], ACT.Exp).then_inc(neg_a_ready, 1)
            act.wait_ge(neg_a_ready, 3)
            def projected(b):
                def silu_x(m):
                    at(act, p_conv, b * MI + m + 1)
                    at(act, y2_ready, b * MI)
                    act.activation(xc[:, m, :], acc[:, m % 2, :], ACT.Silu).then_inc(xc_ready, 1)

                for m in range(MI):
                    at(act, p_psum, b * MI + m + 1)
                    at(act, xc_ready, b * MI + max(0, m - 1))
                    act.activation(acc[:, m % 2, :], bank[2 + m % 2][:, :], ACT.Identity,
                                   bias=par[:, 16 + m:17 + m], scale=par[:, 4 * m + 3:4 * m + 4]).then_inc(p_tap, 1)
                    at(act, z_psum, b * MI + m + 1)
                    at(act, yg_ready, b * MI)
                    act.activation(sz[:, m, :], bank[4][:, :], ACT.Silu).then_inc(sz_ready, 1)
                    if m:
                        silu_x(m - 1)
                silu_x(MI - 1)

            def states(b):
                for m in range(MI):
                    at(act, pre_ready, b * MI + m + 1)
                    act.activation(soft[:, m, :], pre[:, m, :], ACT.Abs).then_inc(abs_ready, 1)
                for m in range(MI):
                    at(act, abs_ready, b * MI + m + 1)
                    act.activation(soft[:, m, :], soft[:, m, :], ACT.Exp, scale=-1.0).then_inc(exp_ready, 1)
                for m in range(MI):
                    at(act, exp_ready, b * MI + m + 1)
                    act.activation(soft[:, m, :], soft[:, m, :], ACT.Ln, bias=1.0).then_inc(ln_ready, 1)
                nm.act_copy(act, b + 1)
                for t in range(TT):
                    at(act, dtxT_psum, b * TT + t + 1)
                    act.activation(dtxT[:, t, :], bank[t][:, :], ACT.Copy).then_inc(dtxT_ready, 1)
                with act.Fori(0, SP2) as j:
                    at(act, bc_ready, b + 1)
                    at(act, dt_ready, (b + 1) * MI)
                    at(act, dtxT_ready, (b + 1) * TT)
                    for p in range(2):
                        at(act, dBx_psum, b * (S * MI) + j * (2 * MI) + (p - 1) * MI)
                        for t in (2, 3):
                            act.activation(w[:, p, t, :], dtxT[:, t, :], ACT.Copy, scale=bc[:, t, :][:, bass.ds(j * 2 + p, 1)]).then_inc(w_act, 1)
                        at(act, hs_ready, b * (S * MI) + j * (2 * MI) + (p - 1) * MI)
                        for c in range(MI):
                            act.activation(dA[:, p, c, :], dt[:, c, :], ACT.Exp, scale=neg_a[:, c, :][:, bass.ds(j * 2 + p, 1)]).then_inc(dA_ready, 1)

            projected(0)
            with act.Fori(0, B - 1) as b:
                states(b)
                projected(b + 1)
            states(B - 1)

        @block.vector
        def _(dve):
            nm.dve_stats(dve, 0)
            nm.dve_apply(dve, 0)
            dve.wait_ge(loaded, 80)
            dve.tensor_scalar(a_log[:, :, :], a_log[:, :, :], -6.0, 6.0, ALU.max, ALU.min).then_inc(neg_a_ready, 1)
            for k in range(MI):
                dve.tensor_scalar(w_dt[:, k, :], K["ones"][:, :], w_x[:, k, 0:1], None, ALU.mult).then_inc(w_dt_ready, 1)
            dve.wait_ge(neg_a_ready, 2)
            dve.tensor_reduce(a_inv[:, :], neg_a[:, :, :], AX.X, ALU.min).then_inc(w_dt_ready, 1)
            dve.wait_ge(w_dt_ready, MI + 1)
            dve.reciprocal(a_inv[:, :], a_inv[:, :]).then_inc(w_dt_ready, 1)
            dve.wait_ge(w_dt_ready, MI + 2)
            dve.tensor_scalar(neg_a[:, :, :], neg_a[:, :, :], -1.0, None, ALU.mult).then_inc(neg_a_ready, 1)
            dve.memset(y[:, :, :], 0.0).then_inc(y_zero, 1)
            def convolve(b):
                for m in range(MI):
                    pb = bank[2 + m % 2]
                    for i, got, done in ((1, p_tap, p_conv1), (2, p_conv1, p_conv2), (3, p_conv2, p_conv)):
                        at(dve, got, b * MI + m + 1)
                        dve.scalar_tensor_tensor(acc[:, m % 2, i:T], pb[:, 0:T - i], par[:, 4 * m + 3 - i:4 * m + 4 - i],
                                                 acc[:, m % 2, i:T], ALU.mult, ALU.add).then_inc(done, 1)

            def states(b):
                at(dve, yg_ready, b * MI)
                for m in range(MI):
                    at(dve, raw_psum, b + 1)
                    dve.tensor_scalar(pre[:, m, :], bank[6][:, :], par[:, 20 + m:21 + m], par[:, 24 + m:25 + m], ALU.mult, ALU.add).then_inc(pre_ready, 1)
                at(dve, bc_psum, b + 1)
                dve.tensor_copy(bc[:, :, :].rearrange("p t s -> p (t s)"), bank[5][:, 0:TT * 2 * S]).then_inc(bc_ready, 1)
                nm.dve_stats(dve, b + 1)
                dve.tensor_reduce(xmax[:, :], xc[:, :, :], AX.X, ALU.max, apply_absolute_value=True).then_inc(bnd, 1)
                at(dve, bc_ready, b + 1)
                dve.tensor_reduce(absmax[:, 1:2], bc[:, :, 0:S], AX.XY, ALU.max, apply_absolute_value=True).then_inc(absmax_ready, 1)
                nm.dve_apply(dve, b + 1)
                for m in range(MI):
                    at(dve, ln_ready, b * MI + m + 1)
                    dve.scalar_tensor_tensor(dt[:, m, :], pre[:, m, :], 0.0, soft[:, m, :], ALU.max, ALU.add).then_inc(dt_ready, 1)
                for m in range(MI):
                    at(dve, dt_ready, b * MI + m + 1)
                    dve.tensor_tensor(dtx[:, m, :], dt[:, m, :], xc[:, m, :], ALU.mult).then_inc(dtx_ready, 1)
                dve.tensor_reduce(dtmax[:, :], dt[:, :, :], AX.X, ALU.max).then_inc(bnd, 1)
                at(dve, bnd, b * 4 + 2)
                dve.tensor_tensor(reach[:, :], dtmax[:, :], a_inv[:, :], ALU.add).then_inc(bnd, 1)
                at(dve, bnd, b * 4 + 3)
                dve.tensor_tensor(dtmax[:, :], reach[:, :], xmax[:, :], ALU.mult).then_inc(bnd, 1)
                at(dve, bnd, (b + 1) * 4)
                dve.tensor_reduce(absmax[:, 0:1], dtmax[:, :], AX.X, ALU.max).then_inc(absmax_ready, 1)
                at(dve, absmax_psum, b + 1)
                dve.tensor_reduce(allmax[:, :], bank[7][0:1, 0:2 * P].rearrange("p (i c) -> p i c", i=2), AX.X, ALU.max).then_inc(allmax_ready, 1)
                at(dve, allmax_ready, b + 1)
                dve.tensor_tensor(bound[:, :], allmax[0:1, 0:1], allmax[0:1, 1:2], ALU.mult).then_inc(clips_ready, 1)
                at(dve, clips_ready, b * 2 + 1)
                dve.tensor_scalar(clips[:, :], bound[:, :], SURE, None, ALU.is_le).then_inc(clips_ready, 1)
                at(dve, clips_ready, b * 2 + 2)
                dve.memset(nm.spare[:, :], 0.0)
                sure = dve.value_load(clips[0:1, 0:1], min_val=0, max_val=1)

                def ready(s, c):
                    at(dve, dA_ready, b * (S * MI) + s * MI + c + 1)
                    at(dve, dBx_psum, b * (S * MI) + s * MI + c + 1)
                    at(dve, hsT_psum, b * (S * TT) + (s - 1) * TT)

                def scan(p, s):
                    for c in range(MI):
                        ready(s, c)
                        dve.tensor_tensor_scan(hs[:, p, c, :], dA[:, p, c, :], bank[c][:, :], 0.0, ALU.mult, ALU.add).then_inc(hs_ready, 1)

                def clipped_scan(p, s):
                    for c in range(MI):
                        ready(s, c)
                        dve.tensor_scalar(hs[:, p, c, 0:1], bank[c][:, 0:1], -LIM, LIM, ALU.max, ALU.min)
                        with dve.Fori(0, T - 1) as n:
                            dve.drain()
                            dve.scalar_tensor_tensor(step_sum[:, :], dA[:, p, c, bass.ds(n + 1, 1)], hs[:, p, c, bass.ds(n, 1)],
                                                     bank[c][:, bass.ds(n + 1, 1)], ALU.mult, ALU.add)
                            dve.drain()
                            dve.tensor_scalar(hs[:, p, c, bass.ds(n + 1, 1)], step_sum[:, :], -LIM, LIM, ALU.max, ALU.min)
                        dve.drain().then_inc(hs_ready, 1)

                def add_y(s):
                    at(dve, y_zero, b + 1)
                    at(dve, y_added, b * (S * TT) + s * TT)
                    for t in range(TT):
                        at(dve, hsT_psum, b * (S * TT) + s * TT + t + 1)
                        factor = bc[:, t, S + s:S + s + 1] if isinstance(s, int) else bc[:, t, :][:, bass.ds(s + S, 1)]
                        dve.scalar_tensor_tensor(y[:, t, :], bank[4 + t][:, :], factor, y[:, t, :], ALU.mult, ALU.add).then_inc(y_added, 1)

                def all_states(scan):
                    scan(0, 0)
                    with dve.Fori(0, SP2 - 1) as j:
                        scan(1, 2 * j + 1)
                        add_y(2 * j)
                        scan(0, 2 * j + 2)
                        add_y(2 * j + 1)
                    scan(1, S - 1)
                    add_y(S - 2)
                    add_y(S - 1)

                with dve.If(sure == 1):
                    all_states(scan)
                with dve.Else():
                    all_states(clipped_scan)
                for c in range(MI):
                    at(dve, yT_psum, b * MI + c + 1)
                    dve.scalar_tensor_tensor(y2[:, c, :], xc[:, c, :], par[:, 28 + c:29 + c], bank[c][:, :], ALU.mult, ALU.add).then_inc(y2_ready, 1)
                for c in (1, 3):
                    at(dve, y2_ready, b * MI + c + 1)
                    dve.tensor_tensor(yg[:, c, :], y2[:, c, :], sz[:, c, :], ALU.mult).then_inc(yg_ready, 1)
                at(dve, yT_psum, (b + 1) * MI)
                dve.memset(y[:, :, :], 0.0).then_inc(y_zero, 1)

            def residual(b):
                for g in range(2):
                    at(dve, o_psum, b * 2 + g + 1)
                    hb = h[:, b, 2 * g:2 * g + 2, :].rearrange("p t d -> p (t d)")
                    dve.tensor_tensor(hb, bank[4 + g][:, :], hb, ALU.add).then_inc(h_ready, 1)
                at(dve, h_ready, (b + 1) * 2)

            convolve(0)
            with dve.Fori(0, B - 1) as b:
                states(b)
                convolve(b + 1)
                residual(b)
            states(B - 1)
            residual(B - 1)

        @block.gpsimd
        def _(pool):
            nm.pool_rstd(pool, 0)
            with pool.Fori(0, B) as b:
                nm.pool_rstd(pool, b + 1)
                with pool.Fori(0, SP2) as j:
                    at(pool, bc_ready, b + 1)
                    at(pool, dtxT_ready, (b + 1) * TT)
                    for p in range(2):
                        at(pool, dBx_psum, b * (S * MI) + j * (2 * MI) + (p - 1) * MI)
                        for t in (0, 1):
                            pool.tensor_tensor(w[:, p, t, :], dtxT[:, t, :], bc[:, t, :][:, bass.ds(j * 2 + p, 1)].broadcast_to([P, INNER]), ALU.mult).then_inc(w_pool, 1)
                for c in (0, 2):
                    at(pool, y2_ready, b * MI + c + 1)
                    at(pool, o_psum, b * 2)
                    pool.tensor_tensor(yg[:, c, :], y2[:, c, :], sz[:, c, :], ALU.mult).then_inc(yg_ready, 1)


def slot_stage(nc, K, a):
    H, NS, F = 16, 16, 1024
    HS, R, KF = H * NS, B * NS, F // P
    G, GW = 4, 32
    NQ = NS // G
    with ExitStack() as ctx:
        sem = lambda n: K["sem"]("s3_" + n)
        sb = lambda n, s, d=F32: ctx.enter_context(nc.sbuf_tensor("s3_" + n, s, d))
        h, ident, bank = K["h"], K["ident"], K["bank"]
        nm = Norm(ctx, nc, K, "s3n", (bank[0], bank[1]))
        wts = {n: sb(n, [P, KD, D]) for n in ("dWq", "dWkT", "dWv", "dWo", "cWqT", "cWk", "cWv", "cWo")}
        cols = sb("cols", [P, KD, 7])
        e_bias, e_b2 = sb("e_bias", [P, 2 * F]), sb("e_b2", [P, KD, NS])
        slotT, rows = sb("slotT", [P, KD, NS]), sb("rows", [R, 4, D])
        c_bo = sb("c_bo", [P, D])
        W1, Wg, W2 = sb("W1", [P, G, KD, F]), sb("Wg", [P, G, KD, F]), sb("W2", [P, G, KF, D])
        mask = sb("mask", [P, KD, H])
        bqw = sb("bqw", [P, KD, P])
        qh, qblk, md, sbias = sb("qh", [P, KD, NS]), sb("qblk", [P, KD, HS]), sb("md", [P, KD, HS]), sb("sbias", [P, 2])
        mx, top, nb, sm, rs = (sb(n, [P, 2]) for n in ("mx", "top", "nb", "sm", "rs"))
        pr, prT, gT = sb("pr", [P, 2, T]), sb("prT", [P, TT, HS]), sb("gT", [P, KD, HS])
        own, att, attb = sb("own", [P, KD, HS]), sb("att", [P, B, KD, NS]), sb("attb", [P, KD, R])
        o, qbo, st, mv, ve, rstd, on, og, ob = (sb("o", [R, D]), sb("qbo", [R, D]), sb("st", [R, 6]), sb("mv", [R, 2]), sb("ve", [R, 1]),
                                               sb("rstd", [R, 1]), sb("on", [R, D]), sb("og", [R, D]), sb("ob", [R, D]))
        oT, hT, oTb, o2T = (sb(n, [P, KD, NS, B]) for n in ("oT", "hT", "oTb", "o2T"))
        hx = sb("hx", [P, KD, G, GW])
        pre, ug, ugT, yx = sb("pre", [P, 2 * F]), sb("ug", [P, F]), sb("ugT", [P, KF, G * GW]), sb("yx", [P, D])
        kc, vc = sb("kc", [P, KD, B, NS]), sb("vc", [P, KD, B, NS])
        mb, rb, vw = sb("mb", [P, KD, HS]), sb("rb", [P, HS]), sb("vw", [P, 2, D])
        by_tile = lambda x: x.rearrange("p (t s) -> p t s", t=TT)
        cm, cs, cr = sb("cm", [P, TT * H]), sb("cs", [P, TT * H]), sb("cr", [P, TT * H])
        kblk, vblk = gT, own
        sc, cp = by_tile(pr[:, :, :].rearrange("p g t -> p (g t)")), prT
        ce, cd, cpT = by_tile(ug[:, :]), by_tile(ugT[:, :, :].rearrange("p f c -> p (f c)")), pre[:, 0:2 * T].rearrange("p (g t) -> p g t", g=2)

        loaded, bias_loaded, W1_loaded, Wg_loaded, W2_loaded = sem("loaded"), sem("bias_loaded"), sem("W1_loaded"), sem("Wg_loaded"), sem("W2_loaded")
        bias_zero, hx_ready, ugT_psum, ugT_ready, yx_ready, yT_psum = sem("bias_zero"), sem("hx_ready"), sem("ugT_psum"), sem("ugT_ready"), sem("yx_ready"), sem("yT_psum")
        setup_pe, setup_dve, qblk_ready = sem("setup_pe"), sem("setup_dve"), sem("qblk_ready")
        s_psum, mx_ready, top_ready, nb_ready, pr_exp, rs_ready, pr_ready = (
            sem(n) for n in ("s_psum", "mx_ready", "top_ready", "nb_ready", "pr_exp", "rs_ready", "pr_ready"))
        prT_psum, prT_ready, g_psum, g_ready, v_psum, own_ready, att_ready = (
            sem(n) for n in ("prT_psum", "prT_ready", "g_psum", "g_ready", "v_psum", "own_ready", "att_ready"))
        join, jpool, jpe, jact = sem("join"), sem("jpool"), sem("jpe"), sem("jact")
        u_psum, pre_ready, silu_ready, ug_ready, y_psum, o2_ready = (sem(n) for n in ("u_psum", "pre_ready", "silu_ready", "ug_ready", "y_psum", "o2_ready"))
        kv_psum, kv_ready = sem("kv_psum"), sem("kv_ready")
        vblk_ready = sem("vblk_ready")
        kblk_ready, mb_psum, mb_ready, rb_psum, rb_ready, vw_psum, vw_ready = (
            sem(n) for n in ("kblk_ready", "mb_psum", "mb_ready", "rb_psum", "rb_ready", "vw_psum", "vw_ready"))
        sc_psum, sc_ready, cm_ready, cd_ready, ce_ready, cs_ready, cr_ready, cp_ready = (
            sem(n) for n in ("sc_psum", "sc_ready", "cm_ready", "cd_ready", "ce_ready", "cs_ready", "cr_ready", "cp_ready"))
        cpT_psum, cpT_ready, c_psum, hb_ready, h_ready = (sem(n) for n in ("cpT_psum", "cpT_ready", "c_psum", "hb_ready", "h_ready"))
        AGAIN = B + 1
        NLOAD = 16 * (len(wts) + 6)
        block = ctx.enter_context(nc.Block())
        headmask = lambda k: mask[:, k, :].rearrange("p (h o) -> p h o", o=1).broadcast_to([P, H, NS])
        by_head = lambda x: x.rearrange("p (h s) -> p h s", h=H)
        over_heads = lambda x: x.rearrange("p (o s) -> p o s", o=1).broadcast_to([P, H, NS])

        @block.sync
        def _(sp):
            start(sp, *nm.sems, s_psum, mx_ready, top_ready, nb_ready, pr_exp, rs_ready, pr_ready, prT_psum, prT_ready, g_psum, g_ready,
                  v_psum, own_ready, att_ready, hx_ready, ugT_psum, ugT_ready, yx_ready, yT_psum, u_psum, pre_ready, silu_ready, ug_ready, y_psum, o2_ready,
                  vblk_ready, kblk_ready, mb_psum, mb_ready, rb_psum, rb_ready, vw_psum, vw_ready, sc_psum, sc_ready, cm_ready, cd_ready,
                  ce_ready, cs_ready, cr_ready, cp_ready, cpT_psum, cpT_ready, c_psum, hb_ready, h_ready)
            for n, t in wts.items():
                sp.dma_start(t[:, :, :], a["s3_" + n]).then_inc(loaded, 16)
            for to, src in ((cols[:, :, :], a["s3_cols"]), (e_b2[:, :, :], a["s3_b2"]),
                            (slotT[:, :, :], a["s3_slotT"]), (rows[:, :, :], a["s3_rows"]), (c_bo[:, :], a["s3_cbo"].broadcast_to([P, D]))):
                sp.dma_start(to, src).then_inc(loaded, 16)
            sp.dma_start(mask[:, :, :], a["s3_mask"]).then_inc(loaded, 16)
            sp.wait_ge(bias_zero, 1)
            with sp.Fori(0, NQ) as q:
                at(sp, pre_ready, q * 4)
                for g in range(G):
                    sp.dma_start(e_bias[GW * g:GW * g + B, :], a["s3_bias"][bass.ds(q * G + g, 1), :].broadcast_to([B, 2 * F])).then_inc(bias_loaded, 16)
                for w, name, done, used in ((W1, "s3_W1", W1_loaded, q * 4), (Wg, "s3_Wg", Wg_loaded, q * 4)):
                    at(sp, u_psum, used - (2 if w is W1 else 0))
                    for g in range(G):
                        sp.dma_start(w[:, g, :, :], a[name][q * G + g]).then_inc(done, 16)
                at(sp, y_psum, q)
                for g in range(G):
                    sp.dma_start(W2[:, g, :, :], a["s3_W2"][q * G + g]).then_inc(W2_loaded, 16)

        @block.tensor
        def _(pe):
            nm.pe_turn(pe, 0)
            pe.wait_ge(loaded, NLOAD)
            for m in range(KD):
                for k in range(KD):
                    mm = pe.matmul(bank[2][:, m * NS:(m + 1) * NS], wts["dWq"][:, k, m * P:(m + 1) * P], slotT[:, k, :], start=(k == 0), stop=(k == KD - 1))
            mm.then_inc(setup_pe, 1)
            pe.wait_ge(qblk_ready, KD)
            for m in range(KD):
                for k in range(KD):
                    mm = pe.matmul(bank[3][:, m * HS:(m + 1) * HS], wts["dWkT"][:, k, m * P:(m + 1) * P], qblk[:, k, :], start=(k == 0), stop=(k == KD - 1))
            for g in range(2):
                for k in range(KD):
                    mm = pe.matmul(bank[4][:, g:g + 1], qblk[:, k, g * P:(g + 1) * P], cols[:, k, 1:2], start=(k == 0), stop=(k == KD - 1))
            mm.then_inc(setup_pe, 1)
            pe.wait_ge(setup_dve, 3)
            with pe.Fori(0, B) as b:
                at(pe, nm.xT_ready, b + 1)
                for g in range(2):
                    at(pe, pr_exp, b * 2 + g)
                    for k in range(KD):
                        mm = pe.matmul(bank[2 + g][:, :], md[:, k, g * P:(g + 1) * P], nm.xT[:, k, :], start=(k == 0), stop=(k == KD - 1))
                    mm.then_inc(s_psum, 1)
                at(pe, pr_ready, (b + 1) * 2)
                for q in range(2):
                    for t in range(2):
                        for g in range(2):
                            mm = pe.transpose(bank[4 + q][:, t * HS + g * P:t * HS + (g + 1) * P], pr[:, g, (2 * q + t) * P:(2 * q + t + 1) * P], ident[:, :])
                    mm.then_inc(prT_psum, 1)
                at(pe, prT_ready, (b + 1) * 2)
                for m in range(KD):
                    for t in range(TT):
                        mm = pe.matmul(bank[6][:, m * HS:(m + 1) * HS], nm.xn[:, t, m * P:(m + 1) * P], prT[:, t, :], start=(t == 0), stop=(t == TT - 1))
                mm.then_inc(g_psum, 1)
                at(pe, g_ready, b + 1)
                at(pe, own_ready, b * KD)
                for m in range(KD):
                    for k in range(KD):
                        mm = pe.matmul(bank[7][:, m * HS:(m + 1) * HS], wts["dWv"][:, k, m * P:(m + 1) * P], gT[:, k, :], start=(k == 0), stop=(k == KD - 1))
                mm.then_inc(v_psum, 1)
                nm.pe_turn(pe, b + 1)
            pe.wait_ge(join, KD)
            pe.wait_ge(nm.xT_ready, AGAIN + START)
            for k in range(KD):
                mm = pe.matmul(bank[0][0:R, 0:D], attb[:, k, :], wts["dWo"][:, k, :], start=(k == 0), stop=(k == KD - 1))
            mm.then_inc(jpe, 1)
            pe.wait_ge(join, KD + 2)
            for k in range(KD):
                mm = pe.transpose(bank[1][:, k * R:(k + 1) * R], o[:, k * P:(k + 1) * P], ident[0:R, 0:R])
            mm.then_inc(jpe, 1)
            pe.wait_ge(jpool, 4)
            for k in range(KD):
                mm = pe.transpose(bank[2][:, k * R:(k + 1) * R], ob[:, k * P:(k + 1) * P], ident[0:R, 0:R])
            mm.then_inc(jpe, 1)
            with pe.Fori(0, NQ) as q:
                at(pe, hx_ready, q + 1)
                for j, (w, there) in enumerate(((W1, W1_loaded), (Wg, Wg_loaded))):
                    pe.wait_ge(there, (q + 1) * (16 * G))
                    for c in range(2):
                        at(pe, pre_ready, q * 4 + (2 * j + c + 1) - 4)
                        for k in range(KD):
                            for g in range(G):
                                mm = pe.matmul(bank[2 * j + c][GW * g:GW * (g + 1), :], hx[:, k, g, :], w[:, g, k, c * 512:(c + 1) * 512],
                                               start=(k == 0), stop=(k == KD - 1))
                        mm.then_inc(u_psum, 1)
                at(pe, ug_ready, q + 1)
                for f in range(KF):
                    mm = pe.transpose(bank[4 + f // 4][:, (f % 4) * P:(f % 4 + 1) * P], ug[:, f * P:(f + 1) * P], ident[:, :])
                mm.then_inc(ugT_psum, 1)
                at(pe, ugT_ready, q * 2 + 2)
                pe.wait_ge(W2_loaded, (q + 1) * (16 * G))
                for f in range(KF):
                    for g in range(G):
                        mm = pe.matmul(bank[6][GW * g:GW * (g + 1), 0:D], ugT[:, f, GW * g:GW * (g + 1)], W2[:, g, f, :], start=(f == 0), stop=(f == KF - 1))
                mm.then_inc(y_psum, 1)
                at(pe, yx_ready, q + 1)
                for k in range(KD):
                    mm = pe.transpose(bank[7][:, k * P:(k + 1) * P], yx[:, k * P:(k + 1) * P], ident[:, :])
                mm.then_inc(yT_psum, 1)
            pe.wait_ge(o2_ready, NQ * KD + START)
            for j, w in enumerate(("cWk", "cWv")):
                for m in range(KD):
                    for k in range(KD):
                        mm = pe.matmul(bank[6 + j][:, m * R:(m + 1) * R], wts[w][:, k, m * P:(m + 1) * P], o2T[:, k, :, :].rearrange("p s b -> p (s b)"), start=(k == 0), stop=(k == KD - 1))
                mm.then_inc(kv_psum, 1)

            def score(b):
                nm.pe_turn(pe, b + AGAIN)
                at(pe, kblk_ready, b * KD + KD)
                at(pe, h_ready, b * 2 - 2)
                for m in range(KD):
                    for k in range(KD):
                        mm = pe.matmul(bank[2][:, m * HS:(m + 1) * HS], wts["cWqT"][:, k, m * P:(m + 1) * P], kblk[:, k, :], start=(k == 0), stop=(k == KD - 1))
                mm.then_inc(mb_psum, 1)
                at(pe, rb_ready, b)
                for k in range(KD):
                    mm = pe.matmul(bank[3][:, 0:HS], bqw[:, k, :], kblk[:, k, :], start=(k == 0), stop=(k == KD - 1))
                mm.then_inc(rb_psum, 1)
                at(pe, nm.xT_ready, b + (AGAIN + 1))
                at(pe, mb_ready, b + 1)
                at(pe, sc_ready, b * 2)
                for q in range(2):
                    for t in range(2):
                        for k in range(KD):
                            mm = pe.matmul(bank[5 + q][:, t * HS:(t + 1) * HS], nm.xT[:, k, (2 * q + t) * P:(2 * q + t + 1) * P], mb[:, k, :], start=(k == 0), stop=(k == KD - 1))
                    mm.then_inc(sc_psum, 1)

            def mix(b):
                at(pe, vblk_ready, b * KD + KD)
                at(pe, vw_ready, b)
                for g in range(2):
                    for k in range(KD):
                        mm = pe.matmul(bank[4][:, g * D:(g + 1) * D], vblk[:, k, g * P:(g + 1) * P], wts["cWo"][:, k, :], start=(k == 0), stop=(k == KD - 1))
                mm.then_inc(vw_psum, 1)
                at(pe, cp_ready, b + 1)
                for g in range(2):
                    for t in range(TT):
                        mm = pe.transpose(bank[g][:, t * P:(t + 1) * P], cp[:, t, g * P:(g + 1) * P], ident[:, :])
                    mm.then_inc(cpT_psum, 1)
                at(pe, cpT_ready, b * 2 + 2)
                at(pe, vw_ready, b + 1)
                at(pe, h_ready, b * 2)
                for q, bk in ((0, 2), (1, 7)):
                    for t in range(2):
                        for g in range(2):
                            mm = pe.matmul(bank[bk][:, t * D:(t + 1) * D], cpT[:, g, (2 * q + t) * P:(2 * q + t + 1) * P], vw[:, g, :], start=(g == 0), stop=(g == 1))
                    mm.then_inc(c_psum, 1)

            score(0)
            with pe.Fori(0, B - 1) as b:
                score(b + 1)
                mix(b)
            mix(B - 1)

        @block.scalar
        def _(act):
            nm.act_copy(act, 0)
            with act.Fori(0, B) as b:
                for g in range(2):
                    at(act, nb_ready, b * 2 + g + 1)
                    at(act, s_psum, b * 2 + g + 1)
                    at(act, prT_psum, b * 2)
                    act.activation(pr[:, g, :], bank[2 + g][:, :], ACT.Exp, bias=nb[:, g:g + 1], accum_out=sm[:, g:g + 1]).then_inc(pr_exp, 1)
                for q in range(2):
                    at(act, prT_psum, b * 2 + q + 1)
                    at(act, g_psum, b)
                    act.activation(prT[:, 2 * q:2 * q + 2, :], bank[4 + q][:, :], ACT.Copy).then_inc(prT_ready, 1)
                at(act, g_psum, b + 1)
                at(act, v_psum, b)
                act.activation(gT[:, :, :], bank[6][:, :], ACT.Copy).then_inc(g_ready, 1)
                nm.act_copy(act, b + 1)
            act.wait_ge(jpe, 2)
            for k in range(KD):
                act.activation(oT[:, k, :, :], bank[1][:, k * R:(k + 1) * R].rearrange("p (b s) -> p s b", b=B), ACT.Copy).then_inc(jact, 1)
            act.wait_ge(jpe, 3)
            for k in range(KD):
                act.activation(hT[:, k, :, :], bank[2][:, k * R:(k + 1) * R].rearrange("p (b s) -> p s b", b=B), ACT.Copy).then_inc(jact, 1)
            with act.Fori(0, NQ) as q:
                at(act, pre_ready, q * 4 + 4)
                act.activation(pre[:, :], pre[:, :], ACT.Silu).then_inc(silu_ready, 1)
                for c in range(2):
                    at(act, ugT_psum, q + 1)
                    act.activation(ugT[:, 4 * c:4 * c + 4, :], bank[4 + c][:, :], ACT.Copy).then_inc(ugT_ready, 1)

            def score(b):
                nm.act_copy(act, b + AGAIN)
                at(act, mb_psum, b + 1)
                at(act, sc_psum, b * 2)
                act.activation(mb[:, :, :], bank[2][:, :], ACT.Copy).then_inc(mb_ready, 1)
                at(act, rb_psum, b + 1)
                at(act, sc_ready, b * 2)
                act.activation(rb[:, :], bank[3][:, 0:HS], ACT.Copy).then_inc(rb_ready, 1)

            def exponent(b):
                at(act, cd_ready, b + 1)
                at(act, cp_ready, b)
                act.activation(ce[:, :, :], cd[:, :, :], ACT.Exp).then_inc(ce_ready, 1)

            def mix(b):
                at(act, vw_psum, b + 1)
                at(act, c_psum, b * 2)
                act.activation(vw[:, :, :], bank[4][:, :], ACT.Copy).then_inc(vw_ready, 1)
                for g in range(2):
                    at(act, cpT_psum, b * 2 + g + 1)
                    at(act, c_psum, b * 2)
                    act.activation(cpT[:, g, :], bank[g][:, :], ACT.Copy).then_inc(cpT_ready, 1)

            score(0)
            with act.Fori(0, B - 1) as b:
                exponent(b)
                score(b + 1)
                mix(b)
            exponent(B - 1)
            mix(B - 1)

        @block.vector
        def _(dve):
            dve.memset(e_bias[:, :], 0.0).then_inc(bias_zero, 1)
            dve.memset(hx[:, :, :, :], 0.0).then_inc(bias_zero, 1)
            nm.dve_stats(dve, 0)
            nm.dve_apply(dve, 0)
            dve.wait_ge(bias_zero, 2)
            dve.wait_ge(loaded, NLOAD)
            dve.wait_ge(setup_pe, 1)
            for m in range(KD):
                dve.tensor_scalar(qh[:, m, :], bank[2][:, m * NS:(m + 1) * NS], cols[:, m, 0:1], 0.25, ALU.add, ALU.mult).then_inc(setup_dve, 1)
            dve.wait_ge(setup_dve, 2)
            for m in range(KD):
                dve.tensor_tensor(by_head(qblk[:, m, :]), headmask(m), over_heads(qh[:, m, :]), ALU.mult).then_inc(qblk_ready, 1)
            for k in range(KD):
                dve.tensor_scalar(bqw[:, k, :], K["ones"][:, :], cols[:, k, 3:4], None, ALU.mult)
            dve.wait_ge(setup_pe, 2)
            dve.tensor_copy(sbias[:, :], bank[4][:, 0:2])
            dve.tensor_copy(md[:, :, :].rearrange("p k s -> p (k s)"), bank[3][:, :]).then_inc(setup_dve, 1)
            dve.wait_ge(setup_dve, 3)
            with dve.Fori(0, B) as b:
                for g in range(2):
                    at(dve, s_psum, b * 2 + g + 1)
                    at(dve, nb_ready, b * 2 + g)
                    dve.tensor_reduce(mx[:, g:g + 1], bank[2 + g][:, :], AX.X, ALU.max).then_inc(mx_ready, 1)
                    at(dve, mx_ready, b * 2 + g + 1)
                    dve.tensor_scalar(top[:, g:g + 1], mx[:, g:g + 1], sbias[:, g:g + 1], -1.0, ALU.add, ALU.mult).then_inc(top_ready, 1)
                    at(dve, top_ready, b * 2 + g + 1)
                    at(dve, pr_exp, b * 2)
                    dve.tensor_scalar(nb[:, g:g + 1], top[:, g:g + 1], sbias[:, g:g + 1], None, ALU.add).then_inc(nb_ready, 1)
                nm.dve_stats(dve, b + 1)
                for g in range(2):
                    at(dve, pr_exp, b * 2 + g + 1)
                    dve.reciprocal(rs[:, g:g + 1], sm[:, g:g + 1]).then_inc(rs_ready, 1)
                    at(dve, rs_ready, b * 2 + g + 1)
                    dve.tensor_scalar(pr[:, g, :], pr[:, g, :], rs[:, g:g + 1], None, ALU.mult).then_inc(pr_ready, 1)
                at(dve, g_psum, b + 1)
                nm.dve_apply(dve, b + 1)
                at(dve, v_psum, b + 1)
                for m in range(KD):
                    dve.tensor_tensor(by_head(own[:, m, :]), by_head(bank[7][:, m * HS:(m + 1) * HS]), headmask(m), ALU.mult).then_inc(own_ready, 1)
                at(dve, own_ready, b * KD + KD)
                for m in range(KD):
                    dve.tensor_reduce(att[:, b, m, :], own[:, m, :].rearrange("p (h s) -> p s h", h=H), AX.X, ALU.add).then_inc(att_ready, 1)
            dve.wait_ge(att_ready, B * KD + START)
            for m in range(KD):
                dve.tensor_scalar(attb[:, m, :].rearrange("p (b s) -> p b s", b=B), att[:, :, m, :], cols[:, m, 2:3], None, ALU.add).then_inc(join, 1)
            dve.tensor_tensor(qbo[:, :], rows[:, 0, :], rows[:, 1, :], ALU.add).then_inc(join, 1)
            dve.wait_ge(join, KD + 1)
            dve.wait_ge(jpe, 1)
            dve.tensor_tensor(o[:, :], bank[0][0:R, 0:D], qbo[:, :], ALU.add).then_inc(join, 1)
            dve.wait_ge(join, KD + 2)
            dve.bn_stats(st[:, :], o[:, :]).then_inc(join, 1)
            dve.wait_ge(join, KD + 3)
            dve.bn_aggr(mv[:, :], st[:, :]).then_inc(join, 1)
            dve.wait_ge(jpool, 2)
            dve.wait_ge(join, KD + 4)
            dve.tensor_scalar(on[:, :], o[:, :], mv[:, 0:1], rstd[:, :], ALU.subtract, ALU.mult).then_inc(join, 1)
            dve.wait_ge(jact, KD)
            for k in range(KD):
                dve.tensor_tensor(oTb[:, k, :, :], oT[:, k, :, :], e_b2[:, k, :].rearrange("p (s o) -> p s o", o=1).broadcast_to([P, NS, B]), ALU.add).then_inc(jact, 1)
            dve.wait_ge(jact, 3 * KD)
            with dve.Fori(0, NQ) as q:
                at(dve, u_psum, q * 4)
                dve.tensor_copy(hx[:, :, :, 0:B], hT[:, :, bass.ds(q * G, G), :]).then_inc(hx_ready, 1)
                dve.wait_ge(bias_loaded, (q + 1) * (16 * G))
                at(dve, ug_ready, q)
                for c in range(4):
                    at(dve, u_psum, q * 4 + c + 1)
                    dve.tensor_tensor(pre[:, c * 512:(c + 1) * 512], bank[c][:, :], e_bias[:, c * 512:(c + 1) * 512], ALU.add).then_inc(pre_ready, 1)
                at(dve, silu_ready, q + 1)
                at(dve, ugT_psum, q)
                dve.tensor_tensor(ug[:, :], pre[:, 0:F], pre[:, F:2 * F], ALU.mult).then_inc(ug_ready, 1)
                at(dve, y_psum, q + 1)
                at(dve, yT_psum, q)
                dve.tensor_copy(yx[:, :], bank[6][:, 0:D]).then_inc(yx_ready, 1)
                at(dve, yT_psum, q + 1)
                for k in range(KD):
                    dve.tensor_tensor(o2T[:, k, bass.ds(q * G, G), :], bank[7][:, k * P:(k + 1) * P].rearrange("p (g c) -> p g c", g=G)[:, :, 0:B],
                                      oTb[:, k, bass.ds(q * G, G), :], ALU.add).then_inc(o2_ready, 1)
            for m in range(KD):
                dve.wait_ge(kv_psum, 1)
                dve.tensor_scalar(kc[:, m, :, :], bank[6][:, m * R:(m + 1) * R].rearrange("p (s b) -> p b s", b=B), cols[:, m, 4:5], 0.25, ALU.add, ALU.mult).then_inc(kv_ready, 1)
            for m in range(KD):
                dve.wait_ge(kv_psum, 2)
                dve.tensor_scalar(vc[:, m, :, :], bank[7][:, m * R:(m + 1) * R].rearrange("p (s b) -> p b s", b=B), cols[:, m, 5:6], None, ALU.add).then_inc(kv_ready, 1)
            dve.wait_ge(kv_ready, 2 * KD)
            flat = lambda x: x.rearrange("p t (h s) -> p (t h) s", h=H)
            wide = lambda x: x.rearrange("p (t o) -> p t o", o=1).broadcast_to([P, TT * H, NS])

            def blocks(b, src, to, ready):
                for m in range(KD):
                    batch = slice(b, b + 1) if isinstance(b, int) else bass.ds(b, 1)
                    dve.tensor_tensor(by_head(to[:, m, :]), headmask(m), src[:, m, batch, :].broadcast_to([P, H, NS]), ALU.mult).then_inc(ready, 1)

            def take_scores(b):
                at(dve, rb_ready, b + 1)
                for q in range(2):
                    at(dve, sc_psum, b * 2 + q + 1)
                    dve.tensor_tensor(sc[:, 2 * q:2 * q + 2, :], bank[5 + q][:, :].rearrange("p (t s) -> p t s", t=2),
                                      rb[:, :].rearrange("p (o s) -> p o s", o=1).broadcast_to([P, 2, HS]), ALU.add).then_inc(sc_ready, 1)

            def below_max(b):
                at(dve, sc_ready, b * 2 + 2)
                dve.tensor_reduce(cm[:, :], flat(sc[:, :, :]), AX.X, ALU.max).then_inc(cm_ready, 1)
                at(dve, cm_ready, b + 1)
                at(dve, ce_ready, b)
                dve.tensor_tensor(flat(cd[:, :, :]), flat(sc[:, :, :]), wide(cm[:, :]), ALU.subtract).then_inc(cd_ready, 1)

            def softmax(b):
                at(dve, ce_ready, b + 1)
                dve.tensor_reduce(cs[:, :], flat(ce[:, :, :]), AX.X, ALU.add).then_inc(cs_ready, 1)
                at(dve, cs_ready, b + 1)
                dve.reciprocal(cr[:, :], cs[:, :]).then_inc(cr_ready, 1)
                at(dve, cr_ready, b + 1)
                at(dve, cpT_psum, b * 2)
                dve.tensor_tensor(flat(cp[:, :, :]), flat(ce[:, :, :]), wide(cr[:, :]), ALU.mult).then_inc(cp_ready, 1)

            def residual(b):
                at(dve, hb_ready, b + 1)
                batch = slice(b, b + 1) if isinstance(b, int) else bass.ds(b, 1)
                for q, bk in ((0, 2), (1, 7)):
                    at(dve, c_psum, b * 2 + q + 1)
                    hb = h[:, batch, 2 * q:2 * q + 2, :].rearrange("p o t d -> p (o t d)")
                    dve.tensor_tensor(hb, bank[bk][:, :], hb, ALU.add).then_inc(h_ready, 1)

            nm.dve_stats(dve, AGAIN, 0)
            nm.dve_apply(dve, AGAIN, 0)
            blocks(0, kc, kblk, kblk_ready)
            take_scores(0)
            nm.dve_stats(dve, AGAIN + 1, 1)
            below_max(0)
            with dve.Fori(0, B - 1) as b:
                nm.dve_apply(dve, b + (AGAIN + 1), b + 1)
                at(dve, rb_psum, b + 1)
                blocks(b + 1, kc, kblk, kblk_ready)
                at(dve, vw_psum, b)
                blocks(b, vc, vblk, vblk_ready)
                softmax(b)
                take_scores(b + 1)
                nm.dve_stats(dve, b + (AGAIN + 2), b + 2)
                below_max(b + 1)
                residual(b)
            dve.wait_ge(vw_psum, B - 1 + START)
            blocks(B - 1, vc, vblk, vblk_ready)
            softmax(B - 1)
            residual(B - 1)

        @block.gpsimd
        def _(pool):
            nm.pool_rstd(pool, 0)
            with pool.Fori(0, B) as b:
                nm.pool_rstd(pool, b + 1)
            pool.wait_ge(join, KD + 4)
            pool.tensor_tensor(ve[:, :], mv[:, 1:2], K["eps"][0:R, 0:1], ALU.add).then_inc(jpool, 1)
            pool.wait_ge(jpool, 1)
            pool.tensor_tensor(rstd[:, :], ve[:, :], K["mhalf"][0:R, 0:1], ALU.pow).then_inc(jpool, 1)
            pool.wait_ge(join, KD + 5)
            pool.tensor_tensor(og[:, :], on[:, :], rows[:, 2, :], ALU.mult).then_inc(jpool, 1)
            pool.wait_ge(jpool, 3)
            pool.tensor_tensor(ob[:, :], og[:, :], rows[:, 3, :], ALU.add).then_inc(jpool, 1)

            def output_bias(b):
                at(pool, nm.xn_ready, b + (AGAIN + 1))
                batch = slice(b, b + 1) if isinstance(b, int) else bass.ds(b, 1)
                hb = h[:, batch, :, :].rearrange("p o t d -> p (o t) d")
                pool.tensor_tensor(hb, hb, c_bo[:, :].rearrange("p (o d) -> p o d", o=1).broadcast_to([P, TT, D]), ALU.add).then_inc(hb_ready, 1)

            nm.pool_rstd(pool, AGAIN)
            with pool.Fori(0, B - 1) as b:
                nm.pool_rstd(pool, b + (AGAIN + 1))
                output_bias(b)
            output_bias(B - 1)


def conv_stage(nc, K, a):
    TAPS, H1 = 4, T + 3
    with ExitStack() as ctx:
        sem = lambda n: K["sem"]("s4_" + n)
        sb = lambda n, s, d=F32: ctx.enter_context(nc.sbuf_tensor("s4_" + n, s, d))
        h, ident, bank = K["h"], K["ident"], K["bank"]
        nm = Norm(ctx, nc, K, "s4n", (bank[0], bank[1]))
        w_in, w_cv, w_fc, w_cp, w_out = (sb("w_in", [P, KD, 2 * INNER]), sb("w_cv", [P, MI, TAPS, P]), sb("w_fc", [P, MI, D]),
                                         sb("w_cp", [P, KD, INNER]), sb("w_out", [P, MI, D]))
        par = sb("par", [P, 4 * MI + KD])
        hc, sg, r = sb("hc", [P, MI, H1]), sb("sg", [P, MI, T]), sb("r", [P, MI, T])
        st, mv, ve, rstd, spare = sb("st", [P, TT, 6]), sb("mv", [P, TT, 2]), sb("ve", [P, TT]), sb("rstd", [P, TT]), sb("spare", [P, 1])
        rn, rnT, f, r2 = sb("rn", [P, TT, INNER]), sb("rnT", [P, MI, T]), sb("f", [P, KD, T]), sb("r2", [P, MI, T])
        loaded, zeroed = sem("loaded"), sem("zeroed")
        p_psum, hc_ready, g_psum, sg_ready, cv_psum, r_ready = (sem(n) for n in ("p_psum", "hc_ready", "g_psum", "sg_ready", "cv_psum", "r_ready"))
        rT_psum, stats, var, veps, rstd_ready, rn_ready = (sem(n) for n in ("rT_psum", "stats", "var", "veps", "rstd_ready", "rn_ready"))
        rnT_psum, rnT_ready, f_psum, f_ready, cp_psum, r2_ready, o_psum, h_ready = (
            sem(n) for n in ("rnT_psum", "rnT_ready", "f_psum", "f_ready", "cp_psum", "r2_ready", "o_psum", "h_ready"))
        block = ctx.enter_context(nc.Block())

        @block.sync
        def _(sp):
            start(sp, *nm.sems, p_psum, hc_ready, g_psum, sg_ready, cv_psum, r_ready, rT_psum, stats, var, veps, rstd_ready, rn_ready,
                  rnT_psum, rnT_ready, f_psum, f_ready, cp_psum, r2_ready, o_psum, h_ready)
            for to, src in ((w_in[:, :, :], a["s4_in"]), (par[:, :], a["s4_par"]), (w_fc[:, :, :], a["s4_fc"]),
                            (w_cp[:, :, :], a["s4_cp"]), (w_out[:, :, :], a["s4_out"])):
                sp.dma_start(to, src).then_inc(loaded, 16)
            sp.wait_ge(zeroed, 1)
            for g in range(2):
                q = slice(64 * g, 64 * g + 64)
                sp.dma_start(w_cv[q, :, :, q], a["s4_cv"][q]).then_inc(loaded, 16)

        @block.tensor
        def _(pe):
            nm.pe_turn(pe, 0)
            pe.wait_ge(loaded, 16 * 7)
            pe.wait_ge(zeroed, 2)
            def project(b):
                at(pe, nm.xT_ready, b + 1)
                for m in range(MI):
                    at(pe, hc_ready, b * MI + m - 1)
                    for k in range(KD):
                        mm = pe.matmul(bank[5 + m % 2][:, :], w_in[:, k, m * P:(m + 1) * P], nm.xT[:, k, :], start=(k == 0), stop=(k == KD - 1))
                    mm.then_inc(p_psum, 1)
                    at(pe, sg_ready, b * MI + m)
                    for k in range(KD):
                        mm = pe.matmul(bank[4][:, :], w_in[:, k, INNER + m * P:INNER + (m + 1) * P], nm.xT[:, k, :], start=(k == 0), stop=(k == KD - 1))
                    mm.then_inc(g_psum, 1)

            project(0)
            with pe.Fori(0, B) as b:
                for m in range(MI):
                    at(pe, r_ready, b * MI + m - 1)
                    if m == 0:
                        at(pe, hc_ready, b * MI + MI)
                        at(pe, h_ready, b * 2)
                    for j in range(TAPS):
                        mm = pe.matmul(bank[5 + m % 2][:, :], w_cv[:, m, j, :], hc[:, m, j:j + T], start=(j == 0), stop=(j == TAPS - 1))
                    mm.then_inc(cv_psum, 1)
                at(pe, f_ready, b * KD)
                nm.pe_turn(pe, b + 1)
                at(pe, r_ready, b * MI + MI)
                at(pe, nm.xT_ready, b + 2)
                at(pe, r2_ready, b * MI)
                for t in range(TT):
                    for c in range(MI):
                        mm = pe.transpose(bank[t][:, c * P:(c + 1) * P], r[:, c, t * P:(t + 1) * P], ident[:, :])
                    mm.then_inc(rT_psum, 1)
                project(b + 1)
                at(pe, rn_ready, b * TT + TT)
                at(pe, hc_ready, (b + 2) * MI)
                at(pe, sg_ready, (b + 2) * MI)
                for c in range(MI):
                    for t in range(TT):
                        mm = pe.transpose(bank[4 + c][:, t * P:(t + 1) * P], rn[:, t, c * P:(c + 1) * P], ident[:, :])
                    mm.then_inc(rnT_psum, 1)
                at(pe, rnT_ready, b * MI + MI)
                for m in range(KD):
                    for k in range(MI):
                        mm = pe.matmul(bank[m][:, :], w_fc[:, k, m * P:(m + 1) * P], rnT[:, k, :], start=(k == 0), stop=(k == MI - 1))
                    mm.then_inc(f_psum, 1)
                at(pe, f_ready, b * KD + KD)
                for m in range(MI):
                    at(pe, r2_ready, b * MI + m - 1)
                    for k in range(KD):
                        mm = pe.matmul(bank[2 + m % 2][:, :], w_cp[:, k, m * P:(m + 1) * P], f[:, k, :], start=(k == 0), stop=(k == KD - 1))
                    mm.then_inc(cp_psum, 1)
                at(pe, r2_ready, b * MI + MI)
                for g in range(2):
                    for t in range(2):
                        for k in range(MI):
                            mm = pe.matmul(bank[6 + g][:, t * D:(t + 1) * D], r2[:, k, (2 * g + t) * P:(2 * g + t + 1) * P], w_out[:, k, :], start=(k == 0), stop=(k == MI - 1))
                    mm.then_inc(o_psum, 1)

        @block.scalar
        def _(act):
            nm.act_copy(act, 0)
            act.wait_ge(loaded, 16 * 7)
            def projected(b):
                for m in range(MI):
                    at(act, p_psum, b * MI + m + 1)
                    at(act, cv_psum, b * MI)
                    act.activation(hc[:, m, TAPS - 1:H1], bank[5 + m % 2][:, :], ACT.Copy).then_inc(hc_ready, 1)
                    at(act, g_psum, b * MI + m + 1)
                    at(act, r_ready, b * MI)
                    act.activation(sg[:, m, :], bank[4][:, :], ACT.Silu).then_inc(sg_ready, 1)

            projected(0)
            with act.Fori(0, B) as b:
                nm.act_copy(act, b + 1)
                projected(b + 1)
                for c in range(MI):
                    at(act, rnT_psum, b * MI + c + 1)
                    at(act, f_psum, b * KD)
                    act.activation(rnT[:, c, :], bank[4 + c][:, :], ACT.Identity, bias=par[:, 8 + c:9 + c], scale=par[:, 4 + c:5 + c]).then_inc(rnT_ready, 1)
                for m in range(KD):
                    at(act, f_psum, b * KD + m + 1)
                    at(act, cp_psum, b * MI)
                    act.activation(f[:, m, :], bank[m][:, :], ACT.Silu, bias=par[:, 16 + m:17 + m]).then_inc(f_ready, 1)

        @block.vector
        def _(dve):
            dve.memset(w_cv[:, :, :, :], 0.0).then_inc(zeroed, 1)
            dve.memset(hc[:, :, 0:TAPS - 1], 0.0).then_inc(zeroed, 1)
            nm.dve_stats(dve, 0)
            nm.dve_apply(dve, 0)
            dve.wait_ge(loaded, 16 * 7)
            with dve.Fori(0, B) as b:
                for m in range(MI):
                    if m == 0:
                        nm.dve_stats(dve, b + 1)
                    if m == 1:
                        nm.dve_apply(dve, b + 1)
                    at(dve, cv_psum, b * MI + m + 1)
                    at(dve, sg_ready, b * MI + m + 1)
                    dve.scalar_tensor_tensor(r[:, m, :], bank[5 + m % 2][:, :], par[:, m:m + 1], sg[:, m, :], ALU.add, ALU.mult).then_inc(r_ready, 1)
                for t in range(TT):
                    at(dve, rT_psum, b * TT + t + 1)
                    i = dve.bn_stats(st[:, t, :], bank[t][:, :])
                i.then_inc(stats, 1)
                at(dve, stats, b + 1)
                at(dve, veps, b)
                dve.memset(spare[:, :], 0.0)
                for t in range(TT):
                    i = dve.bn_aggr(mv[:, t, :], st[:, t, :])
                i.then_inc(var, 1)
                at(dve, rstd_ready, b + 1)
                at(dve, rnT_psum, b * MI)
                for t in range(TT):
                    dve.tensor_scalar(rn[:, t, :], bank[t][:, :], mv[:, t, 0:1], rstd[:, t:t + 1], ALU.subtract, ALU.mult).then_inc(rn_ready, 1)
                at(dve, o_psum, b * 2)
                for m in range(MI):
                    at(dve, cp_psum, b * MI + m + 1)
                    dve.scalar_tensor_tensor(r2[:, m, :], bank[2 + m % 2][:, :], par[:, 12 + m:13 + m], r[:, m, :], ALU.add, ALU.add).then_inc(r2_ready, 1)
                for g in range(2):
                    at(dve, o_psum, b * 2 + g + 1)
                    hb = h[:, b, 2 * g:2 * g + 2, :].rearrange("p t d -> p (t d)")
                    dve.tensor_tensor(hb, bank[6 + g][:, :], hb, ALU.add).then_inc(h_ready, 1)

        @block.gpsimd
        def _(pool):
            nm.pool_rstd(pool, 0)
            with pool.Fori(0, B) as b:
                nm.pool_rstd(pool, b + 1)
                at(pool, var, b + 1)
                at(pool, rstd_ready, b)
                pool.tensor_tensor(ve[:, :], mv[:, :, 1], K["eps"][:, 0:TT], ALU.add).then_inc(veps, 1)
                at(pool, veps, b + 1)
                at(pool, rn_ready, b * TT)
                pool.tensor_tensor(rstd[:, :], ve[:, :], K["mhalf"][:, 0:TT], ALU.pow).then_inc(rstd_ready, 1)


def expert_stage(nc, K, a, out):
    E, F, TOK = 8, 704, B * T
    NTT = TOK // P
    NT = (2 * TOK + E * (P - 1)) // P
    U = 3
    STEPS = NT // U
    FC = [(i * P, min(P, F - i * P)) for i in range(-(-F // P))]
    assert NT == U * STEPS
    with ExitStack() as ctx:
        sem = lambda n: K["sem"]("s5_" + n)
        sb = lambda n, s, d=F32: ctx.enter_context(nc.sbuf_tensor("s5_" + n, s, d))
        h, ident, bank = K["h"], K["ident"], K["bank"]
        X = nc.dram_tensor("expert_inputs", (NT * P, D), F32, kind="Internal").ap()
        Y = nc.dram_tensor("expert_outputs", (NT * P, D), F32, kind="Internal").ap()
        with ExitStack() as first:
            fsb = lambda n, s, d=F32: first.enter_context(nc.sbuf_tensor("s5_" + n, s, d))
            w13, w2 = sb("w13", [P, E, KD, 2 * F]), sb("w2", [P, E, len(FC), D])
            wts, slots, texp = sb("wts", [P, 2, NTT]), sb("slots", [P, 2, NTT], I32), sb("texp", [1, NT], I32)
            w_loaded = sem("w_loaded")
            nm = Norm(first, nc, K, "s5n", (bank[0], bank[1]))
            zeros = fsb("zeros", [P, D])
            wg, xall = fsb("wg", [P, KD, E]), fsb("xall", [P, B, TT, D])
            tri, iota_e, iota_t = fsb("tri", [P, P]), fsb("iota_e", [P, E]), fsb("iota_t", [1, NT])
            lg, mx, ex, sm, rs, scr = (fsb("lg", [P, NTT, E]), fsb("mx", [P, NTT]), fsb("ex", [P, NTT, E]), fsb("sm", [P, NTT]), fsb("rs", [P, NTT]), fsb("scr", [P, NTT, E]))
            m8, i8, best = fsb("m8", [P, NTT, 8]), fsb("i8", [P, NTT, 8], U32), fsb("best", [P, 2, NTT])
            den, rden = fsb("den", [P, NTT]), fsb("rden", [P, NTT])
            hot, both = fsb("hot", [P, 2, NTT, E]), fsb("both", [P, NTT, E])
            place, base, cnt, cnti, tiles, ends = (fsb("place", [P, NTT, E]), fsb("base", [P, NTT + 1, E]), fsb("cnt", [P, E]), fsb("cnti", [P, E], I32),
                                                   fsb("tiles", [P, E]), fsb("ends", [P, E + 1]))
            pick, slotf, tef = fsb("pick", [P, NTT, E]), fsb("slotf", [P, 2, NTT]), fsb("tef", [1, NT])
            loaded, zero_set, cleared = sem("loaded"), sem("zero_set"), sem("cleared")
            xall_ready, l_psum, l_ready, step, exped, rank_psum = sem("xall_ready"), sem("l_psum"), sem("l_ready"), sem("step"), sem("exped"), sem("rank_psum")
            scattered = sem("scattered")
            with nc.Block() as block:
                @block.sync
                def _(sp):
                    start(sp, *nm.sems, xall_ready, l_psum, l_ready)
                    for to, src in ((wg[:, :, :], a["s5_wg"]), (tri[:, :], a["s5_tri"]), (iota_e[:, :], a["s5_iota_e"]), (iota_t[:, :], a["s5_iota_t"])):
                        sp.dma_start(to, src).then_inc(loaded, 16)
                    sp.wait_ge(zero_set, 1)
                    for i in range(NT):
                        sp.dma_start(X[i * P:(i + 1) * P, :], zeros[:, :]).then_inc(cleared, 16)
                    for e in range(E):
                        sp.dma_start(w13[:, e, :, :], a["s5_w13"][e]).then_inc(w_loaded, 16)
                        sp.dma_start(w2[:, e, 0:5, :], a["s5_w2"][e, 0:5 * P].rearrange("(c p) d -> p c d", p=P)).then_inc(w_loaded, 16)
                        sp.dma_start(w2[0:F - 5 * P, e, 5, :], a["s5_w2"][e, 5 * P:F]).then_inc(w_loaded, 16)

                @block.tensor
                def _(pe):
                    nm.pe_turn(pe, 0)
                    pe.wait_ge(loaded, 64)
                    with pe.Fori(0, B) as b:
                        at(pe, nm.xT_ready, b + 1)
                        at(pe, l_ready, b)
                        for t in range(TT):
                            for k in range(KD):
                                mm = pe.matmul(bank[2][:, t * E:(t + 1) * E], nm.xT[:, k, t * P:(t + 1) * P], wg[:, k, :], start=(k == 0), stop=(k == KD - 1))
                        mm.then_inc(l_psum, 1)
                        nm.pe_turn(pe, b + 1)
                    pe.wait_ge(step, 11)
                    pe.matmul(bank[3][:, 0:NTT * E], tri[:, :], both[:, :, :], start=True, stop=True)
                    pe.matmul(bank[4][:, 0:NTT * E], K["ones"][:, :], both[:, :, :], start=True, stop=True).then_inc(rank_psum, 1)

                @block.scalar
                def _(act):
                    nm.act_copy(act, 0)
                    with act.Fori(0, B) as b:
                        at(act, nm.xn_ready, b + 1)
                        act.activation(xall[:, b, :, :], nm.xn[:, :, :], ACT.Copy).then_inc(xall_ready, 1)
                        nm.act_copy(act, b + 1)
                    act.wait_ge(step, 2)
                    act.activation(ex[:, :, :], ex[:, :, :], ACT.Exp).then_inc(exped, 1)

                @block.vector
                def _(dve):
                    dve.memset(zeros[:, :], 0.0).then_inc(zero_set, 1)
                    nm.dve_stats(dve, 0)
                    nm.dve_apply(dve, 0)
                    with dve.Fori(0, B) as b:
                        nm.dve_stats(dve, b + 1)
                        at(dve, xall_ready, b + 1)
                        nm.dve_apply(dve, b + 1)
                        at(dve, l_psum, b + 1)
                        dve.tensor_copy(lg[:, bass.ds(b * TT, TT), :].rearrange("p t e -> p (t e)"), bank[2][:, 0:TT * E]).then_inc(l_ready, 1)
                    dve.wait_ge(l_ready, B + START)
                    dve.wait_ge(loaded, 64)
                    done = 0

                    def then(i):
                        nonlocal done
                        i.then_inc(step, 1)
                        done += 1
                        dve.wait_ge(step, done)

                    per_tile = lambda x: x.rearrange("p (t o) -> p t o", o=1).broadcast_to([P, NTT, E])
                    per_exp = lambda x: x.rearrange("p (o e) -> p o e", o=1).broadcast_to([P, NTT, E])
                    then(dve.tensor_reduce(mx[:, :], lg[:, :, :], AX.X, ALU.max))
                    then(dve.tensor_tensor(ex[:, :, :], lg[:, :, :], per_tile(mx[:, :]), ALU.subtract))
                    dve.wait_ge(exped, 1)
                    then(dve.tensor_reduce(sm[:, :], ex[:, :, :], AX.X, ALU.add))
                    then(dve.reciprocal(rs[:, :], sm[:, :]))
                    then(dve.tensor_tensor(scr[:, :, :], ex[:, :, :], per_tile(rs[:, :]), ALU.mult))
                    for t in range(NTT):
                        i = dve.max(m8[:, t, :], scr[:, t, :])
                    then(i)
                    for t in range(NTT):
                        i = dve.max_index(i8[:, t, :], m8[:, t, :], scr[:, t, :])
                    then(i)
                    then(dve.tensor_copy(best[:, :, :], i8[:, :, 0:2].rearrange("p t k -> p k t")))
                    for k in range(2):
                        then(dve.tensor_tensor(hot[:, k, :, :], per_exp(iota_e[:, :]), per_tile(best[:, k, :]), ALU.is_equal))
                    then(dve.tensor_tensor(both[:, :, :], hot[:, 0, :, :], hot[:, 1, :, :], ALU.add))
                    then(dve.scalar_tensor_tensor(den[:, :], m8[:, :, 0], 1e-20, m8[:, :, 1], ALU.add, ALU.add))
                    then(dve.reciprocal(rden[:, :], den[:, :]))
                    for k in range(2):
                        then(dve.tensor_tensor(wts[:, k, :], m8[:, :, k], rden[:, :], ALU.mult))
                    dve.wait_ge(rank_psum, 1)
                    then(dve.memset(base[:, 0, :], 0.0))
                    for t in range(NTT):
                        then(dve.tensor_tensor(base[:, t + 1, :], bank[4][:, t * E:(t + 1) * E], base[:, t, :], ALU.add))
                    then(dve.tensor_scalar(cnt[:, :], base[:, NTT, :], float(P - 1), None, ALU.add))
                    then(dve.tensor_copy(cnti[:, :], cnt[:, :]))
                    then(dve.tensor_scalar(cnti[:, :], cnti[:, :], 7, None, ALU.arith_shift_right))
                    then(dve.tensor_copy(tiles[:, :], cnti[:, :]))
                    then(dve.memset(ends[:, 0:1], 0.0))
                    for e in range(E):
                        then(dve.tensor_tensor(ends[:, e + 1:e + 2], ends[:, e:e + 1], tiles[:, e:e + 1], ALU.add))
                    then(dve.tensor_tensor(place[:, :, :].rearrange("p t e -> p (t e)"), bank[3][:, 0:NTT * E], base[:, 0:NTT, :].rearrange("p t e -> p (t e)"), ALU.add))
                    then(dve.tensor_scalar(cnt[:, :], ends[:, 0:E], float(P), None, ALU.mult))
                    then(dve.tensor_tensor(place[:, :, :], place[:, :, :], per_exp(cnt[:, :]), ALU.add))
                    for k in range(2):
                        then(dve.tensor_tensor(pick[:, :, :], place[:, :, :], hot[:, k, :, :], ALU.mult))
                        then(dve.tensor_reduce(slotf[:, k, :], pick[:, :, :], AX.X, ALU.add))
                    then(dve.tensor_copy(slots[:, :, :], slotf[:, :, :]))
                    K["routed"] = done
                    then(dve.tensor_scalar(tef[:, :], iota_t[:, :], ends[0:1, 1:2], None, ALU.is_ge))
                    for e in range(2, E):
                        then(dve.scalar_tensor_tensor(tef[:, :], iota_t[:, :], ends[0:1, e:e + 1], tef[:, :], ALU.is_ge, ALU.add))
                    then(dve.tensor_copy(texp[:, :], tef[:, :]))

                @block.gpsimd
                def _(pool):
                    nm.pool_rstd(pool, 0)
                    with pool.Fori(0, B) as b:
                        nm.pool_rstd(pool, b + 1)
                    pool.wait_ge(step, K["routed"])
                    pool.wait_ge(xall_ready, B + START)
                    pool.wait_ge(cleared, 16 * NT)
                    for k in range(2):
                        for t in range(NTT):
                            pool.indirect_dma_start(
                                out=X[:, :], out_offset=bass.IndirectOffsetOnAxis(ap=slots[:, k, t:t + 1].bitcast(U32), axis=0),
                                in_=xall[:, t // TT, t % TT, :], in_offset=None).then_inc(scattered, 16)
                    pool.wait_ge(scattered, 16 * 2 * NTT)

        xt, xT = sb("xt", [P, U, D]), sb("xT", [P, U, KD, P])
        s1, hh, hT, yt = sb("s1", [P, 2, F]), sb("hh", [P, U, F]), sb("hT", [P, 2, len(FC), P]), sb("yt", [P, U, D])
        x_loaded, x_psum, x_ready = [sem(f"x_loaded{u}") for u in range(U)], sem("x_psum"), sem("x_ready")
        h_psum, s1_ready, hh_ready, hT_psum, hT_ready, y_psum, y_ready = (sem(n) for n in ("h_psum", "s1_ready", "hh_ready", "hT_psum", "hT_ready", "y_psum", "y_ready"))
        y_stored = [sem(f"y_stored{u}") for u in range(U)]
        with nc.Block() as block:
            @block.sync
            def _(sp):
                start(sp, x_psum, x_ready, h_psum, s1_ready, hh_ready, hT_psum, hT_ready, y_psum, y_ready)
                for u in range(U):
                    sp.dma_start(xt[:, u, :], X[u * P:(u + 1) * P, :]).then_inc(x_loaded[u], 16)

                def store(i, u):
                    at(sp, y_ready, i * U + u + 1)
                    sp.dma_start(Y[bass.ds(i * (U * P) + u * P, P), :], yt[:, u, :]).then_inc(y_stored[u], 16)

                with sp.Fori(0, STEPS - 1) as i:
                    for u in range(U):
                        at(sp, x_psum, i * U + u + 1)
                        sp.dma_start(xt[:, u, :], X[bass.ds(i * (U * P) + (U + u) * P, P), :]).then_inc(x_loaded[u], 16)
                        store(i, u)
                for u in range(U):
                    store(STEPS - 1, u)
                for u in range(U):
                    sp.wait_ge(y_stored[u], 16 * STEPS)

            @block.tensor
            def _(pe):
                def turn(i, u):
                    pe.wait_ge(x_loaded[u % U], (i + u // U) * 16 + 16)
                    at(pe, x_ready, i * U + u)
                    for k in range(KD):
                        mm = pe.transpose(bank[3][:, k * P:(k + 1) * P], xt[:, u % U, k * P:(k + 1) * P], ident[:, :])
                    mm.then_inc(x_psum, 1)

                def expert_of(i, u):
                    return pe.value_load(texp[0:1, bass.ds(i * U + u, 1)], min_val=0, max_val=E - 1)

                def up(i, u, e, parts):
                    if 0 in parts:
                        at(pe, x_ready, i * U + u + 1)
                        at(pe, hh_ready, i * U + u)
                    for bk in parts:
                        c0, c1 = bk * 512, min(bk * 512 + 512, 2 * F)
                        for k in range(KD):
                            mm = pe.matmul(bank[bk][:, 0:c1 - c0], xT[:, u % U, k, :], w13[:, bass.ds(e, 1), k, c0:c1].rearrange("p o c -> p (o c)"), start=(k == 0), stop=(k == KD - 1))
                        mm.then_inc(h_psum, 1)

                def turn_hidden(i, u):
                    at(pe, hh_ready, i * U + u + 1)
                    at(pe, hT_ready, i * U + u)
                    for c, (c0, w) in enumerate(FC):
                        mm = pe.transpose(bank[4 + c // 4][0:w, (c % 4) * P:(c % 4 + 1) * P], hh[:, u % U, c0:c0 + w], ident[:, :])
                    mm.then_inc(hT_psum, 1)

                def down(i, u):
                    e = expert_of(i, u)
                    at(pe, hT_ready, i * U + u + 1)
                    at(pe, y_ready, i * U + u)
                    for c, (c0, w) in enumerate(FC):
                        mm = pe.matmul(bank[6][:, 0:D], hT[0:w, 0, c, :], w2[0:w, bass.ds(e, 1), c, :].rearrange("p o c -> p (o c)"), start=(c == 0), stop=(c == len(FC) - 1))
                    mm.then_inc(y_psum, 1)

                def up_next(i, u):
                    e = expert_of(i, u + 1)
                    up(i, u + 1, e, (0, 1))
                    turn_hidden(i, u)
                    up(i, u + 1, e, (2,))

                pe.wait_ge(w_loaded, 48 * E)
                turn(0, 0)
                turn(0, 1)
                up(0, 0, expert_of(0, 0), (0, 1, 2))
                with pe.Fori(0, STEPS - 1) as i:
                    for u in range(U):
                        up_next(i, u)
                        turn(i, u + 2)
                        down(i, u)
                up_next(STEPS - 1, 0)
                turn(STEPS - 1, 2)
                down(STEPS - 1, 0)
                up_next(STEPS - 1, 1)
                down(STEPS - 1, 1)
                turn_hidden(STEPS - 1, 2)
                down(STEPS - 1, 2)

            @block.scalar
            def _(act):
                def copy_x(i, u):
                    at(act, x_psum, i * U + u + 1)
                    act.activation(xT[:, u % U, :, :], bank[3][:, 0:D], ACT.Copy).then_inc(x_ready, 1)

                def silu(i, u):
                    at(act, h_psum, i * (3 * U) + 3 * u + 2)
                    at(act, hh_ready, i * U + u - 1)
                    act.activation(s1[:, 0, 0:512], bank[0][:, :], ACT.Silu)
                    act.activation(s1[:, 0, 512:F], bank[1][:, 0:F - 512], ACT.Silu).then_inc(s1_ready, 1)

                def copy_h(i, u):
                    at(act, hT_psum, i * U + u + 1)
                    at(act, y_psum, i * U + u)
                    act.activation(hT[:, 0, 0:4, :], bank[4][:, :], ACT.Copy)
                    act.activation(hT[:, 0, 4, :], bank[5][:, 0:P], ACT.Copy)
                    act.activation(hT[0:F - 5 * P, 0, 5, :], bank[5][0:F - 5 * P, P:2 * P], ACT.Copy).then_inc(hT_ready, 1)

                copy_x(0, 0)
                copy_x(0, 1)
                silu(0, 0)
                with act.Fori(0, STEPS - 1) as i:
                    for u in range(U):
                        copy_h(i, u)
                        silu(i, u + 1)
                        copy_x(i, u + 2)
                copy_h(STEPS - 1, 0)
                silu(STEPS - 1, 1)
                copy_x(STEPS - 1, 2)
                copy_h(STEPS - 1, 1)
                silu(STEPS - 1, 2)
                copy_h(STEPS - 1, 2)

            @block.vector
            def _(dve):
                def gate(i, u):
                    at(dve, s1_ready, i * U + u + 1)
                    at(dve, h_psum, i * (3 * U) + 3 * u + 3)
                    at(dve, hT_psum, i * U + u - (U - 1))
                    q = 1024 - F
                    dve.tensor_tensor(hh[:, u % U, 0:q], s1[:, 0, 0:q], bank[1][:, F - 512:512], ALU.mult)
                    dve.tensor_tensor(hh[:, u % U, q:F], s1[:, 0, q:F], bank[2][:, 0:F - q], ALU.mult).then_inc(hh_ready, 1)

                def copy_y(i, u, first):
                    at(dve, y_psum, i * U + u + 1)
                    if not first:
                        dve.wait_ge(y_stored[u], i * 16)
                    dve.tensor_copy(yt[:, u, :], bank[6][:, 0:D]).then_inc(y_ready, 1)

                gate(0, 0)
                for u in range(U):
                    gate(0, u + 1)
                    copy_y(0, u, True)
                with dve.Fori(1, STEPS - 1) as i:
                    for u in range(U):
                        gate(i, u + 1)
                        copy_y(i, u, False)
                gate(STEPS - 1, 1)
                copy_y(STEPS - 1, 0, False)
                gate(STEPS - 1, 2)
                copy_y(STEPS - 1, 1, False)
                copy_y(STEPS - 1, 2, False)

        G = 4
        yg = sb("yg", [P, G, 2, D])
        gathered, added, out_written = [sem(f"gathered{g}") for g in range(G)], sem("added"), sem("out_written")
        with nc.Block() as block:
            @block.gpsimd
            def _(pool):
                for t in range(NTT):
                    if t >= G:
                        pool.wait_ge(added, 2 * (t - G + 1))
                    for k in range(2):
                        pool.indirect_dma_start(out=yg[:, t % G, k, :], out_offset=None, in_=Y[:, :],
                                                in_offset=bass.IndirectOffsetOnAxis(ap=slots[:, k, t:t + 1].bitcast(U32), axis=0)).then_inc(gathered[t % G], 16)

            @block.vector
            def _(dve):
                for t in range(NTT):
                    dve.wait_ge(gathered[t % G], 32 * (t // G + 1))
                    for k in range(2):
                        ht = h[:, t // TT, t % TT, :]
                        dve.scalar_tensor_tensor(ht, yg[:, t % G, k, :], wts[:, k, t:t + 1], ht, ALU.mult, ALU.add).then_inc(added, 1)
                        dve.wait_ge(added, 2 * t + k + 1)

            @block.sync
            def _(sp):
                for b in range(B):
                    sp.wait_ge(added, 2 * TT * (b + 1))
                    sp.dma_start(out[b].rearrange("(t p) d -> p t d", p=P), h[:, b, :, :]).then_inc(out_written, 16)
                sp.wait_ge(out_written, 16 * B)


def write_out(nc, K, out):
    with nc.semaphore("out_written") as out_written, nc.Block() as block:
        @block.sync
        def _(sp):
            sp.dma_start(out.rearrange("b (t p) d -> p b t d", p=P), K["h"][:, 0:B, :, :]).then_inc(out_written, 16)
            sp.wait_ge(out_written, 16)


def program(nc, a, out):
    with ExitStack() as ctx:
        sb = lambda n, s, d=F32: ctx.enter_context(nc.sbuf_tensor(n, s, d))
        K = {"h": sb("h", [P, B + 1, TT, D]), "ident": sb("ident", [P, P]), "ones": sb("ones", [P, P]), "mhalf": sb("mhalf", [P, 16]), "eps": sb("eps", [P, 16]),
             "bank": [ctx.enter_context(nc.psum_tensor(f"bank{i}", [P, 512], F32)) for i in range(8)]}
        made = []

        def new_semaphore(name):
            made.append(nc.alloc_semaphore(name))
            return made[-1]

        K["sem"] = new_semaphore
        for stage in (embed_stage, token_stage, scan_stage, slot_stage, conv_stage):
            stage(nc, K, a)
            nc.clear_and_free_semaphores(made)
            nc.all_engine_barrier()
            made.clear()
        expert_stage(nc, K, a, out)


def kernel(**inputs):
    import concourse.bacc as _bacc
    from concourse.bass_utils import run_bass_kernel_spmd as _run
    i = {k: np.asarray(v) for k, v in inputs.items()}
    L = 4

    def kT(w, k):
        w = np.swapaxes(w, -1, -2)
        return np.moveaxis(w.reshape(*w.shape[:-2], k, w.shape[-2] // k, w.shape[-1]), -2, -3)

    def col(v):
        return np.swapaxes(v.reshape(*v.shape[:-1], v.shape[-1] // P, P), -1, -2)

    cw = i["L0_tok_conv_w"][:, :, 0, :].reshape(L, MI, P, 4).transpose(0, 2, 1, 3).reshape(L, P, 16)
    lay = {
        "x": i["x"].reshape(B * TT, P).T,
        "tok_emb": i["L0_tok_tok_emb"], "pos_emb": i["L0_tok_pos_emb"],
        "W_inT": kT(i["L0_tok_W_in"], KD),
        "W_BT": kT(i["L0_tok_W_B"], MI),
        "W_CT": np.swapaxes(i["L0_tok_W_C"], 1, 2),
        "W_outT": kT(i["L0_tok_W_out"], MI),
        "tok_par": np.concatenate([cw, col(i["L0_tok_conv_b"]), col(i["L0_tok_D_vec"])], axis=-1),
        "tok_ln_g": i["L0_tok_ln_g"].reshape(L, 1, D), "tok_ln_b": i["L0_tok_ln_b"].reshape(L, 1, D),
    }
    cw = i["L0_attn_conv_w"][:, 0, :].reshape(MI, P, 4).transpose(1, 0, 2).reshape(P, 16)
    rows = lambda w, k: w.reshape(k, w.shape[0] // k, w.shape[1]).transpose(1, 0, 2)
    lay.update({
        "s2_in": rows(i["L0_attn_in_proj_w"], KD), "s2_x": rows(i["L0_attn_x_proj_w"], MI), "s2_out": rows(i["L0_attn_out_proj_w"], MI),
        "s2_par": np.concatenate([cw] + [col(i["L0_attn_" + k]) for k in ("conv_b", "dt_w", "dt_b", "D")], axis=-1),
        "s2_alog": rows(i["L0_attn_A_log"], MI),
    })
    g = lambda k: i["L0_ffn_" + k]
    lay.update({"s3_" + n: rows(g(n[0] + "_" + n[1:3]), KD) for n in ("dWq", "dWv", "dWo", "cWk", "cWv", "cWo")})
    lay.update({
        "s3_dWkT": rows(g("d_Wk").T, KD), "s3_cWqT": rows(g("c_Wq").T, KD),
        "s3_cols": np.stack([g(k).reshape(KD, P).T for k in ("d_bq", "d_bk", "d_bv", "c_bq", "c_bk", "c_bv", "c_bo")], axis=-1),
        "s3_bias": np.concatenate([g("e_b1"), g("e_bg")], axis=1),
        "s3_b2": g("e_b2").reshape(16, KD, P).transpose(2, 1, 0),
        "s3_slotT": rows(g("slot_query")[0].T, KD),
        "s3_rows": np.stack([np.tile(g("slot_query")[0], (B, 1)), np.tile(g("d_bo"), (B * 16, 1)), np.tile(g("e_ln_g"), (B, 1)), np.tile(g("e_ln_b"), (B, 1))], axis=1),
        "s3_cbo": g("c_bo").reshape(1, D),
        "s3_mask": (np.arange(D)[:, None] // 16 == np.arange(16)[None, :]).astype(np.float32).reshape(KD, P, 16).transpose(1, 0, 2),
        "s3_W1": g("e_W1").reshape(16, KD, P, 1024).transpose(0, 2, 1, 3), "s3_Wg": g("e_Wg").reshape(16, KD, P, 1024).transpose(0, 2, 1, 3),
        "s3_W2": g("e_W2").reshape(16, 8, P, D).transpose(0, 2, 1, 3),
    })
    g = lambda k: i["L1_attn_" + k]
    lay.update({
        "s4_in": rows(g("in_proj_w").T, KD), "s4_fc": rows(g("fc_w").T, MI), "s4_cp": rows(g("cproj_w").T, KD), "s4_out": rows(g("out_w").T, MI),
        "s4_cv": g("conv_w").reshape(MI, 2, 64, 64, 4).transpose(1, 3, 0, 4, 2).reshape(P, MI, 4, 64),
        "s4_par": np.concatenate([col(g(k)) for k in ("conv_b", "ln_g", "ln_b", "cproj_b", "fc_b")], axis=-1),
    })
    g = lambda k: i["L1_ffn_" + k]
    w13 = np.concatenate([g("W1"), g("W3")], axis=1).transpose(0, 2, 1)
    lay.update({
        "s5_wg": rows(g("Wg").T, KD), "s5_w13": w13.reshape(8, KD, P, -1).transpose(0, 2, 1, 3), "s5_w2": g("W2").transpose(0, 2, 1),
        "s5_tri": np.triu(np.ones((P, P), np.float32), 1), "s5_iota_e": np.tile(np.arange(8, dtype=np.float32), (P, 1)),
        "s5_iota_t": np.arange(39, dtype=np.float32)[None],
    })
    nc = _bacc.Bacc("TRN2", target_bir_lowering=False, num_devices=1)
    arrays, args = {}, {}
    for name, v in lay.items():
        v = np.ascontiguousarray(v)
        arrays[f"in_{name}"] = v
        args[name] = nc.dram_tensor(f"in_{name}", v.shape, mybir.dt.from_np(v.dtype), kind="ExternalInput").ap()
    out = nc.dram_tensor("out_h", (B, T, D), F32, kind="ExternalOutput").ap()
    program(nc, args, out)
    r = _run(nc, [arrays], core_ids=[0])
    return r.results[0]["out_h"]
```
